# Optimizing a Trainium2 kernel written in Bass

```python
import numpy as np
import jax
import jax.numpy as jnp

def _softmax(x, axis=-1):
    return jax.nn.softmax(x, axis=axis)

def _gelu(x):
    return jax.nn.gelu(x, approximate=True)

def _silu(x):
    return jax.nn.silu(x)

def _sigmoid(x):
    return jax.nn.sigmoid(x)

def _layernorm(x, axis=-1, eps=1e-05):
    m = jnp.mean(x, axis=axis, keepdims=True)
    v = jnp.var(x, axis=axis, keepdims=True)
    return (x - m) / jnp.sqrt(v + eps)

def _scatter_add(tgt, idx, src, axis=0):
    return tgt.at[idx].add(src)

def _segment_sum(src, seg, n):
    return jax.ops.segment_sum(src, seg, n)
kernel_name = 'mk_xattn_ffn_d4_seqx_r8_074e1c'

def setup_inputs(seed: int=0):
    np.random.seed(seed)
    _w = jnp.asarray

    def _rec_inputs():
        import jax
        import jax.numpy as jnp
        _rk = jax.random.key(seed)
        x = -0.0002928 + 1 * jax.random.normal(jax.random.fold_in(_rk, 1), (64, 64, 128), jnp.float32)
        _lenS = 64 - jax.random.randint(jax.random.fold_in(_rk, 7), (64,), 0, max(1, 64 // 4) + 1, jnp.int32)
        _lenS2 = 64 - jax.random.randint(jax.random.fold_in(_rk, 8), (64,), 0, max(1, 64 // 4) + 1, jnp.int32)
        _ctx_1024P = jax.random.normal(jax.random.fold_in(_rk, 11), (64, 16, 128), jnp.float32)
        _ctx_1024c = jax.random.dirichlet(jax.random.fold_in(_rk, 511), 0.3 * jnp.ones((16,), jnp.float32), (64, 64))
        _ctx_1024t = jnp.einsum('bsk,bkd->bsd', _ctx_1024c, _ctx_1024P)
        _ctx_1024t = _ctx_1024t * jax.lax.rsqrt(jnp.mean(jnp.square(_ctx_1024t)) + 1e-12) * 0.953939
        ctx_1024 = -1.39393e-06 + 0.999914 * (_ctx_1024t + 0.3 * jax.random.normal(jax.random.fold_in(_rk, 611), (64, 64, 128), jnp.float32))
        itok_BxS_0_511 = jax.random.randint(jax.random.fold_in(_rk, 13), (64, 64), 0, 64, jnp.int32)
        _validS = jnp.arange(64)[None, :] < _lenS[:, None]
        _validS2 = jnp.arange(64)[None, :] < _lenS2[:, None]
        _causal = jnp.tril(jnp.ones((64, 64), dtype=bool))
        mask_BxS2_if1 = jnp.where(jnp.ones((64, 64), dtype=bool), 1, 0).astype(jnp.int32)
        mask_BxS2_bf1 = jnp.ones((64, 64), dtype=bool)
        return (x, ctx_1024, itok_BxS_0_511, mask_BxS2_if1, mask_BxS2_bf1)
    x, ctx_1024, itok_BxS_0_511, mask_BxS2_if1, mask_BxS2_bf1 = _rec_inputs()

    def _L0_xattn_setup():
        import jax, jax.numpy as jnp
        import numpy as np
        D_MODEL = 128
        NUM_HEADS = 16
        D_K = D_MODEL // NUM_HEADS
        key = jax.random.key(seed)
        ks = jax.random.split(key, 7)
        B, S = (2, 256)
        query = jax.random.normal(ks[0], (B, S, D_MODEL), dtype=jnp.float32)
        key_t = jax.random.normal(ks[1], (B, S, D_MODEL), dtype=jnp.float32)
        value = jax.random.normal(ks[2], (B, S, D_MODEL), dtype=jnp.float32)
        attention_mask = jnp.ones((B, S), dtype=jnp.int32)
        limit = np.sqrt(6.0 / (D_MODEL + D_MODEL)).astype(np.float32)

        def xav(k):
            return jax.random.uniform(k, (D_MODEL, D_MODEL), dtype=jnp.float32, minval=-limit, maxval=limit)
        return {'query': query, 'key': key_t, 'value': value, 'attention_mask': attention_mask, 'w_q': xav(ks[3]), 'w_k': xav(ks[4]), 'w_v': xav(ks[5]), 'w_o': xav(ks[6])}
    _L0_xattn_all = _L0_xattn_setup()
    _L0_xattn_in = {k: v for k, v in _L0_xattn_all.items() if k in ('w_q', 'w_k', 'w_v', 'w_o')}
    del _L0_xattn_all

    def _L0_ffn_setup():
        import jax, jax.numpy as jnp
        import numpy as np
        BLOCK = 32
        W_BITS = 4
        ACT_BITS = 16

        def act_qdq(x):
            qmax = 2.0 ** (ACT_BITS - 1) - 1.0
            scale = jnp.maximum(jnp.max(jnp.abs(x)) / qmax, 1e-12)
            return jnp.clip(jnp.round(x / scale), -qmax - 1.0, qmax) * scale

        def fixed_qdq_u16(x):
            scale = 1.0 / 65536.0
            return jnp.clip(jnp.round(x / scale), 0.0, 65535.0) * scale

        def lpbq_dequant(w):
            O, I = w.shape
            qmax = 2.0 ** (W_BITS - 1) - 1.0
            wb = w.reshape(O, I // BLOCK, BLOCK)
            s = jnp.maximum(jnp.max(jnp.abs(wb), axis=-1, keepdims=True) / qmax, 1e-12)
            wq = jnp.clip(jnp.round(wb / s), -qmax - 1.0, qmax) * s
            return wq.reshape(O, I)
        key = jax.random.key(seed)
        k1, k2, k3, k4 = jax.random.split(key, 4)
        B, S, H, I = (2, 512, 128, 384)
        x = jax.random.normal(k1, (B, S, H), jnp.float32)
        w_gate = jax.random.normal(k2, (I, H), jnp.float32) * 0.02
        w_up = jax.random.normal(k3, (I, H), jnp.float32) * 0.02
        w_down = jax.random.normal(k4, (H, I), jnp.float32) * 0.02
        return {'x': x, 'w_gate': w_gate, 'w_up': w_up, 'w_down': w_down}
    _L0_ffn_all = _L0_ffn_setup()
    _L0_ffn_in = {k: v for k, v in _L0_ffn_all.items() if k in ('w_gate', 'w_up', 'w_down')}
    del _L0_ffn_all

    def _L1_xattn_setup():
        import jax, jax.numpy as jnp
        import numpy as np
        Q_DIM = 128
        KV_DIM = 128
        D_ATTN = 128
        N_HEADS = 16
        HDIM = D_ATTN // N_HEADS
        LOOKBACK = 3
        KW = LOOKBACK + 1
        SCALE = HDIM ** (-0.5)
        B, LQ, LKV = (4, 512, 64)

        def _split_heads(x):
            b, l, _ = x.shape
            return x.reshape(b, l, N_HEADS, HDIM).transpose(0, 2, 1, 3)
        key = jax.random.key(seed)
        ks = jax.random.split(key, 6)
        q = jax.random.normal(ks[0], (B, LQ, Q_DIM), dtype=jnp.float32)
        kv_src = jax.random.normal(ks[1], (B, LKV, KV_DIM), dtype=jnp.float32)
        seg_id = jnp.sort(jax.random.randint(ks[2], (B, LQ), 0, LKV), axis=-1)
        Wq = jax.random.normal(ks[3], (D_ATTN, Q_DIM), dtype=jnp.float32) * Q_DIM ** (-0.5)
        Wkv = jax.random.normal(ks[4], (2 * D_ATTN, KV_DIM), dtype=jnp.float32) * KV_DIM ** (-0.5)
        Wo = jax.random.normal(ks[5], (Q_DIM, D_ATTN), dtype=jnp.float32) * D_ATTN ** (-0.5)
        return {'q': q, 'kv_src': kv_src, 'seg_id': seg_id, 'Wq': Wq, 'Wkv': Wkv, 'Wo': Wo}
    _L1_xattn_all = _L1_xattn_setup()
    _L1_xattn_in = {k: v for k, v in _L1_xattn_all.items() if k in ('Wq', 'Wkv', 'Wo')}
    del _L1_xattn_all

    def _L1_ffn_setup():
        import jax, jax.numpy as jnp
        import numpy as np
        key = jax.random.key(seed)
        ks = jax.random.split(key, 4)
        B, T, M, E, F = (4, 256, 128, 8, 512)
        hidden_states = jax.random.normal(ks[0], (B, T, M), dtype=jnp.float32)
        wg = jax.random.normal(ks[1], (M, E), dtype=jnp.float32) * (1.0 / np.sqrt(M))
        w1 = jax.random.normal(ks[2], (E, M, F), dtype=jnp.float32) * (1.0 / np.sqrt(M))
        b1 = jnp.zeros((E, F), dtype=jnp.float32)
        w2 = jax.random.normal(ks[3], (E, F, M), dtype=jnp.float32) * (1.0 / np.sqrt(F))
        b2 = jnp.zeros((E, M), dtype=jnp.float32)
        return {'hidden_states': hidden_states, 'wg': wg, 'w1': w1, 'b1': b1, 'w2': w2, 'b2': b2}
    _L1_ffn_all = _L1_ffn_setup()
    _L1_ffn_in = {k: v for k, v in _L1_ffn_all.items() if k in ('wg', 'w1', 'b1', 'w2', 'b2')}
    del _L1_ffn_all

    def _L2_xattn_setup():
        import jax, jax.numpy as jnp
        import numpy as np
        DIM = 128
        HEAD_DIM = 64
        NUM_HEADS = 8
        INNER = HEAD_DIM * NUM_HEADS
        ROT_DIM = HEAD_DIM
        ROPE_BASE = 10000.0
        EPS = 1e-05

        def layer_norm(x, g, b):
            mu = jnp.mean(x, axis=-1, keepdims=True)
            var = jnp.var(x, axis=-1, keepdims=True)
            return (x - mu) * jax.lax.rsqrt(var + EPS) * g + b

        def rope_rotate_k(k):
            n = k.shape[1]
            half = ROT_DIM // 2
            inv_freq = 1.0 / ROPE_BASE ** (jnp.arange(0, ROT_DIM, 2, dtype=jnp.float32) / ROT_DIM)
            theta = jnp.arange(n, dtype=jnp.float32)[:, None] * inv_freq[None, :]
            angles = jnp.concatenate([theta, theta], axis=-1)
            cos = jnp.cos(angles)[None, :, None, :].astype(k.dtype)
            sin = jnp.sin(angles)[None, :, None, :].astype(k.dtype)
            k_rope, k_pass = (k[..., :ROT_DIM], k[..., ROT_DIM:])
            neg_half = jnp.concatenate([-k_rope[..., half:], k_rope[..., :half]], axis=-1)
            k_rope = k_rope * cos + neg_half * sin
            return jnp.concatenate([k_rope, k_pass], axis=-1)
        key = jax.random.key(seed)
        ks = jax.random.split(key, 5)
        b, n, m = (8, 1024, 64)
        s = 1.0 / np.sqrt(DIM)
        return {'x': jax.random.normal(ks[0], (b, n, DIM), jnp.float32), 'latents': jax.random.normal(ks[1], (b, m, DIM), jnp.float32), 'gamma_x': jnp.ones((DIM,), jnp.float32), 'beta_x': jnp.zeros((DIM,), jnp.float32), 'gamma_l': jnp.ones((DIM,), jnp.float32), 'beta_l': jnp.zeros((DIM,), jnp.float32), 'Wq': jax.random.normal(ks[2], (DIM, INNER), jnp.float32) * s, 'Wkv': jax.random.normal(ks[3], (DIM, 2 * INNER), jnp.float32) * s, 'Wo': jax.random.normal(ks[4], (INNER, DIM), jnp.float32) * (1.0 / np.sqrt(INNER))}
    _L2_xattn_all = _L2_xattn_setup()
    _L2_xattn_in = {k: v for k, v in _L2_xattn_all.items() if k in ('gamma_x', 'beta_x', 'gamma_l', 'beta_l', 'Wq', 'Wkv', 'Wo')}
    del _L2_xattn_all

    def _L2_ffn_setup():
        import jax, jax.numpy as jnp
        import numpy as np
        DIM = 128
        HID = 512
        NUM_EXPERTS = 8
        TOP_K = 2
        ALPHA = 2.0
        B, S = (4, 256)

        def _swiglu(x, wu, wg, wd):
            up = x @ wu
            g = x @ wg
            gate = jax.nn.sigmoid(g) * g
            return up * gate @ wd
        key = jax.random.key(seed)
        ks = jax.random.split(key, 8)
        x = jax.random.normal(ks[0], (B, S, DIM), dtype=jnp.float32)
        Wr = jax.random.normal(ks[1], (DIM, NUM_EXPERTS), dtype=jnp.float32) * 0.02
        Wu = jax.random.normal(ks[2], (NUM_EXPERTS - 1, DIM, HID), dtype=jnp.float32) * 0.02
        Wg = jax.random.normal(ks[3], (NUM_EXPERTS - 1, DIM, HID), dtype=jnp.float32) * 0.02
        Wd = jax.random.normal(ks[4], (NUM_EXPERTS - 1, HID, DIM), dtype=jnp.float32) * 0.002
        Wu_s = jax.random.normal(ks[5], (DIM, HID), dtype=jnp.float32) * 0.02
        Wg_s = jax.random.normal(ks[6], (DIM, HID), dtype=jnp.float32) * 0.02
        Wd_s = jax.random.normal(ks[7], (HID, DIM), dtype=jnp.float32) * 0.002
        return {'x': x, 'Wr': Wr, 'Wu': Wu, 'Wg': Wg, 'Wd': Wd, 'Wu_s': Wu_s, 'Wg_s': Wg_s, 'Wd_s': Wd_s}
    _L2_ffn_all = _L2_ffn_setup()
    _L2_ffn_in = {k: v for k, v in _L2_ffn_all.items() if k in ('Wr', 'Wu', 'Wg', 'Wd', 'Wu_s', 'Wg_s', 'Wd_s')}
    del _L2_ffn_all

    def _L3_xattn_setup():
        import jax, jax.numpy as jnp
        import numpy as np
        HEADS = 16
        DIM_HEAD = 64
        SCALE = DIM_HEAD ** (-0.5)
        key = jax.random.key(seed)
        ks = jax.random.split(key, 6)
        B, Nq, Nkv, D = (4, 256, 128, 128)
        inner = HEADS * DIM_HEAD
        return {'x': jax.random.normal(ks[0], (B, Nq, D), dtype=jnp.float32), 'context': jax.random.normal(ks[1], (B, Nkv, D), dtype=jnp.float32), 'mask': jnp.ones((B, Nkv), dtype=bool), 'Wq': jax.random.normal(ks[2], (inner, D), dtype=jnp.float32) * D ** (-0.5), 'Wkv': jax.random.normal(ks[3], (2 * inner, D), dtype=jnp.float32) * D ** (-0.5), 'Wout': jax.random.normal(ks[4], (D, inner), dtype=jnp.float32) * inner ** (-0.5), 'b_out': jnp.zeros((D,), dtype=jnp.float32)}
    _L3_xattn_all = _L3_xattn_setup()
    _L3_xattn_in = {k: v for k, v in _L3_xattn_all.items() if k in ('Wq', 'Wkv', 'Wout', 'b_out')}
    del _L3_xattn_all

    def _L3_ffn_setup():
        import jax, jax.numpy as jnp
        import numpy as np
        E = 8
        K = 2
        CF = 1.2
        D = 128
        F = 512
        B, S = (4, 128)
        key = jax.random.key(seed)
        ks = jax.random.split(key, 4)

        def init(k, shape, fan_in):
            return jax.random.normal(k, shape, jnp.float32) * (1.0 / np.sqrt(fan_in))
        return {'x': jax.random.normal(ks[0], (B, S, D), jnp.float32), 'Wg': init(ks[1], (D, E), D), 'bg': jnp.zeros((E,), jnp.float32), 'W1': init(ks[2], (E, D, F), D), 'b1': jnp.zeros((E, F), jnp.float32), 'W2': init(ks[3], (E, F, D), F), 'b2': jnp.zeros((E, D), jnp.float32)}
    _L3_ffn_all = _L3_ffn_setup()
    _L3_ffn_in = {k: v for k, v in _L3_ffn_all.items() if k in ('Wg', 'bg', 'W1', 'b1', 'W2', 'b2')}
    del _L3_ffn_all
    return {'x': x, 'ctx_1024': ctx_1024, 'itok_BxS_0_511': itok_BxS_0_511, 'mask_BxS2_if1': mask_BxS2_if1, 'mask_BxS2_bf1': mask_BxS2_bf1, 'L0_xattn_w_q': _L0_xattn_in['w_q'], 'L0_xattn_w_k': _L0_xattn_in['w_k'], 'L0_xattn_w_v': _L0_xattn_in['w_v'], 'L0_xattn_w_o': _L0_xattn_in['w_o'], 'L0_ffn_w_gate': _L0_ffn_in['w_gate'], 'L0_ffn_w_up': _L0_ffn_in['w_up'], 'L0_ffn_w_down': _L0_ffn_in['w_down'], 'L1_xattn_Wq': _L1_xattn_in['Wq'], 'L1_xattn_Wkv': _L1_xattn_in['Wkv'], 'L1_xattn_Wo': _L1_xattn_in['Wo'], 'L1_ffn_wg': _L1_ffn_in['wg'], 'L1_ffn_w1': _L1_ffn_in['w1'], 'L1_ffn_b1': _L1_ffn_in['b1'], 'L1_ffn_w2': _L1_ffn_in['w2'], 'L1_ffn_b2': _L1_ffn_in['b2'], 'L2_xattn_gamma_x': _L2_xattn_in['gamma_x'], 'L2_xattn_beta_x': _L2_xattn_in['beta_x'], 'L2_xattn_gamma_l': _L2_xattn_in['gamma_l'], 'L2_xattn_beta_l': _L2_xattn_in['beta_l'], 'L2_xattn_Wq': _L2_xattn_in['Wq'], 'L2_xattn_Wkv': _L2_xattn_in['Wkv'], 'L2_xattn_Wo': _L2_xattn_in['Wo'], 'L2_ffn_Wr': _L2_ffn_in['Wr'], 'L2_ffn_Wu': _L2_ffn_in['Wu'], 'L2_ffn_Wg': _L2_ffn_in['Wg'], 'L2_ffn_Wd': _L2_ffn_in['Wd'], 'L2_ffn_Wu_s': _L2_ffn_in['Wu_s'], 'L2_ffn_Wg_s': _L2_ffn_in['Wg_s'], 'L2_ffn_Wd_s': _L2_ffn_in['Wd_s'], 'L3_xattn_Wq': _L3_xattn_in['Wq'], 'L3_xattn_Wkv': _L3_xattn_in['Wkv'], 'L3_xattn_Wout': _L3_xattn_in['Wout'], 'L3_xattn_b_out': _L3_xattn_in['b_out'], 'L3_ffn_Wg': _L3_ffn_in['Wg'], 'L3_ffn_bg': _L3_ffn_in['bg'], 'L3_ffn_W1': _L3_ffn_in['W1'], 'L3_ffn_b1': _L3_ffn_in['b1'], 'L3_ffn_W2': _L3_ffn_in['W2'], 'L3_ffn_b2': _L3_ffn_in['b2']}

def reference(x, ctx_1024, itok_BxS_0_511, mask_BxS2_if1, mask_BxS2_bf1, L0_xattn_w_q, L0_xattn_w_k, L0_xattn_w_v, L0_xattn_w_o, L0_ffn_w_gate, L0_ffn_w_up, L0_ffn_w_down, L1_xattn_Wq, L1_xattn_Wkv, L1_xattn_Wo, L1_ffn_wg, L1_ffn_w1, L1_ffn_b1, L1_ffn_w2, L1_ffn_b2, L2_xattn_gamma_x, L2_xattn_beta_x, L2_xattn_gamma_l, L2_xattn_beta_l, L2_xattn_Wq, L2_xattn_Wkv, L2_xattn_Wo, L2_ffn_Wr, L2_ffn_Wu, L2_ffn_Wg, L2_ffn_Wd, L2_ffn_Wu_s, L2_ffn_Wg_s, L2_ffn_Wd_s, L3_xattn_Wq, L3_xattn_Wkv, L3_xattn_Wout, L3_xattn_b_out, L3_ffn_Wg, L3_ffn_bg, L3_ffn_W1, L3_ffn_b1, L3_ffn_W2, L3_ffn_b2):
    import jax
    import jax.numpy as jnp

    def _L0_xattn_ref(query, key, value, attention_mask, w_q, w_k, w_v, w_o):
        import jax, jax.numpy as jnp
        import numpy as np
        D_MODEL = 128
        NUM_HEADS = 16
        D_K = D_MODEL // NUM_HEADS
        B, S, _ = query.shape

        def proj(x, w):
            y = jnp.einsum('bsd,ed->bse', x, w)
            return y.reshape(B, S, NUM_HEADS, D_K).transpose(0, 2, 1, 3)
        q = proj(query, w_q)
        k = proj(key, w_k)
        v = proj(value, w_v)
        scores = jnp.einsum('bhqd,bhkd->bhqk', q, k) / jnp.sqrt(jnp.float32(D_K))
        mask = attention_mask[:, None, None, :] == 0
        scores = jnp.where(mask, jnp.float32(-1000000000.0), scores)
        attn = jax.nn.softmax(scores, axis=-1)
        context = jnp.einsum('bhqk,bhkd->bhqd', attn, v)
        context = context.transpose(0, 2, 1, 3).reshape(B, S, D_MODEL)
        return jnp.einsum('bsd,ed->bse', context, w_o)

    def _L0_ffn_ref(x, w_gate, w_up, w_down):
        import jax, jax.numpy as jnp
        import numpy as np
        BLOCK = 32
        W_BITS = 4
        ACT_BITS = 16

        def act_qdq(x):
            qmax = 2.0 ** (ACT_BITS - 1) - 1.0
            scale = jnp.maximum(jnp.max(jnp.abs(x)) / qmax, 1e-12)
            return jnp.clip(jnp.round(x / scale), -qmax - 1.0, qmax) * scale

        def fixed_qdq_u16(x):
            scale = 1.0 / 65536.0
            return jnp.clip(jnp.round(x / scale), 0.0, 65535.0) * scale

        def lpbq_dequant(w):
            O, I = w.shape
            qmax = 2.0 ** (W_BITS - 1) - 1.0
            wb = w.reshape(O, I // BLOCK, BLOCK)
            s = jnp.maximum(jnp.max(jnp.abs(wb), axis=-1, keepdims=True) / qmax, 1e-12)
            wq = jnp.clip(jnp.round(wb / s), -qmax - 1.0, qmax) * s
            return wq.reshape(O, I)
        x = act_qdq(x)
        up = act_qdq(x @ lpbq_dequant(w_up).T)
        gate = act_qdq(x @ lpbq_dequant(w_gate).T)
        sig = fixed_qdq_u16(jax.nn.sigmoid(gate))
        gate = act_qdq(gate * sig)
        o = act_qdq(gate * up)
        return o @ lpbq_dequant(w_down).T

    def _L1_xattn_ref(q, kv_src, seg_id, Wq, Wkv, Wo):
        import jax, jax.numpy as jnp
        import numpy as np
        Q_DIM = 128
        KV_DIM = 128
        D_ATTN = 128
        N_HEADS = 16
        HDIM = D_ATTN // N_HEADS
        LOOKBACK = 3
        KW = LOOKBACK + 1
        SCALE = HDIM ** (-0.5)
        B, LQ, LKV = (4, 512, 64)

        def _split_heads(x):
            b, l, _ = x.shape
            return x.reshape(b, l, N_HEADS, HDIM).transpose(0, 2, 1, 3)
        b, lq, _ = q.shape
        lkv = kv_src.shape[1]
        qh = _split_heads(q @ Wq.T)
        kv = kv_src @ Wkv.T
        k, v = jnp.split(kv, 2, axis=-1)
        kh = _split_heads(k)
        vh = _split_heads(v)
        offsets = jnp.arange(KW)
        gather = seg_id[:, :, None] - offsets
        neg_mask = gather < 0
        gc = jnp.clip(gather, 0, lkv - 1)
        b_idx = jnp.arange(b)[:, None, None]
        k_sel = kh[b_idx, :, gc].transpose(0, 3, 1, 2, 4)
        v_sel = vh[b_idx, :, gc].transpose(0, 3, 1, 2, 4)
        scores = jnp.einsum('bhqd,bhqkd->bhqk', qh, k_sel) * SCALE
        neg_inf = jnp.finfo(scores.dtype).min
        scores = jnp.where(neg_mask[:, None, :, :], neg_inf, scores)
        probs = jax.nn.softmax(scores, axis=-1)
        out = jnp.einsum('bhqk,bhqkd->bhqd', probs, v_sel)
        out = out.transpose(0, 2, 1, 3).reshape(b, lq, D_ATTN)
        return out @ Wo.T

    def _L1_ffn_ref(hidden_states, wg, w1, b1, w2, b2):
        import jax, jax.numpy as jnp
        import numpy as np
        B, T, M = hidden_states.shape
        E = wg.shape[1]
        S = B * T
        MIN_CAPACITY = 4
        C = max((S + E - 1) // E, MIN_CAPACITY)
        x = hidden_states.reshape(S, M)
        logits = x @ wg
        gates = jax.nn.softmax(logits, axis=-1)
        idx = jnp.argmax(gates, axis=-1)
        mask1 = jax.nn.one_hot(idx, E, dtype=gates.dtype)
        l_aux = jnp.sum(gates.mean(0) * mask1.mean(0)) * E
        locations1 = jnp.cumsum(mask1, axis=0) - 1.0
        mask1 = mask1 * (locations1 < C)
        gates1_s = jnp.sum(gates * mask1, axis=1)
        loc_s = jnp.sum(locations1 * mask1, axis=1).astype(jnp.int32)
        loc_sc = jax.nn.one_hot(loc_s, C, dtype=gates.dtype)
        combine_weights = jnp.einsum('se,sc->sec', gates1_s[:, None] * mask1, loc_sc)
        dispatch_mask = (combine_weights > 0).astype(x.dtype)
        dispatched = jnp.einsum('sec,sm->ecm', dispatch_mask, x)
        h = jax.nn.gelu(jnp.einsum('ecm,emf->ecf', dispatched, w1) + b1[:, None, :])
        expert_out = jnp.einsum('ecf,efm->ecm', h, w2) + b2[:, None, :]
        out = jnp.einsum('sec,ecm->sm', combine_weights, expert_out)
        return out.reshape(B, T, M)

    def _L2_xattn_ref(x, latents, gamma_x, beta_x, gamma_l, beta_l, Wq, Wkv, Wo):
        import jax, jax.numpy as jnp
        import numpy as np
        DIM = 128
        HEAD_DIM = 64
        NUM_HEADS = 8
        INNER = HEAD_DIM * NUM_HEADS
        ROT_DIM = HEAD_DIM
        ROPE_BASE = 10000.0
        EPS = 1e-05

        def layer_norm(x, g, b):
            mu = jnp.mean(x, axis=-1, keepdims=True)
            var = jnp.var(x, axis=-1, keepdims=True)
            return (x - mu) * jax.lax.rsqrt(var + EPS) * g + b

        def rope_rotate_k(k):
            n = k.shape[1]
            half = ROT_DIM // 2
            inv_freq = 1.0 / ROPE_BASE ** (jnp.arange(0, ROT_DIM, 2, dtype=jnp.float32) / ROT_DIM)
            theta = jnp.arange(n, dtype=jnp.float32)[:, None] * inv_freq[None, :]
            angles = jnp.concatenate([theta, theta], axis=-1)
            cos = jnp.cos(angles)[None, :, None, :].astype(k.dtype)
            sin = jnp.sin(angles)[None, :, None, :].astype(k.dtype)
            k_rope, k_pass = (k[..., :ROT_DIM], k[..., ROT_DIM:])
            neg_half = jnp.concatenate([-k_rope[..., half:], k_rope[..., :half]], axis=-1)
            k_rope = k_rope * cos + neg_half * sin
            return jnp.concatenate([k_rope, k_pass], axis=-1)
        b, n, _ = x.shape
        m = latents.shape[1]
        h, d = (NUM_HEADS, HEAD_DIM)
        scale = d ** (-0.5)
        xn = layer_norm(x, gamma_x, beta_x)
        ln = layer_norm(latents, gamma_l, beta_l)
        q = (ln @ Wq).reshape(b, m, h, d)
        kv_x = xn @ Wkv
        k_x, v_x = (kv_x[..., :INNER], kv_x[..., INNER:])
        kv_l = ln @ Wkv
        k_l, v_l = (kv_l[..., :INNER], kv_l[..., INNER:])
        k_x = k_x.reshape(b, n, h, d)
        v_x = v_x.reshape(b, n, h, d)
        k_x = rope_rotate_k(k_x)
        q = jnp.transpose(q, (0, 2, 1, 3)) * scale
        k_x = jnp.transpose(k_x, (0, 2, 1, 3))
        v_x = jnp.transpose(v_x, (0, 2, 1, 3))
        k_l = jnp.transpose(k_l.reshape(b, m, h, d), (0, 2, 1, 3))
        v_l = jnp.transpose(v_l.reshape(b, m, h, d), (0, 2, 1, 3))
        k = jnp.concatenate([k_x, k_l], axis=2)
        v = jnp.concatenate([v_x, v_l], axis=2)
        sim = jnp.einsum('bhid,bhjd->bhij', q, k)
        attn = jax.nn.softmax(sim, axis=-1)
        out = jnp.einsum('bhij,bhjd->bhid', attn, v)
        out = jnp.transpose(out, (0, 2, 1, 3)).reshape(b, m, INNER)
        return out @ Wo

    def _L2_ffn_ref(x, Wr, Wu, Wg, Wd, Wu_s, Wg_s, Wd_s):
        import jax, jax.numpy as jnp
        import numpy as np
        DIM = 128
        HID = 512
        NUM_EXPERTS = 8
        TOP_K = 2
        ALPHA = 2.0
        B, S = (4, 256)

        def _swiglu(x, wu, wg, wd):
            up = x @ wu
            g = x @ wg
            gate = jax.nn.sigmoid(g) * g
            return up * gate @ wd
        logits = x @ Wr
        probs = jax.nn.softmax(logits, axis=-1)
        topk_vals, topk_idx = jax.lax.top_k(probs, TOP_K)
        out = jnp.zeros_like(x)
        for i in range(TOP_K - 1):
            p = topk_vals[..., i:i + 1]
            ind = topk_idx[..., i]
            acc = jnp.zeros_like(x)
            for j in range(NUM_EXPERTS - 1):
                mask = (ind == j).astype(x.dtype)[..., None]
                acc = acc + _swiglu(x, Wu[j], Wg[j], Wd[j]) * mask
            out = out + ALPHA * p * acc
        out = out + _swiglu(x, Wu_s, Wg_s, Wd_s)
        return out

    def _L3_xattn_ref(x, context, mask, Wq, Wkv, Wout, b_out):
        import jax, jax.numpy as jnp
        import numpy as np
        HEADS = 16
        DIM_HEAD = 64
        SCALE = DIM_HEAD ** (-0.5)
        B, Nq, _ = x.shape
        Nkv = context.shape[1]
        q = x @ Wq.T
        kv = context @ Wkv.T
        k, v = jnp.split(kv, 2, axis=-1)
        q = q.reshape(B, Nq, HEADS, DIM_HEAD).transpose(0, 2, 1, 3)
        k = k.reshape(B, Nkv, HEADS, DIM_HEAD).transpose(0, 2, 1, 3)
        v = v.reshape(B, Nkv, HEADS, DIM_HEAD).transpose(0, 2, 1, 3)
        sim = jnp.einsum('bhid,bhjd->bhij', q, k) * SCALE
        max_neg = -jnp.finfo(sim.dtype).max
        sim = jnp.where(mask[:, None, None, :], sim, max_neg)
        attn = jax.nn.softmax(sim, axis=-1)
        out = jnp.einsum('bhij,bhjd->bhid', attn, v)
        out = out.transpose(0, 2, 1, 3).reshape(B, Nq, HEADS * DIM_HEAD)
        return out @ Wout.T + b_out

    def _L3_ffn_ref(x, Wg, bg, W1, b1, W2, b2):
        import jax, jax.numpy as jnp
        import numpy as np
        E = 8
        K = 2
        CF = 1.2
        D = 128
        F = 512
        B, S = (4, 128)
        Bx, Sx, Dx = x.shape
        T = Bx * Sx
        xt = x.reshape(T, Dx)
        logits = xt @ Wg + bg
        probs = jax.nn.softmax(logits, axis=-1)
        gate_vals, exp_idx = jax.lax.top_k(probs, K)
        gate_vals = gate_vals / jnp.sum(gate_vals, axis=-1, keepdims=True)
        capacity = int(np.ceil(CF * T * K / E))
        eidx = exp_idx.T.reshape(-1)
        gv = gate_vals.T.reshape(-1)
        oh = jax.nn.one_hot(eidx, E, dtype=jnp.int32)
        pos = jnp.sum((jnp.cumsum(oh, axis=0) - oh) * oh, axis=-1)
        keep = pos < capacity
        pos_c = jnp.where(keep, pos, capacity)
        xk = jnp.tile(xt, (K, 1))
        buf = jnp.zeros((E, capacity + 1, Dx), x.dtype)
        buf = buf.at[eidx, pos_c].add(jnp.where(keep[:, None], xk, 0.0))
        buf = buf[:, :capacity]
        h = jax.nn.gelu(jnp.einsum('ecd,edf->ecf', buf, W1) + b1[:, None, :], approximate=True)
        ye = jnp.einsum('ecf,efd->ecd', h, W2) + b2[:, None, :]
        ye = jnp.concatenate([ye, jnp.zeros((E, 1, Dx), ye.dtype)], axis=1)
        gathered = ye[eidx, pos_c] * (gv * keep.astype(gv.dtype))[:, None]
        out = jnp.sum(gathered.reshape(K, T, Dx), axis=0)
        return out.reshape(Bx, Sx, Dx)
    x = x + _L0_xattn_ref(_layernorm(x, axis=-1), ctx_1024, ctx_1024, mask_BxS2_if1, L0_xattn_w_q, L0_xattn_w_k, L0_xattn_w_v, L0_xattn_w_o)
    x = x + _L0_ffn_ref(_layernorm(x, axis=-1), L0_ffn_w_gate, L0_ffn_w_up, L0_ffn_w_down)
    x = x + _L1_xattn_ref(_layernorm(x, axis=-1), ctx_1024, itok_BxS_0_511, L1_xattn_Wq, L1_xattn_Wkv, L1_xattn_Wo)
    x = x + _L1_ffn_ref(_layernorm(x, axis=-1), L1_ffn_wg, L1_ffn_w1, L1_ffn_b1, L1_ffn_w2, L1_ffn_b2)
    x = x + _L2_xattn_ref(ctx_1024, _layernorm(x, axis=-1), L2_xattn_gamma_x, L2_xattn_beta_x, L2_xattn_gamma_l, L2_xattn_beta_l, L2_xattn_Wq, L2_xattn_Wkv, L2_xattn_Wo)
    x = x + _L2_ffn_ref(_layernorm(x, axis=-1), L2_ffn_Wr, L2_ffn_Wu, L2_ffn_Wg, L2_ffn_Wd, L2_ffn_Wu_s, L2_ffn_Wg_s, L2_ffn_Wd_s)
    x = x + _L3_xattn_ref(_layernorm(x, axis=-1), ctx_1024, mask_BxS2_bf1, L3_xattn_Wq, L3_xattn_Wkv, L3_xattn_Wout, L3_xattn_b_out)
    x = x + _L3_ffn_ref(_layernorm(x, axis=-1), L3_ffn_Wg, L3_ffn_bg, L3_ffn_W1, L3_ffn_b1, L3_ffn_W2, L3_ffn_b2)
    return x

_drawn_inputs = setup_inputs


def setup_inputs(seed=0):
    import zlib

    import numpy as np

    out = dict(_drawn_inputs(seed))
    spreads = {'L1_ffn_b1': (0.0, 0.1),
     'L1_ffn_b2': (0.0, 0.1),
     'L2_xattn_gamma_x': (1.0, 0.2),
     'L2_xattn_beta_x': (0.0, 0.1),
     'L2_xattn_gamma_l': (1.0, 0.2),
     'L2_xattn_beta_l': (0.0, 0.1),
     'L3_xattn_b_out': (0.0, 0.1),
     'L3_ffn_bg': (0.0, 0.1),
     'L3_ffn_b1': (0.0, 0.318),
     'L3_ffn_b2': (0.0, 0.1)}
    factors = {'L2_ffn_Wr': 8.0,
     'L2_ffn_Wu': 8.0,
     'L2_ffn_Wg': 8.0,
     'L2_ffn_Wd': 8.0,
     'L2_ffn_Wu_s': 8.0,
     'L2_ffn_Wg_s': 8.0,
     'L2_ffn_Wd_s': 8.0}
    for name, (base, spread) in spreads.items():
        noise = np.random.default_rng([zlib.crc32(name.encode()), seed]).standard_normal(out[name].shape)
        drawn = base * np.exp(spread * noise) if base else spread * noise
        out[name] = jnp.asarray(drawn.astype(out[name].dtype))
    for name, factor in factors.items():
        out[name] = (out[name] * factor).astype(out[name].dtype)
    return out
```

```python
from contextlib import ExitStack

import numpy as np

import concourse.bass as bass
from concourse import mybir

F32 = mybir.dt.float32
BF16 = mybir.dt.bfloat16
I32 = mybir.dt.int32
U32 = mybir.dt.uint32
ACT = mybir.ActivationFunctionType
ALU = mybir.AluOpType
AX = mybir.AxisListType.X

P = 128
B, S, D = 64, 64, 128
NTOK = B * S
NT = NTOK // P
EPS = 1e-5
NEG = 1e30
ROUND = 12582912.0


def tile_of(ap, t):
    if isinstance(t, int):
        return ap[:, t, :]
    return ap[:, bass.ds(t, 1), :].rearrange("p a n -> p (a n)")


def wait(eng, sem, value):
    if not isinstance(value, int) or value > 0:
        eng.wait_ge(sem, value)


class Turn:

    def __init__(self, t, m, on, unroll, start):
        self.t, self.m, self.on, self.unroll, self.start = t, m, on, unroll, start

    def tile(self, p):
        return self.t - p, (self.m - p) % self.unroll

    def group(self, p):
        if isinstance(self.t, int):
            return (self.t - p) // self.unroll
        i, first = self.start
        return i + (first - p) // self.unroll

    def half(self, p):
        if isinstance(self.t, int):
            return (self.t - p) // 2
        i, first = self.start
        return i * (self.unroll // 2) + (first - p) // 2


def pipeline_by(eng, depth, step, tiles, unroll, lead=None):
    lead = depth - 1 if lead is None else lead

    def turn(t):
        step(Turn(t, t % unroll, [0 <= t - p < tiles for p in range(depth)], unroll, None))

    for t in range(lead):
        turn(t)
    full = (tiles - lead) // unroll
    with eng.Fori(0, full) as i:
        for j in range(unroll):
            first = lead + j
            step(Turn(i * unroll + first, first % unroll, [True] * depth, unroll, (i, first)))
    for t in range(lead + unroll * full, tiles + depth - 1):
        turn(t)


def pipeline(eng, depth, step, tiles=NT, lead=None):
    pipeline_by(eng, depth, step, tiles, 2, lead)


def up_to(value, most=NT):
    return min(value, most) if isinstance(value, int) else value


class Stage:

    def __init__(self, nc, name):
        self.nc, self.name, self.ctx, self.sems = nc, name, ExitStack(), []
        self.ctx.callback(self.clear)

    def clear(self):
        self.nc.clear_and_free_semaphores(self.sems)
        self.nc.all_engine_barrier()

    def sb(self, name, shape, dt=F32):
        return self.ctx.enter_context(self.nc.sbuf_tensor(f"{self.name}_{name}", shape, dt))

    def ps(self, name, shape, dt=F32):
        return self.ctx.enter_context(self.nc.psum_tensor(f"{self.name}_{name}", shape, dt))

    def sem(self, name):
        self.sems.append(self.nc.alloc_semaphore(name=f"{self.name}_{name}"))
        return self.sems[-1]


class Chain:

    def __init__(self, eng, sem, per_turn, turn):
        self.eng, self.sem, self.per_turn = eng, sem, per_turn
        self.base, self.n = turn * per_turn, 0

    def __call__(self, ins):
        self.n += 1
        ins.then_inc(self.sem, 1)
        self.eng.wait_ge(self.sem, self.base + self.n)

    def close(self):
        assert self.n == self.per_turn, (self.n, self.per_turn)


def finish_statistics(nc, act, dve, k, part, sem):
    st, mu, rs = k.stats, k.mean, k.rstd
    ta, tb, va = k.tmp_a, k.tmp_b, k.var
    if part == "dve":
        c = Chain(dve, sem, 0, 0)
        c(nc.vector.tensor_tensor(mu[:], st[:, :, 1], st[:, :, 4], ALU.add))
        c(nc.vector.tensor_scalar(mu[:], mu[:], 0.5, None, ALU.mult))
        c(nc.vector.tensor_tensor(ta[:], st[:, :, 1], st[:, :, 4], ALU.subtract))
        c(nc.vector.tensor_tensor(ta[:], ta[:], ta[:], ALU.mult))
        c(nc.vector.tensor_tensor(tb[:], st[:, :, 2], st[:, :, 5], ALU.add))
        c(nc.vector.tensor_scalar(tb[:], tb[:], 1.0 / D, None, ALU.mult))
        c(nc.vector.tensor_scalar(ta[:], ta[:], 0.25, None, ALU.mult))
        c(nc.vector.tensor_tensor(va[:], ta[:], tb[:], ALU.add))
        inverse_root(nc, dve, c, k, va, rs)
    else:
        act.wait_ge(sem, 9)
        nc.scalar.activation(k.root[:], k.vareps[:], ACT.Sqrt).then_inc(sem, 1)


def inverse_root(nc, dve, c, k, va, rs):
    c(nc.vector.tensor_scalar(k.vareps[:], va[:], EPS, None, ALU.add))
    c.n += 1
    dve.wait_ge(c.sem, c.base + c.n)
    c(nc.vector.reciprocal(rs[:], k.root[:]))
    c(nc.vector.tensor_tensor(k.tmp_a[:], rs[:], rs[:], ALU.mult))
    c(nc.vector.tensor_tensor(k.tmp_a[:], k.tmp_a[:], k.vareps[:], ALU.mult))
    c(nc.vector.tensor_scalar(k.tmp_a[:], k.tmp_a[:], -0.5, 1.5, ALU.mult, ALU.add))
    c(nc.vector.tensor_tensor(rs[:], rs[:], k.tmp_a[:], ALU.mult))


class Kept:
    pass


def add_residual(nc, dve, k, c, t, r):
    c(nc.vector.tensor_tensor(tile_of(k.x, t), tile_of(k.x, t), r, ALU.add))
    return nc.vector.bn_stats(tile_of(k.stats, t), tile_of(k.x, t))


def load_stage(nc, k, x, ctx, itok):
    s = Stage(nc, "load")
    with s.ctx:
        loaded = s.sem("loaded")
        ident_set, ctx_t, ctx_copied = s.sem("ident_set"), s.sem("ctx_t"), s.sem("ctx_copied")
        step = s.sem("step")
        pt = [s.ps(f"pt{i}", [P, 4, P]) for i in range(2)]
        block = s.ctx.enter_context(nc.Block())

        @block.sync
        def _(sp):
            sp.dma_start(k.c[:], ctx.rearrange("(t b) s d -> (b s) t d", b=2)).then_inc(loaded, 16)
            sp.wait_ge(loaded, 16)
            sp.dma_start(k.x[:], x.rearrange("(t b) s d -> (b s) t d", b=2)).then_inc(loaded, 16)

        @block.gpsimd
        def _(pool):
            nc.gpsimd.memset(k.ident[:], 0.0).then_inc(ident_set, 1)
            pool.wait_ge(ident_set, 1)
            nc.gpsimd.affine_select(out=k.ident[:], in_=k.ident[:], compare_op=ALU.not_equal, fill=1.0, base=0,
                                    pattern=[[-1, P]], channel_multiplier=1).then_inc(ident_set, 1)

        @block.tensor
        def _(pe):
            pe.wait_ge(ident_set, 2)
            pe.wait_ge(loaded, 16)
            for g in range(NT // 4):
                wait(pe, ctx_copied, g - 1)
                for j in range(4):
                    last = nc.tensor.transpose(pt[g % 2][:, j, :], k.c[:, 4 * g + j, :], k.ident[:])
                last.then_inc(ctx_t, 1)

        @block.scalar
        def _(act):
            for g in range(NT // 4):
                act.wait_ge(ctx_t, g + 1)
                nc.scalar.activation(k.ct[:, 4 * g:4 * g + 4, :], pt[g % 2][:], ACT.Copy).then_inc(ctx_copied, 1)

        @block.vector
        def _(dve):
            dve.wait_ge(loaded, 32)
            for t in range(NT):
                nc.vector.bn_stats(k.stats[:, t, :], k.x[:, t, :]).then_inc(step, 1)


def attention_8(nc, k, mask, w_q, w_k, w_v, w_o):
    H, HD = 16, 8
    scale = float(HD) ** -0.5
    s = Stage(nc, "a0")
    with s.ctx:
        wn, wt = s.sb("wn", [P, 4, P]), s.sb("wt", [P, 4, P])
        head = s.sb("head", [P, 8])
        mask_i, mask_f = s.sb("mask_i", [P, NT, P], I32), s.sb("mask_f", [P, NT, P], BF16)
        mb_i, mb = s.sb("mb_i", [2, NT, S], I32), s.sb("mb", [2, NT, S], BF16)
        mb_f = s.sb("mb_f", [2, NT, S])
        own = s.sb("own", [2, P], BF16)
        xn, xt = s.sb("xn", [P, 2, P]), s.sb("xt", [P, 2, P])
        ct, cm = s.sb("ct", [P, 2, P]), s.sb("cm", [P, 2, P])
        q = s.sb("q", [P, 2, 2, P])
        kt = s.sb("kt", [P, 2, 2, S])
        ke = s.sb("ke", [P, 2, 2, 8, S])
        v = s.sb("v", [P, 2, 2, 8, 2, HD])
        pr = s.sb("pr", [P, 2, H, S])
        top, tot, rec = s.sb("top", [P, 2, H]), s.sb("tot", [P, 2, H]), s.sb("rec", [P, 2, H])
        prt = s.sb("prt", [P, 8, P])
        o, ot = s.sb("o", [P, 2, H, HD]), s.sb("ot", [P, P])
        p_xt, p_qkv = s.ps("p_xt", [P, 4, P]), s.ps("p_qkv", [P, 4, P])
        p_s, p_t = s.ps("p_s", [P, 2, 8, S]), s.ps("p_t", [P, 8, P])
        p_o, p_r = s.ps("p_o", [P, 4, H, HD]), s.ps("p_r", [P, 4, P])
        names = ("w_in w_t w_ready masks_in consts stats mask_steps xn_ready ct_ready xt_done xt_ready proj_done "
                 "qkv_ready ke_ready s_done top_done sub_done exp_done rec_steps t_done prt_ready pv_done o_ready "
                 "v_done v_ready ot_done ot_ready wo_done add_step add_done").split()
        g = {n: s.sem(n) for n in names}
        block = s.ctx.enter_context(nc.Block())

        @block.sync
        def _(sp):
            for j, w in enumerate((w_q, w_k, w_v, w_o)):
                sp.dma_start(wn[:, j, :], w).then_inc(g["w_in"], 16)
            per_batch = mask.rearrange("(t b) s -> b t s", b=2)
            sp.dma_start(mb_i[:], per_batch).then_inc(g["masks_in"], 16)
            sp.dma_start(mask_i[:].rearrange("p t n -> p (t n)"),
                         mask.rearrange("b s -> (b s)").partition_broadcast(P)).then_inc(g["masks_in"], 16)

        @block.gpsimd
        def _(pool):
            nc.gpsimd.memset(head[:], 1.0).then_inc(g["consts"], 1)
            nc.gpsimd.memset(own[:], 1.0).then_inc(g["consts"], 1)
            nc.gpsimd.memset(q[:], 0.0).then_inc(g["consts"], 1)
            nc.gpsimd.memset(v[:], 0.0).then_inc(g["consts"], 1)
            pool.wait_ge(g["consts"], 4)
            nc.gpsimd.affine_select(out=own[:], in_=own[:], compare_op=ALU.is_ge, fill=0.0, base=0,
                                    pattern=[[1, P]], channel_multiplier=-S).then_inc(g["consts"], 1)
            for b in range(2):
                part = head[64 * b:64 * b + 64, :]
                nc.gpsimd.affine_select(out=part, in_=part, compare_op=ALU.is_ge, fill=0.0, base=0,
                                        pattern=[[-HD, 8]], channel_multiplier=1).then_inc(g["consts"], 1)
            pool.wait_ge(g["consts"], 7)
            nc.gpsimd.affine_select(out=own[:], in_=own[:], compare_op=ALU.is_ge, fill=0.0, base=S - 1,
                                    pattern=[[-1, P]], channel_multiplier=S).then_inc(g["consts"], 1)
            for b in range(2):
                part = head[64 * b:64 * b + 64, :]
                nc.gpsimd.affine_select(out=part, in_=part, compare_op=ALU.is_ge, fill=0.0, base=HD - 1,
                                        pattern=[[HD, 8]], channel_multiplier=-1).then_inc(g["consts"], 1)
            pool.wait_ge(g["consts"], 10)
            pool.wait_ge(g["mask_steps"], 3)

            def step(turn):
                if turn.on[2]:
                    t, u = turn.tile(2)
                    wait(pool, g["proj_done"], t - 1)
                    wait(pool, g["v_done"], t - 1)
                    nc.gpsimd.tensor_copy(ct[:, u, :], tile_of(k.ct, t))
                    nc.gpsimd.tensor_tensor(cm[:, u, :], tile_of(k.ct, t), tile_of(mask_f, t), ALU.mult)\
                        .then_inc(g["ct_ready"], 1)
                    pool.wait_ge(g["qkv_ready"], t + 1)
                    wait(pool, g["s_done"], t - 1)
                    nc.gpsimd.tensor_tensor(
                        ke[:, u], kt[:, u].unsqueeze(2).broadcast_to([P, 2, 8, S]),
                        head[:].unsqueeze(1).unsqueeze(3).broadcast_to([P, 2, 8, S]), ALU.mult).then_inc(g["ke_ready"], 1)

            pipeline(pool, 6, step)

        @block.tensor
        def _(pe):
            pe.wait_ge(g["w_in"], 64)
            for j in range(4):
                last = nc.tensor.transpose(p_xt[:, j, :], wn[:, j, :], k.ident[:])
            last.then_inc(g["w_t"], 1)
            pe.wait_ge(g["w_ready"], 1)
            pe.wait_ge(g["consts"], 10)
            pe.wait_ge(g["mask_steps"], 3)

            def step(turn):
                if turn.on[3]:
                    t, u = turn.tile(3)
                    pe.wait_ge(g["ke_ready"], t + 1)
                    wait(pe, g["sub_done"], t)
                    bias = tile_of(mb, t).unsqueeze(1).broadcast_to([2, 8, S])
                    for h in range(2):
                        nc.tensor.matmul(p_s[:, h], own[:], bias, start=True, stop=False)
                        last = nc.tensor.matmul(p_s[:, h], q[:, u, h, :], ke[:, u, h], start=False, stop=True)
                    last.then_inc(g["s_done"], 1)
                if turn.on[3]:
                    t, u = turn.tile(3)
                    pe.wait_ge(g["ct_ready"], t + 1)
                    wait(pe, g["v_ready"], t)
                    wait(pe, g["add_done"], t - 2)
                    for h in range(2):
                        wv = wt[:, 2, :].rearrange("p (j h d) -> p j h d", j=8, h=2)[:, :, h, :]
                        for b in range(2):
                            last = nc.tensor.matmul(p_r[64 * h:64 * h + 64, 2, 64 * b:64 * b + 64],
                                                    ct[:, u, 64 * b:64 * b + 64], wv, start=True, stop=True)
                    last.then_inc(g["v_done"], 1)
                if turn.on[1]:
                    t, u = turn.tile(1)
                    pe.wait_ge(g["xn_ready"], t + 1)
                    wait(pe, g["xt_ready"], t)
                    nc.tensor.transpose(p_xt[:, 0, :], xn[:, u, :], k.ident[:]).then_inc(g["xt_done"], 1)
                if turn.on[4]:
                    t, u = turn.tile(4)
                    pe.wait_ge(g["exp_done"], t + 1)
                    wait(pe, g["prt_ready"], t)
                    for j in range(8):
                        last = nc.tensor.transpose(p_t[:, j, :], pr[:, u, 2 * j:2 * j + 2, :].rearrange("p h k -> p (h k)"), k.ident[:])
                    last.then_inc(g["t_done"], 1)
                if turn.on[5]:
                    t, u = turn.tile(5)
                    pe.wait_ge(g["o_ready"], t + 1)
                    pe.wait_ge(g["v_ready"], up_to(t + 3))
                    wait(pe, g["add_done"], t)
                    nc.tensor.transpose(p_r[:, 0, :], o[:, u].rearrange("p h d -> p (h d)"), k.ident[:]).then_inc(g["ot_done"], 1)
                if turn.on[2]:
                    t, u = turn.tile(2)
                    pe.wait_ge(g["xt_ready"], t + 1)
                    pe.wait_ge(g["ct_ready"], t + 1)
                    wait(pe, g["qkv_ready"], t)
                    for b in range(2):
                        rows = slice(64 * b, 64 * b + 64)
                        for h in range(2):
                            cols = slice(64 * h, 64 * h + 64)
                            nc.tensor.matmul(p_qkv[rows, 0, cols], wt[:, 0, cols], xt[:, u, rows], start=True, stop=True)
                            last = nc.tensor.matmul(p_qkv[rows, 1, cols], wt[:, 1, cols], cm[:, u, rows], start=True, stop=True)
                    last.then_inc(g["proj_done"], 1)
                if turn.on[5]:
                    t, u = turn.tile(5)
                    pe.wait_ge(g["ot_ready"], t + 1)
                    nc.tensor.matmul(p_r[:, 1, :], ot[:], wt[:, 3, :], start=True, stop=True).then_inc(g["wo_done"], 1)
                if turn.on[4]:
                    t, u = turn.tile(4)
                    pe.wait_ge(g["prt_ready"], t + 1)
                    wait(pe, g["o_ready"], t)
                    for b in range(2):
                        for j in range(8):
                            last = nc.tensor.matmul(p_o[64 * b:64 * b + 64, 0, 2 * j:2 * j + 2, :],
                                                    prt[:, j, 64 * b:64 * b + 64], v[:, u, b, j, :, :],
                                                    start=True, stop=True)
                    last.then_inc(g["pv_done"], 1)

            pipeline(pe, 6, step)

        @block.scalar
        def _(act):
            finish_statistics(nc, act, None, k, "act", g["stats"])
            act.wait_ge(g["w_t"], 1)
            nc.scalar.activation(wt[:], p_xt[:], ACT.Copy).then_inc(g["w_ready"], 1)
            act.wait_ge(g["consts"], 10)

            def step(turn):
                if turn.on[3]:
                    t, u = turn.tile(3)
                    act.wait_ge(g["v_done"], t + 1)
                    wait(act, g["pv_done"], t - 1)
                    for h in range(2):
                        rows = slice(64 * h, 64 * h + 64)
                        last = nc.scalar.activation(v[rows, u, :, :, h, :],
                                                    p_r[rows, 2, :].rearrange("p (b j d) -> p b j d", b=2, j=8), ACT.Copy)
                    last.then_inc(g["v_ready"], 1)
                if turn.on[1]:
                    t, u = turn.tile(1)
                    act.wait_ge(g["xt_done"], t + 1)
                    wait(act, g["proj_done"], t - 1)
                    nc.scalar.activation(xt[:, u, :], p_xt[:, 0, :], ACT.Copy).then_inc(g["xt_ready"], 1)
                if turn.on[4]:
                    t, u = turn.tile(4)
                    act.wait_ge(g["t_done"], t + 1)
                    wait(act, g["pv_done"], t)
                    nc.scalar.activation(prt[:], p_t[:], ACT.Copy).then_inc(g["prt_ready"], 1)
                if turn.on[5]:
                    t, u = turn.tile(5)
                    act.wait_ge(g["ot_done"], t + 1)
                    wait(act, g["wo_done"], t)
                    nc.scalar.activation(ot[:], p_r[:, 0, :], ACT.Copy).then_inc(g["ot_ready"], 1)
                if turn.on[2]:
                    t, u = turn.tile(2)
                    act.wait_ge(g["proj_done"], t + 1)
                    wait(act, g["s_done"], t - 1)
                    wait(act, g["ke_ready"], t - 1)
                    for b in range(2):
                        rows = slice(64 * b, 64 * b + 64)
                        nc.scalar.activation(q[rows, u, :, rows], p_qkv[rows, 0, :].rearrange("p (h n) -> p h n", h=2), ACT.Copy)
                    nc.scalar.activation(kt[:, u], p_qkv[:, 1, :].rearrange("p (h n) -> p h n", h=2), ACT.Copy)\
                        .then_inc(g["qkv_ready"], 1)
                if turn.on[3]:
                    t, u = turn.tile(3)
                    act.wait_ge(g["sub_done"], t + 1)
                    nc.scalar.activation(pr[:, u], pr[:, u], ACT.Exp, scale=scale).then_inc(g["exp_done"], 1)

            pipeline(act, 6, step)

        @block.vector
        def _(dve):
            finish_statistics(nc, None, dve, k, "dve", g["stats"])
            dve.wait_ge(g["masks_in"], 32)
            nc.vector.tensor_scalar(mask_f[:], mask_i[:], 0.0, None, ALU.not_equal).then_inc(g["mask_steps"], 1)
            nc.vector.tensor_scalar(mb_f[:], mb_i[:], 0.0, None, ALU.not_equal).then_inc(g["mask_steps"], 1)
            dve.wait_ge(g["mask_steps"], 2)
            nc.vector.tensor_scalar(mb[:], mb_f[:], NEG, -NEG, ALU.mult, ALU.add).then_inc(g["mask_steps"], 1)

            def step(turn):
                if turn.on[0]:
                    t, u = turn.tile(0)
                    wait(dve, g["xt_done"], t - 1)
                    nc.vector.tensor_scalar(xn[:, u, :], tile_of(k.x, t), k.mean[:, bass.ds(t, 1)], k.rstd[:, bass.ds(t, 1)],
                                            ALU.subtract, ALU.mult).then_inc(g["xn_ready"], 1)
                if turn.on[4]:
                    t, u = turn.tile(4)
                    dve.wait_ge(g["exp_done"], t + 1)
                    c = Chain(dve, g["rec_steps"], 2, t)
                    c(nc.vector.tensor_reduce(tot[:, u], pr[:, u], AX, ALU.add))
                    c(nc.vector.reciprocal(rec[:, u], tot[:, u]))
                if turn.on[3]:
                    t, u = turn.tile(3)
                    scores = p_s[:].rearrange("p g h k -> p (g h) k")
                    dve.wait_ge(g["s_done"], t + 1)
                    nc.vector.tensor_reduce(top[:, u], scores, AX, ALU.max).then_inc(g["top_done"], 1)
                    dve.wait_ge(g["top_done"], t + 1)
                    wait(dve, g["t_done"], t - 1)
                    nc.vector.tensor_tensor(pr[:, u], scores, top[:, u].unsqueeze(2).broadcast_to([P, H, S]), ALU.subtract)\
                        .then_inc(g["sub_done"], 1)
                if turn.on[5]:
                    t, u = turn.tile(5)
                    dve.wait_ge(g["wo_done"], t + 1)
                    c = Chain(dve, g["add_step"], 1, t)
                    add_residual(nc, dve, k, c, t, p_r[:, 1, :]).then_inc(g["add_done"], 1)
                if turn.on[4]:
                    t, u = turn.tile(4)
                    dve.wait_ge(g["pv_done"], t + 1)
                    wait(dve, g["ot_done"], t - 1)
                    nc.vector.tensor_tensor(o[:, u], p_o[:, 0], rec[:, u].unsqueeze(2).broadcast_to([P, H, HD]), ALU.mult)\
                        .then_inc(g["o_ready"], 1)

            pipeline(dve, 6, step)


def ffn_quantised(nc, k, w_gate, w_up, w_down):
    F, BLK = w_gate.shape[0], 32
    NF, NB = F // P, D // BLK
    CH = 512
    NC = NTOK // CH
    QMAX, WMAX = 32767.0, 7.0
    s = Stage(nc, "f0")
    with s.ctx:
        wn = s.sb("wn", [P, 3 * NF, P])
        wa, ws, wr = s.sb("wa", [P, 3 * NF, NB]), s.sb("ws", [P, 3 * NF, NB]), s.sb("wr", [P, 3 * NF, NB])
        wt = s.sb("wt", [P, 3 * NF, P])
        xq = s.sb("xq", [P, NT, P])
        up, gate = s.sb("up", [P, NF, NTOK]), s.sb("gate", [P, NF, NTOK])
        sig = s.sb("sig", [P, NTOK])
        most = s.sb("most", [P, 5, NF * NC])
        part, whole = s.sb("part", [P, 5]), s.sb("whole", [P, 5])
        sc, rc = s.sb("sc", [P, 5]), s.sb("rc", [P, 5])
        xt = s.sb("xt", [P, NT, P])
        pb = [s.ps(f"pb{i}", [P, CH]) for i in range(6)]
        names = ("w_in stats w_quantised w_t w_ready steps maxes xq_ready xt_done xt_ready up_done up_ready "
                 "gq_in sig_done down_done add_step add_done o_ready g_rounded").split()
        g = {n: s.sem(n) for n in names}
        block = s.ctx.enter_context(nc.Block())
        X, UP, GATE, PROD, OUT = range(5)

        @block.sync
        def _(sp):
            sp.dma_start(wn[:, 0:NF, :], w_up.rearrange("(j p) d -> p j d", p=P)).then_inc(g["w_in"], 16)
            sp.dma_start(wn[:, NF:2 * NF, :], w_gate.rearrange("(j p) d -> p j d", p=P)).then_inc(g["w_in"], 16)
            sp.dma_start(wn[:, 2 * NF:, :], w_down.rearrange("p (j d) -> p j d", d=P)).then_inc(g["w_in"], 16)

        @block.gpsimd
        def _(pool):
            for n in (X, UP, GATE, PROD, OUT):
                pool.wait_ge(g["maxes"], 2 * n + 1)
                nc.gpsimd.partition_all_reduce(whole[:, n:n + 1], part[:, n:n + 1], P, bass.bass_isa.ReduceOp.absmax)\
                    .then_inc(g["maxes"], 1)

        @block.tensor
        def _(pe):
            pe.wait_ge(g["w_quantised"], 1)
            for j in range(3 * NF):
                last = nc.tensor.transpose(pb[j // 4][:, (j % 4) * P:(j % 4 + 1) * P], wn[:, j, :], k.ident[:])
            last.then_inc(g["w_t"], 1)
            pe.wait_ge(g["xq_ready"], 1)
            for c in range(NC):
                wait(pe, g["xt_ready"], c - 1)
                for j in range(4):
                    last = nc.tensor.transpose(pb[4 + c % 2][:, j * P:(j + 1) * P], xq[:, 4 * c + j, :], k.ident[:])
                last.then_inc(g["xt_done"], 1)
            pe.wait_ge(g["w_ready"], 1)
            for n in range(2 * NF * NC):
                j, c = n // NC, n % NC
                if n < NC:
                    pe.wait_ge(g["xt_ready"], c + 1)
                wait(pe, g["up_ready"], n - 3)
                nc.tensor.matmul(pb[n % 4][:], wt[:, j, :], xt[:, 4 * c:4 * c + 4, :], start=True, stop=True)\
                    .then_inc(g["up_done"], 1)
            pe.wait_ge(g["up_ready"], 2 * NF * NC)
            pe.wait_ge(g["o_ready"], 1)
            for t in range(NT):
                wait(pe, g["add_done"], t - 3)
                for j in range(NF):
                    last = nc.tensor.matmul(pb[t % 4][:, 0:P], up[:, j, t * P:(t + 1) * P], wt[:, 2 * NF + j, :],
                                            start=(j == 0), stop=(j == NF - 1))
                last.then_inc(g["down_done"], 1)

        @block.scalar
        def _(act):
            finish_statistics(nc, act, None, k, "act", g["stats"])
            act.wait_ge(g["w_t"], 1)
            for b in range(3):
                n = min(4, 3 * NF - 4 * b)
                last = nc.scalar.activation(wt[:, 4 * b:4 * b + n, :], pb[b][:, 0:n * P].rearrange("p (j d) -> p j d", d=P), ACT.Copy)
            last.then_inc(g["w_ready"], 1)
            for c in range(NC):
                act.wait_ge(g["xt_done"], c + 1)
                nc.scalar.activation(xt[:, 4 * c:4 * c + 4, :], pb[4 + c % 2][:].rearrange("p (j d) -> p j d", d=P), ACT.Copy)\
                    .then_inc(g["xt_ready"], 1)
            for n in range(2 * NF * NC):
                j, c = n // NC, n % NC
                act.wait_ge(g["up_done"], n + 1)
                dst = up if j < NF else gate
                nc.scalar.activation(dst[:, j % NF, c * CH:(c + 1) * CH], pb[n % 4][:], ACT.Copy).then_inc(g["up_ready"], 1)
            for j in range(NF):
                act.wait_ge(g["gq_in"], j + 1)
                wait(act, g["g_rounded"], j)
                nc.scalar.activation(sig[:], gate[:, j, :], ACT.Sigmoid).then_inc(g["sig_done"], 1)

        @block.vector
        def _(dve):
            finish_statistics(nc, None, dve, k, "dve", g["stats"])
            c = Chain(dve, g["steps"], 0, 0)
            v = nc.vector

            def scales(n):
                dve.wait_ge(g["maxes"], 2 * n + 2)
                c(v.tensor_scalar(sc[:, n:n + 1], whole[:, n:n + 1], 1.0 / QMAX, 1e-12, ALU.mult, ALU.max))
                c(v.reciprocal(rc[:, n:n + 1], sc[:, n:n + 1]))

            def quantise(ap, n):
                c(v.tensor_scalar(ap, ap, rc[:, n:n + 1], ROUND, ALU.mult, ALU.add))
                c(v.tensor_scalar(ap, ap, ROUND, sc[:, n:n + 1], ALU.subtract, ALU.mult))

            dve.wait_ge(g["w_in"], 48)
            wb = wn[:].rearrange("p j (b n) -> p j b n", n=BLK)
            c(v.tensor_reduce(wa[:], wb, AX, ALU.max, apply_absolute_value=True))
            c(v.tensor_scalar(ws[:], wa[:], 1.0 / WMAX, 1e-12, ALU.mult, ALU.max))
            c(v.reciprocal(wr[:], ws[:]))
            flat = wn[:].rearrange("p j (b n) -> p (j b) n", n=BLK)
            spread = [P, 3 * NF * NB, BLK]
            c(v.tensor_tensor(flat, flat, wr[:].rearrange("p j b -> p (j b)").unsqueeze(2).broadcast_to(spread), ALU.mult))
            c(v.tensor_scalar(flat, flat, ROUND, ROUND, ALU.add, ALU.subtract))
            c(v.tensor_tensor(flat, flat, ws[:].rearrange("p j b -> p (j b)").unsqueeze(2).broadcast_to(spread), ALU.mult))
            v.tensor_copy(part[:, 0:1], ws[:, 0, 0:1]).then_inc(g["w_quantised"], 1)
            dve.wait_ge(g["w_quantised"], 1)
            c(v.tensor_tensor(xq[:], k.x[:], k.mean[:].unsqueeze(2).broadcast_to([P, NT, P]), ALU.subtract))
            c(v.tensor_tensor(xq[:], xq[:], k.rstd[:].unsqueeze(2).broadcast_to([P, NT, P]), ALU.mult))
            v.tensor_reduce(part[:, X:X + 1], xq[:].rearrange("p t d -> p (t d)"), AX, ALU.max, apply_absolute_value=True)\
                .then_inc(g["maxes"], 1)
            scales(X)
            quantise(xq[:], X)
            v.tensor_copy(most[:, 0, 0:1], sc[:, 0:1]).then_inc(g["xq_ready"], 1)
            dve.wait_ge(g["xq_ready"], 1)
            for n in range(2 * NF * NC):
                j, ch = n // NC, n % NC
                src = up if j < NF else gate
                dve.wait_ge(g["up_ready"], n + 1)
                kind = UP if j < NF else GATE
                ins = v.tensor_reduce(most[:, kind, (j % NF) * NC + ch:(j % NF) * NC + ch + 1],
                                      src[:, j % NF, ch * CH:(ch + 1) * CH], AX, ALU.max, apply_absolute_value=True)
                if n % (NF * NC) == NF * NC - 1:
                    c(ins)
                    v.tensor_reduce(part[:, kind:kind + 1], most[:, kind, :], AX, ALU.max).then_inc(g["maxes"], 1)
                    if kind == UP:
                        scales(UP)
            scales(GATE)
            for j in range(NF):
                c(v.tensor_scalar(gate[:, j], gate[:, j], rc[:, GATE:GATE + 1], ROUND, ALU.mult, ALU.add))
                v.tensor_scalar(gate[:, j], gate[:, j], ROUND, sc[:, GATE:GATE + 1], ALU.subtract, ALU.mult).then_inc(g["gq_in"], 1)
            for j in range(NF):
                quantise(up[:, j], UP)
                dve.wait_ge(g["sig_done"], j + 1)
                c(v.tensor_scalar(sig[:], sig[:], 65536.0, ROUND, ALU.mult, ALU.add))
                c(v.tensor_scalar(sig[:], sig[:], ROUND, 65535.0, ALU.subtract, ALU.min))
                v.scalar_tensor_tensor(gate[:, j], sig[:], 1.0 / 65536.0, gate[:, j], ALU.mult, ALU.mult).then_inc(g["g_rounded"], 1)
                dve.wait_ge(g["g_rounded"], j + 1)
                c(v.tensor_reduce(most[:, PROD, j:j + 1], gate[:, j], AX, ALU.max, apply_absolute_value=True))
            v.tensor_reduce(part[:, PROD:PROD + 1], most[:, PROD, 0:NF], AX, ALU.max).then_inc(g["maxes"], 1)
            scales(PROD)
            for j in range(NF):
                quantise(gate[:, j], PROD)
                c(v.tensor_tensor(up[:, j], up[:, j], gate[:, j], ALU.mult))
                c(v.tensor_reduce(most[:, OUT, j:j + 1], up[:, j], AX, ALU.max, apply_absolute_value=True))
            v.tensor_reduce(part[:, OUT:OUT + 1], most[:, OUT, 0:NF], AX, ALU.max).then_inc(g["maxes"], 1)
            scales(OUT)
            for j in range(NF):
                quantise(up[:, j], OUT)
            v.tensor_copy(most[:, 0, 0:1], sc[:, 0:1]).then_inc(g["o_ready"], 1)
            for t in range(NT):
                dve.wait_ge(g["down_done"], t + 1)
                c2 = Chain(dve, g["add_step"], 1, t)
                add_residual(nc, dve, k, c2, t, pb[t % 4][:, 0:P]).then_inc(g["add_done"], 1)


def attention_lookback(nc, k, seg, w_q, w_kv, w_o):
    H, HD, KW = 16, 8, 4
    scale = float(HD) ** -0.5
    s = Stage(nc, "a1")
    with s.ctx:
        wn, wt = s.sb("wn", [P, 4, P]), s.sb("wt", [P, 4, P])
        seg_i, row = s.sb("seg_i", [P, NT, P], I32), s.sb("row", [P, NT, P])
        seg_ti, seg_t = s.sb("seg_ti", [P, NT], I32), s.sb("seg_t", [P, NT])
        keys = s.sb("keys", [P, KW])
        bias = s.sb("bias", [P, NT, KW])
        xn, xt, ct = s.sb("xn", [P, 2, P]), s.sb("xt", [P, 2, P]), s.sb("ct", [P, 2, P])
        pick = s.sb("pick", [P, 2, KW, P])
        kv, q = s.sb("kv", [P, 2, 2 * P]), s.sb("q", [P, 2, P])
        prod = s.sb("prod", [P, KW, H, HD])
        sc, pr = s.sb("sc", [P, KW, H]), s.sb("pr", [P, 2, KW, H])
        vs = s.sb("vs", [P, 2, KW, P])
        top, tot, rec = s.sb("top", [P, H]), s.sb("tot", [P, H]), s.sb("rec", [P, H])
        mix = s.sb("mix", [P, KW, H, HD])
        o, ot = s.sb("o", [P, 2, P]), s.sb("ot", [P, P])
        p_x, p_q, p_kv, p_r = (s.ps(n, [P, 4, P]) for n in ("p_x", "p_q", "p_kv", "p_r"))
        p_g = [s.ps(f"p_g{i}", [P, 2, 2 * P]) for i in range(2)]
        p_ot = s.ps("p_ot", [P, 4, P])
        names = ("w_in w_t w_ready seg_in consts stats pre xn_ready xt_done xt_ready pick_ready ct_ready "
                 "kv_done kv_ready q_done q_ready g_done vs_ready sc_read mid exp_done late o_ready ot_done ot_ready "
                 "wo_done add_step add_done").split()
        g = {n: s.sem(n) for n in names}
        block = s.ctx.enter_context(nc.Block())

        @block.sync
        def _(sp):
            sp.dma_start(wn[:, 0, :], w_q).then_inc(g["w_in"], 16)
            sp.dma_start(wn[:, 1:3, :], w_kv.rearrange("(j p) d -> p j d", p=P)).then_inc(g["w_in"], 16)
            sp.dma_start(wn[:, 3, :], w_o).then_inc(g["w_in"], 16)
            sp.dma_start(seg_i[:].rearrange("p t n -> p (t n)"),
                         seg.rearrange("b s -> (b s)").partition_broadcast(P)).then_inc(g["seg_in"], 16)
            with nc.allow_non_contiguous_dma(reason="one index a token"):
                sp.dma_start(seg_ti[:], seg.rearrange("(t b) s -> (b s) t", b=2)).then_inc(g["seg_in"], 16)

        @block.gpsimd
        def _(pool):
            nc.gpsimd.iota(keys[:], [[1, KW]], base=0, channel_multiplier=1,
                           allow_small_or_imprecise_dtypes=True).then_inc(g["consts"], 1)

            def step(turn):
                if turn.on[1]:
                    t, u = turn.tile(1)
                    wait(pool, g["kv_done"], t - 1)
                    nc.gpsimd.tensor_copy(ct[:, u, :], tile_of(k.ct, t)).then_inc(g["ct_ready"], 1)

            pipeline(pool, 5, step)

        @block.tensor
        def _(pe):
            pe.wait_ge(g["w_in"], 48)
            for j in range(4):
                last = nc.tensor.transpose(p_x[:, j, :], wn[:, j, :], k.ident[:])
            last.then_inc(g["w_t"], 1)
            pe.wait_ge(g["w_ready"], 1)

            def step(turn):
                if turn.on[2]:
                    t, u = turn.tile(2)
                    pe.wait_ge(g["kv_ready"], t + 1)
                    pe.wait_ge(g["pick_ready"], t + 1)
                    wait(pe, g["vs_ready"], t)
                    wait(pe, g["sc_read"], t)
                    for o_ in range(KW):
                        last = nc.tensor.matmul(p_g[o_ // 2][:, o_ % 2, :], pick[:, u, o_, :], kv[:, u, :], start=True, stop=True)
                    last.then_inc(g["g_done"], 1)
                if turn.on[1]:
                    t, u = turn.tile(1)
                    pe.wait_ge(g["xn_ready"], t + 1)
                    wait(pe, g["xt_ready"], t)
                    nc.tensor.transpose(p_x[:, 0, :], xn[:, u, :], k.ident[:]).then_inc(g["xt_done"], 1)
                    pe.wait_ge(g["ct_ready"], t + 1)
                    wait(pe, g["kv_ready"], t)
                    nc.tensor.matmul(p_kv[:, 0:2, :], ct[:, u, :], wt[:, 1:3, :], start=True, stop=True).then_inc(g["kv_done"], 1)
                if turn.on[4]:
                    t, u = turn.tile(4)
                    pe.wait_ge(g["o_ready"], t + 1)
                    wait(pe, g["ot_ready"], t)
                    nc.tensor.transpose(p_ot[:, 0, :], o[:, u, :], k.ident[:]).then_inc(g["ot_done"], 1)
                if turn.on[1]:
                    t, u = turn.tile(1)
                    pe.wait_ge(g["xt_ready"], t + 1)
                    wait(pe, g["q_ready"], t)
                    nc.tensor.matmul(p_q[:, 0, :], xt[:, u, :], wt[:, 0, :], start=True, stop=True).then_inc(g["q_done"], 1)
                if turn.on[4]:
                    t, u = turn.tile(4)
                    pe.wait_ge(g["ot_ready"], t + 1)
                    wait(pe, g["add_done"], t)
                    nc.tensor.matmul(p_r[:, 0, :], ot[:], wt[:, 3, :], start=True, stop=True).then_inc(g["wo_done"], 1)

            pipeline(pe, 5, step)

        @block.scalar
        def _(act):
            finish_statistics(nc, act, None, k, "act", g["stats"])
            act.wait_ge(g["w_t"], 1)
            nc.scalar.activation(wt[:], p_x[:], ACT.Copy).then_inc(g["w_ready"], 1)

            def step(turn):
                if turn.on[3]:
                    t, u = turn.tile(3)
                    act.wait_ge(g["mid"], t * 4 + 4)
                    nc.scalar.activation(pr[:, u], sc[:], ACT.Exp, scale=scale).then_inc(g["exp_done"], 1)
                if turn.on[2]:
                    t, u = turn.tile(2)
                    act.wait_ge(g["g_done"], t + 1)
                    act.wait_ge(g["sc_read"], t + 1)
                    wait(act, g["o_ready"], t - 1)
                    for j in range(2):
                        last = nc.scalar.activation(vs[:, u, 2 * j:2 * j + 2, :], p_g[j][:, :, P:2 * P], ACT.Copy)
                    last.then_inc(g["vs_ready"], 1)
                if turn.on[1]:
                    t, u = turn.tile(1)
                    act.wait_ge(g["xt_done"], t + 1)
                    wait(act, g["q_done"], t - 1)
                    nc.scalar.activation(xt[:, u, :], p_x[:, 0, :], ACT.Copy).then_inc(g["xt_ready"], 1)
                    act.wait_ge(g["kv_done"], t + 1)
                    wait(act, g["g_done"], t - 1)
                    nc.scalar.activation(kv[:, u, :], p_kv[:, 0:2, :].rearrange("p j d -> p (j d)"), ACT.Copy).then_inc(g["kv_ready"], 1)
                if turn.on[4]:
                    t, u = turn.tile(4)
                    act.wait_ge(g["ot_done"], t + 1)
                    wait(act, g["wo_done"], t)
                    nc.scalar.activation(ot[:], p_ot[:, 0, :], ACT.Copy).then_inc(g["ot_ready"], 1)
                if turn.on[1]:
                    t, u = turn.tile(1)
                    act.wait_ge(g["q_done"], t + 1)
                    wait(act, g["sc_read"], t - 1)
                    nc.scalar.activation(q[:, u, :], p_q[:, 0, :], ACT.Copy).then_inc(g["q_ready"], 1)

            pipeline(act, 5, step)

        @block.vector
        def _(dve):
            finish_statistics(nc, None, dve, k, "dve", g["stats"])
            v = nc.vector
            dve.wait_ge(g["seg_in"], 32)
            c = Chain(dve, g["pre"], 0, 0)
            r4, s4 = (z[:].rearrange("p t (b n) -> p t b n", b=2) for z in (row, seg_i))
            for b in range(2):
                v.tensor_scalar(r4[:, :, b, :], s4[:, :, b, :], float(S * b), None, ALU.add)
            c(v.tensor_copy(seg_t[:], seg_ti[:]))
            for o_ in range(KW):
                c(v.tensor_scalar(bias[:, :, o_], seg_t[:], float(o_), NEG, ALU.is_ge, ALU.mult))
            c(v.tensor_scalar(bias[:], bias[:], NEG, None, ALU.subtract))
            dve.wait_ge(g["consts"], 1)

            def step(turn):
                if turn.on[0]:
                    t, u = turn.tile(0)
                    wait(dve, g["xt_done"], t - 1)
                    v.tensor_scalar(xn[:, u, :], tile_of(k.x, t), k.mean[:, bass.ds(t, 1)], k.rstd[:, bass.ds(t, 1)],
                                    ALU.subtract, ALU.mult).then_inc(g["xn_ready"], 1)
                    wait(dve, g["g_done"], t - 1)
                    for o_ in range(KW):
                        last = v.tensor_scalar(pick[:, u, o_, :], tile_of(row, t), keys[:, o_:o_ + 1], None, ALU.is_equal)
                    last.then_inc(g["pick_ready"], 1)
                if turn.on[3]:
                    t, u = turn.tile(3)
                    dve.wait_ge(g["exp_done"], t + 1)
                    c = Chain(dve, g["late"], 4, t)
                    c(v.tensor_reduce(tot[:], pr[:, u].rearrange("p o h -> p h o"), AX, ALU.add))
                    c(v.reciprocal(rec[:], tot[:]))
                    dve.wait_ge(g["vs_ready"], t + 1)
                    c(v.tensor_tensor(pr[:, u], pr[:, u], rec[:].unsqueeze(1).broadcast_to([P, KW, H]), ALU.mult))
                    c(v.tensor_tensor(mix[:].rearrange("p o h d -> p (o h) d"),
                                      vs[:, u].rearrange("p o (h d) -> p (o h) d", h=H),
                                      pr[:, u].rearrange("p o h -> p (o h)").unsqueeze(2).broadcast_to([P, KW * H, HD]), ALU.mult))
                    wait(dve, g["ot_done"], t - 1)
                    v.tensor_reduce(o[:, u, :], mix[:].rearrange("p o h d -> p (h d) o"), AX, ALU.add)\
                        .then_inc(g["o_ready"], 1)
                if turn.on[2]:
                    t, u = turn.tile(2)
                    dve.wait_ge(g["g_done"], t + 1)
                    dve.wait_ge(g["q_ready"], t + 1)
                    for j in range(2):
                        last = v.tensor_tensor(prod[:, 2 * j:2 * j + 2].rearrange("p o h d -> p o (h d)"), p_g[j][:, :, 0:P],
                                               q[:, u, :].unsqueeze(1).broadcast_to([P, 2, P]), ALU.mult)
                    last.then_inc(g["sc_read"], 1)
                    dve.wait_ge(g["sc_read"], t + 1)
                    wait(dve, g["exp_done"], t)
                    c = Chain(dve, g["mid"], 4, t)
                    c(v.tensor_reduce(sc[:], prod[:], AX, ALU.add))
                    c(v.tensor_tensor(sc[:], sc[:], tile_of(bias, t).unsqueeze(2).broadcast_to([P, KW, H]), ALU.add))
                    c(v.tensor_reduce(top[:], sc[:].rearrange("p o h -> p h o"), AX, ALU.max))
                    c(v.tensor_tensor(sc[:], sc[:], top[:].unsqueeze(1).broadcast_to([P, KW, H]), ALU.subtract))
                if turn.on[4]:
                    t, u = turn.tile(4)
                    dve.wait_ge(g["wo_done"], t + 1)
                    c = Chain(dve, g["add_step"], 1, t)
                    add_residual(nc, dve, k, c, t, p_r[:, 0, :]).then_inc(g["add_done"], 1)

            pipeline(dve, 5, step)


E = 8


class Route:
    pass


def route(nc, k, s, r, w_gate, b_gate, choices, capacity, slots, normal_rows, buf):
    xn, xt = s.sb("xn", [P, 2, P]), s.sb("xt", [P, 2, P])
    wg, bg = s.sb("wg", [P, E]), s.sb("bg", [P, E])
    logit, expo = s.sb("logit", [P, NT, E]), s.sb("expo", [P, NT, E])
    best, tot, place, keep, diff = (s.sb(n, [P, choices, NT]) for n in ("best", "tot", "place", "keep", "diff"))
    which = s.sb("which", [P, choices, NT])
    hot, hot_b = s.sb("hot", [P, choices, NT, E]), s.sb("hot_b", [P, choices, NT, E], BF16)
    cand, iota_e, iota_far = s.sb("cand", [P, NT, E]), s.sb("iota_e", [P, NT, E]), s.sb("iota_far", [P, NT, E])
    run = s.sb("run", [P, choices, E, NT])
    total, reset = s.sb("total", [P, choices, E, NT]), s.sb("reset", [P, E, NT])
    loc = s.sb("loc", [P, NT, E])
    spare, slot = s.sb("spare", [P, choices, NT]), s.sb("slot", [P, choices, NT])
    before, ones_b = s.sb("before", [P, P], BF16), s.sb("ones_b", [P, P], BF16)
    zero = s.sb("zero", [P, P])
    r.to, r.frm = s.sb("to", [P, choices, NT], I32), s.sb("frm", [P, choices, NT], I32)
    r.weight = s.sb("weight", [P, choices, NT])
    r.xn = s.sb("xn_all", [P, NT, P])
    if capacity is None:
        n_tiles = normal_rows // P
        tiles_e, end_e, start_e = (s.sb(n, [P, E]) for n in ("tiles_e", "end_e", "start_e"))
        one_e = s.sb("one_e", [P, E])
        tile_no, past = s.sb("tile_no", [1, n_tiles, E - 2]), s.sb("past", [1, n_tiles, E - 2])
        tile_f = s.sb("tile_f", [1, n_tiles])
        r.tile_expert = s.sb("tile_expert", [1, n_tiles], I32)
    with ExitStack() as inner:
        p_x = inner.enter_context(nc.psum_tensor(f"{s.name}_p_x", [P, 4, P], F32))
        p_l = inner.enter_context(nc.psum_tensor(f"{s.name}_p_l", [P, 2, 512], F32))
        p_c = inner.enter_context(nc.psum_tensor(f"{s.name}_p_c", [P, 2, 2, NT * E], F32))
        names = ("r_in stats xn_ready xt_done xt_ready kept l_done l_copied consts hot_ready exp_in exp_done counted "
                 "steps routed scattered zeroed zero_set add_bias").split()
        g = {n: s.sem(n) for n in names}
        block = inner.enter_context(nc.Block())

        @block.sync
        def _(sp):
            sp.dma_start(wg[:], w_gate).then_inc(g["r_in"], 16)
            if b_gate is not None:
                sp.dma_start(bg[:], b_gate.partition_broadcast(P)).then_inc(g["r_in"], 16)
            sp.wait_ge(g["zero_set"], 1)
            rows = normal_rows // P
            sp.dma_start(buf[0:normal_rows, :].rearrange("(n p) d -> p n d", p=P),
                         zero[:].unsqueeze(1).broadcast_to([P, rows, P])).then_inc(g["zeroed"], 16)

        @block.gpsimd
        def _(pool):
            cs = g["consts"]
            nc.gpsimd.memset(zero[:], 0.0).then_inc(g["zero_set"], 1)
            nc.gpsimd.memset(before[:], 1.0).then_inc(cs, 1)
            nc.gpsimd.memset(ones_b[:], 1.0).then_inc(cs, 1)
            nc.gpsimd.memset(reset[:], 1.0).then_inc(cs, 1)
            nc.gpsimd.iota(iota_e[:], [[0, NT], [1, E]], base=0, channel_multiplier=0, allow_small_or_imprecise_dtypes=True).then_inc(cs, 1)
            nc.gpsimd.iota(iota_far[:], [[0, NT], [1, E]], base=E, channel_multiplier=0, allow_small_or_imprecise_dtypes=True).then_inc(cs, 1)
            nc.gpsimd.iota(spare[:], [[NTOK, choices], [P, NT]], base=normal_rows, channel_multiplier=1,
                           allow_small_or_imprecise_dtypes=True).then_inc(cs, 1)
            pool.wait_ge(cs, 6)
            nc.gpsimd.affine_select(out=before[:], in_=before[:], compare_op=ALU.is_gt, fill=0.0, base=0,
                                    pattern=[[1, P]], channel_multiplier=-1).then_inc(cs, 1)
            nc.gpsimd.memset(reset[:, :, 0], 0.0).then_inc(cs, 1)
            if capacity is None:
                nc.gpsimd.memset(one_e[:], 1.0).then_inc(cs, 1)
                nc.gpsimd.iota(tile_no[:], [[1, n_tiles], [0, E - 2]], base=0, channel_multiplier=0,
                               allow_small_or_imprecise_dtypes=True).then_inc(cs, 1)

            def step(turn):
                if turn.on[1]:
                    t, u = turn.tile(1)
                    pool.wait_ge(g["xn_ready"], t + 1)
                    nc.gpsimd.tensor_copy(tile_of(r.xn, t), xn[:, u, :]).then_inc(g["kept"], 1)

            pipeline(pool, 4, step)
            pool.wait_ge(g["kept"], NT)
            pool.wait_ge(g["zeroed"], 16)
            pool.wait_ge(g["routed"], 1)
            for c in range(choices):
                for t in range(NT):
                    nc.gpsimd.indirect_dma_start(out=buf, out_offset=bass.IndirectOffsetOnAxis(ap=r.to[:, c, t:t + 1], axis=0),
                                                 in_=r.xn[:, t, :], in_offset=None).then_inc(g["scattered"], 16)
            pool.wait_ge(g["scattered"], 16 * NT * choices)

        @block.tensor
        def _(pe):
            pe.wait_ge(g["r_in"], 16)

            def step(turn):
                if turn.on[1]:
                    t, u = turn.tile(1)
                    pe.wait_ge(g["xn_ready"], t + 1)
                    wait(pe, g["xt_ready"], t)
                    nc.tensor.transpose(p_x[:, 0, :], xn[:, u, :], k.ident[:]).then_inc(g["xt_done"], 1)
                if turn.on[2]:
                    t, u = turn.tile(2)
                    pe.wait_ge(g["xt_ready"], t + 1)
                    wait(pe, g["l_copied"], t - 1)
                    nc.tensor.matmul(p_l[:, u, 0:E], xt[:, u, :], wg[:], start=True, stop=True).then_inc(g["l_done"], 1)

            pipeline(pe, 4, step)
            pe.wait_ge(g["consts"], 8)
            for c in range(choices):
                pe.wait_ge(g["hot_ready"], c + 1)
                h = hot_b[:, c].rearrange("p t e -> p (t e)")
                nc.tensor.matmul(p_c[:, c, 0, :], before[:], h, start=True, stop=True)
                nc.tensor.matmul(p_c[:, c, 1, :], ones_b[:], h, start=True, stop=True).then_inc(g["counted"], 1)

        @block.scalar
        def _(act):
            finish_statistics(nc, act, None, k, "act", g["stats"])

            def step(turn):
                if turn.on[1]:
                    t, u = turn.tile(1)
                    act.wait_ge(g["xt_done"], t + 1)
                    wait(act, g["l_done"], t - 1)
                    nc.scalar.activation(xt[:, u, :], p_x[:, 0, :], ACT.Copy).then_inc(g["xt_ready"], 1)

            pipeline(act, 4, step)
            act.wait_ge(g["exp_in"], 1)
            if choices == 1:
                nc.scalar.activation(expo[:], expo[:], ACT.Exp).then_inc(g["exp_done"], 1)
            else:
                nc.scalar.activation(diff[:, 1], diff[:, 1], ACT.Exp).then_inc(g["exp_done"], 1)

        @block.vector
        def _(dve):
            v = nc.vector
            finish_statistics(nc, None, dve, k, "dve", g["stats"])
            if b_gate is not None:
                dve.wait_ge(g["r_in"], 32)

            def step(turn):
                if turn.on[0]:
                    t, u = turn.tile(0)
                    wait(dve, g["xt_done"], t - 1)
                    wait(dve, g["kept"], t - 1)
                    v.tensor_scalar(xn[:, u, :], tile_of(k.x, t), k.mean[:, bass.ds(t, 1)], k.rstd[:, bass.ds(t, 1)],
                                    ALU.subtract, ALU.mult).then_inc(g["xn_ready"], 1)
                if turn.on[3]:
                    t, u = turn.tile(3)
                    dve.wait_ge(g["l_done"], t + 1)
                    v.tensor_copy(tile_of(logit, t), p_l[:, u, 0:E]).then_inc(g["l_copied"], 1)

            pipeline(dve, 4, step)
            dve.wait_ge(g["l_copied"], NT)
            dve.wait_ge(g["consts"], 10 if capacity is None else 8)
            c = Chain(dve, g["steps"], 0, 0)
            if b_gate is not None:
                c(v.tensor_tensor(logit[:], logit[:], bg[:].unsqueeze(1).broadcast_to([P, NT, E]), ALU.add))
            for n in range(choices):
                c(v.tensor_reduce(best[:, n], logit[:], AX, ALU.max))
                top = best[:, n].unsqueeze(2).broadcast_to([P, NT, E])
                c(v.tensor_tensor(cand[:], logit[:], top, ALU.is_equal))
                if choices == 1:
                    v.tensor_tensor(expo[:], logit[:], top, ALU.subtract).then_inc(g["exp_in"], 1)
                c(v.scalar_tensor_tensor(cand[:], cand[:], -float(E), iota_far[:], ALU.mult, ALU.add))
                c(v.tensor_reduce(which[:, n], cand[:], AX, ALU.min))
                c(v.tensor_tensor(hot[:, n], iota_e[:], which[:, n].unsqueeze(2).broadcast_to([P, NT, E]), ALU.is_equal))
                v.tensor_copy(hot_b[:, n], hot[:, n]).then_inc(g["hot_ready"], 1)
                if n + 1 < choices:
                    c(v.scalar_tensor_tensor(logit[:], hot[:, n], -NEG, logit[:], ALU.mult, ALU.add))
            if choices == 2:
                v.tensor_tensor(diff[:, 1], best[:, 1], best[:, 0], ALU.subtract).then_inc(g["exp_in"], 1)
            for n in range(choices):
                dve.wait_ge(g["counted"], n + 1)
                c(v.tensor_copy(total[:, n], p_c[:, n, 1, :].rearrange("p (t e) -> p e t", e=E)))
                c(v.tensor_tensor_scan(run[:, n].rearrange("p e t -> p (e t)"), reset[:].rearrange("p e t -> p (e t)"),
                                       total[:, n].rearrange("p e t -> p (e t)"), 0.0, ALU.mult, ALU.add))
                c(v.tensor_tensor(total[:, n], run[:, n], total[:, n], ALU.subtract))
                if n == 1:
                    c(v.tensor_tensor(total[:, n], total[:, n], run[:, 0, :, NT - 1:NT].broadcast_to([P, E, NT]), ALU.add))
                c(v.tensor_tensor(loc[:], p_c[:, n, 0, :].rearrange("p (t e) -> p t e", e=E),
                                  total[:, n].rearrange("p e t -> p t e"), ALU.add))
                if capacity is None:
                    c(v.tensor_scalar(tiles_e[:], run[:, 0, :, NT - 1], 1.0 / P, (P - 1.0) / P - (P - 1.0) / (2 * P), ALU.mult, ALU.add))
                    c(v.tensor_scalar(tiles_e[:], tiles_e[:], ROUND, ROUND, ALU.add, ALU.subtract))
                    c(v.tensor_tensor_scan(end_e[:], one_e[:], tiles_e[:], 0.0, ALU.mult, ALU.add))
                    c(v.tensor_tensor(start_e[:], end_e[:], tiles_e[:], ALU.subtract))
                    c(v.tensor_scalar(start_e[:], start_e[:], float(P), None, ALU.mult))
                    c(v.tensor_tensor(loc[:], loc[:], start_e[:].unsqueeze(1).broadcast_to([P, NT, E]), ALU.add))
                    c(v.tensor_tensor(past[:], tile_no[:], end_e[0:1, 0:E - 2].unsqueeze(1).broadcast_to([1, n_tiles, E - 2]), ALU.is_ge))
                    c(v.tensor_reduce(tile_f[:], past[:], AX, ALU.add))
                    c(v.tensor_copy(r.tile_expert[:], tile_f[:]))
                c(v.tensor_tensor(loc[:], loc[:], hot[:, n], ALU.mult))
                c(v.tensor_reduce(place[:, n], loc[:], AX, ALU.add))
                if capacity is None:
                    c(v.tensor_scalar(keep[:, n], which[:, n], float(E - 1), None, ALU.is_lt))
                    c(v.tensor_copy(slot[:, n], place[:, n]))
                else:
                    c(v.tensor_scalar(keep[:, n], place[:, n], float(capacity), None, ALU.is_lt))
                    c(v.scalar_tensor_tensor(slot[:, n], which[:, n], float(slots), place[:, n], ALU.mult, ALU.add))
            c(v.tensor_tensor(place[:], slot[:], spare[:], ALU.subtract))
            c(v.tensor_tensor(place[:], place[:], keep[:], ALU.mult))
            c(v.tensor_tensor(place[:], place[:], spare[:], ALU.add))
            c(v.tensor_copy(r.to[:], place[:]))
            c(v.tensor_tensor(slot[:], slot[:], keep[:], ALU.mult))
            c(v.tensor_copy(r.frm[:], slot[:]))
            v.tensor_copy(tot[:, 0], slot[:, 0]).then_inc(g["routed"], 1)
            dve.wait_ge(g["routed"], 1)
            dve.wait_ge(g["exp_done"], 1)
            if choices == 1:
                c(v.tensor_reduce(tot[:, 0], expo[:], AX, ALU.add))
                c(v.reciprocal(r.weight[:, 0], tot[:, 0]))
                if capacity is None:
                    c(v.tensor_scalar(keep[:], keep[:], 2.0, None, ALU.mult))
            else:
                c(v.tensor_scalar(diff[:, 0], diff[:, 1], 1.0, None, ALU.add))
                c(v.reciprocal(r.weight[:, 0], diff[:, 0]))
                c(v.tensor_tensor(r.weight[:, 1], r.weight[:, 0], diff[:, 1], ALU.mult))
            c(v.tensor_tensor(r.weight[:], r.weight[:], keep[:], ALU.mult))


def experts_gelu(nc, k, s, per_expert, w1, b1, w2, b2, xbuf, ybuf):
    CH, F = 256, w1.shape[2]
    NF = F // P
    chunks = E * per_expert
    ws1, ws2 = s.sb("ws1", [P, 2, F]), s.sb("ws2", [P, 2, NF, P])
    b1n, b1t = s.sb("b1n", [E * NF, P]), s.sb("b1t", [P, E * NF])
    b1c, b2s = s.sb("b1c", [P, 2, NF]), s.sb("b2s", [P, E, P])
    xs, xt = s.sb("xs", [P, 2, 2, P]), s.sb("xts", [P, 2, CH])
    h, y = s.sb("h", [P, 2, NF, CH]), s.sb("y", [P, 2, 2, P])
    with ExitStack() as inner:
        p_t = inner.enter_context(nc.psum_tensor(f"{s.name}_p_t", [P, 4, P], F32))
        p_h = inner.enter_context(nc.psum_tensor(f"{s.name}_p_h", [P, 2, NF, CH], F32))
        p_y = inner.enter_context(nc.psum_tensor(f"{s.name}_p_y", [P, 2, 4, P], F32))
        names = ("b1_ready b_in w_in0 w_in1 x_in0 x_in1 b_t b_ready t_done e_xt_ready h_done h_ready y_done y_ready stored0 stored1").split()
        g = {n: s.sem("e_" + n) for n in names}
        block = inner.enter_context(nc.Block())
        xrows = xbuf[0:chunks * CH, :].rearrange("(c j p) d -> p c j d", p=P, j=2)
        yrows = ybuf.rearrange("(c j p) d -> p c j d", p=P, j=2)
        unroll = 2 * per_expert

        def chunk(ap, c):
            return ap[:, c] if isinstance(c, int) else ap[:, bass.ds(c, 1)].rearrange("p a j d -> p (a j) d")

        def expert_of(turn, p):
            c, m = turn.tile(p)
            if isinstance(c, int):
                return c // per_expert, (c // per_expert) % 2
            w = m // per_expert
            return turn.group(p) * 2 + w, w

        def loop(eng, step):
            pipeline_by(eng, 3, step, chunks, unroll, 3)

        @block.sync
        def _(sp):
            sp.dma_start(b1n[:], b1.rearrange("e (f p) -> (e f) p", p=P)).then_inc(g["b_in"], 16)
            sp.dma_start(b2s[:].rearrange("p e d -> p (e d)"), b2.rearrange("e d -> (e d)").partition_broadcast(P)).then_inc(g["b_in"], 16)

            def load_expert(e, w):
                wait(sp, g["y_done"], (e - 1) * per_expert)
                if isinstance(e, int):
                    src1, src2 = w1[e], w2[e].rearrange("(f p) d -> p f d", p=P)
                else:
                    src1 = w1[bass.ds(e, 1)].rearrange("a p f -> p (a f)")
                    src2 = w2[bass.ds(e, 1)].rearrange("a (f p) d -> p (a f) d", p=P)
                sp.dma_start(ws1[:, w, :], src1).then_inc(g[f"w_in{w}"], 16)
                sp.dma_start(ws2[:, w], src2).then_inc(g[f"w_in{w}"], 16)

            def load_chunk(c, u):
                wait(sp, g["t_done"], c - 1)
                sp.dma_start(xs[:, u], chunk(xrows, c)).then_inc(g[f"x_in{u}"], 16)

            def group(base, e0):
                for w in range(2):
                    load_expert(e0 + w, w)
                    for j in range(per_expert):
                        load_chunk(base + (w * per_expert + j), (w * per_expert + j) % 2)

            group(0, 0)
            with sp.Fori(1, E // 2) as i:
                group(i * unroll, i * 2)

        @block.gpsimd
        def _(pool):
            def step(turn):
                if turn.on[2]:
                    c, m = turn.tile(2)
                    pool.wait_ge(g["y_ready"], c + 1)
                    pool.dma_start(chunk(yrows, c), y[:, m % 2]).then_inc(g[f"stored{m % 2}"], 16)

            loop(pool, step)
            for u in range(2):
                pool.wait_ge(g[f"stored{u}"], 16 * (chunks // 2))

        @block.tensor
        def _(pe):
            pe.wait_ge(g["b_in"], 32)
            nc.tensor.transpose(p_t[:, 0, 0:E * NF], b1n[:], k.ident[0:E * NF, 0:E * NF]).then_inc(g["b_t"], 1)
            pe.wait_ge(g["b_ready"], 1)

            def step(turn):
                if turn.on[0]:
                    c, m = turn.tile(0)
                    pe.wait_ge(g[f"x_in{m % 2}"], turn.half(0) * 16 + 16)
                    wait(pe, g["e_xt_ready"], c)
                    for j in range(2):
                        last = nc.tensor.transpose(p_t[:, j, :], xs[:, m % 2, j, :], k.ident[:])
                    last.then_inc(g["t_done"], 1)
                if turn.on[1]:
                    c, m = turn.tile(1)
                    e, w = expert_of(turn, 1)
                    pe.wait_ge(g["e_xt_ready"], c + 1)
                    if m % per_expert == 0:
                        pe.wait_ge(g[f"w_in{w}"], (turn.group(1) + 1) * 32)
                    wait(pe, g["h_ready"], c - 1)
                    for f in range(NF):
                        last = nc.tensor.matmul(p_h[:, m % 2, f, :], ws1[:, w, f * P:(f + 1) * P], xt[:, m % 2, :], start=True, stop=True)
                    last.then_inc(g["h_done"], 1)
                if turn.on[2]:
                    c, m = turn.tile(2)
                    e, w = expert_of(turn, 2)
                    pe.wait_ge(g["h_ready"], c + 1)
                    wait(pe, g["y_ready"], c - 1)
                    for j in range(2):
                        for f in range(NF):
                            last = nc.tensor.matmul(p_y[:, m % 2, j, :], h[:, m % 2, f, j * P:(j + 1) * P], ws2[:, w, f, :],
                                                    start=(f == 0), stop=(f == NF - 1))
                    last.then_inc(g["y_done"], 1)

            loop(pe, step)

        @block.scalar
        def _(act):
            act.wait_ge(g["b_t"], 1)
            nc.scalar.activation(b1t[:], p_t[:, 0, 0:E * NF], ACT.Copy).then_inc(g["b_ready"], 1)
            act.wait_ge(g["b_ready"], 1)

            def step(turn):
                if turn.on[1]:
                    c, m = turn.tile(1)
                    e, w = expert_of(turn, 1)
                    act.wait_ge(g["h_done"], c + 1)
                    wait(act, g["y_done"], c - 1)
                    if m % per_expert == 0:
                        act.wait_ge(g["b1_ready"], e + 1)
                    for f in range(NF):
                        last = nc.scalar.activation(h[:, m % 2, f, :], p_h[:, m % 2, f, :], ACT.Gelu_apprx_tanh,
                                                    bias=b1c[:, w, f:f + 1])
                    last.then_inc(g["h_ready"], 1)

            loop(act, step)

        @block.vector
        def _(dve):
            dve.wait_ge(g["b_in"], 32)
            dve.wait_ge(g["b_ready"], 1)

            def step(turn):
                if turn.on[0]:
                    c, m = turn.tile(0)
                    dve.wait_ge(g["t_done"], c + 1)
                    wait(dve, g["h_done"], c - 1)
                    nc.vector.tensor_copy(xt[:, m % 2, :], p_t[:, 0:2, :].rearrange("p j n -> p (j n)")).then_inc(g["e_xt_ready"], 1)
                    if m % per_expert == 0:
                        e, w = expert_of(turn, 0)
                        wait(dve, g["h_ready"], (e - 1) * per_expert)
                        nc.vector.tensor_copy(b1c[:, w, :], b1t[:, bass.ds(e * NF, NF)]).then_inc(g["b1_ready"], 1)
                if turn.on[2]:
                    c, m = turn.tile(2)
                    e, w = expert_of(turn, 2)
                    dve.wait_ge(g["y_done"], c + 1)
                    wait(dve, g[f"stored{m % 2}"], turn.half(2) * 16)
                    bias = tile_of(b2s, e).unsqueeze(1).broadcast_to([P, 2, P])
                    nc.vector.tensor_tensor(y[:, m % 2], p_y[:, m % 2, 0:2, :], bias, ALU.add).then_inc(g["y_ready"], 1)

            loop(dve, step)


def combine(nc, k, s, r, choices, ybuf):
    yg = s.sb("yg", [P, choices, NT, P])
    with ExitStack() as inner:
        names = "gathered0 gathered1 added stat".split()
        g = {n: s.sem("c_" + n) for n in names}
        block = inner.enter_context(nc.Block())

        @block.gpsimd
        def _(pool):
            for t in range(NT):
                for c in range(choices):
                    nc.gpsimd.indirect_dma_start(out=yg[:, c, t, :], out_offset=None, in_=ybuf,
                                                 in_offset=bass.IndirectOffsetOnAxis(ap=r.frm[:, c, t:t + 1], axis=0))\
                        .then_inc(g[f"gathered{t % 2}"], 16)

        @block.vector
        def _(dve):
            for u in range(2):
                dve.wait_ge(g[f"gathered{u}"], 16 * choices * (NT // 2))

            def step(turn):
                t, u = turn.tile(0)
                c = Chain(dve, g["added"], choices, t)
                for n in range(choices):
                    src = yg[:, n]
                    c(nc.vector.scalar_tensor_tensor(tile_of(k.x, t), tile_of(src, t), r.weight[:, n, bass.ds(t, 1)], tile_of(k.x, t),
                                                     ALU.mult, ALU.add))
                nc.vector.bn_stats(tile_of(k.stats, t), tile_of(k.x, t)).then_inc(g["stat"], 1)

            pipeline(dve, 1, step)


def mixture_gelu(nc, k, name, w_gate, b_gate, w1, b1, w2, b2, choices, capacity):
    CH = 256
    per_expert = -(-capacity // CH)
    slots = per_expert * CH
    rows = E * slots
    s, r = Stage(nc, name), Route()
    xbuf = nc.dram_tensor(f"{name}_xbuf", [rows + choices * NTOK, D], F32, kind="Internal").ap()
    ybuf = nc.dram_tensor(f"{name}_ybuf", [rows, D], F32, kind="Internal").ap()
    with s.ctx:
        route(nc, k, s, r, w_gate, b_gate, choices, capacity, slots, rows, xbuf)
        experts_gelu(nc, k, s, per_expert, w1, b1, w2, b2, xbuf, ybuf)
        combine(nc, k, s, r, choices, ybuf)


def experts_swiglu(nc, k, s, r, n_tiles, w_up, w_gate, w_down, w_up_s, w_gate_s, w_down_s, xbuf, ybuf):
    F = w_up.shape[2]
    NF, NE = F // P, w_up.shape[0]
    total = n_tiles + NT
    wu, wg, wd = s.sb("wu", [P, NE + 1, F]), s.sb("wgt", [P, NE + 1, F]), s.sb("wd", [P, (NE + 1), NF * P])
    xs, xt = s.sb("xs", [P, 2, P]), s.sb("xts", [P, 2, P])
    sig, a, at = s.sb("sig", [P, 2, F]), s.sb("a", [P, 2, F]), s.sb("at", [P, 2, F])
    y = s.sb("y", [P, 2, P])
    with ExitStack() as inner:
        p_x, p_y, p_a = (inner.enter_context(nc.psum_tensor(f"{s.name}_p_{n}", [P, F], F32)) for n in ("xe", "ye", "ae"))
        p_u, p_g = (inner.enter_context(nc.psum_tensor(f"{s.name}_p_{n}", [P, 2, F], F32)) for n in ("ue", "ge"))
        names = ("w_in ws_in x_in0 x_in1 x_kept t_done xt_ready u_done sig_done u_read at_done at_ready y_done y_ready "
                 "stored0 stored1 add_step").split()
        g = {n: s.sem("e_" + n) for n in names}
        block = inner.enter_context(nc.Block())
        xrows = xbuf.rearrange("(t p) d -> p t d", p=P)
        yrows = ybuf.rearrange("(t p) d -> p t d", p=P)

        def both(eng, depth, routed, shared, lead):
            pipeline(eng, depth, routed, n_tiles, lead)
            pipeline(eng, depth, shared, NT, lead)

        @block.sync
        def _(sp):
            sp.dma_start(wu[:, 0:NE, :], w_up.rearrange("e p f -> p e f")).then_inc(g["w_in"], 16)
            sp.dma_start(wg[:, 0:NE, :], w_gate.rearrange("e p f -> p e f")).then_inc(g["w_in"], 16)
            sp.dma_start(wd[:, 0:NE, :].rearrange("p e (f d) -> p e f d", d=P),
                         w_down.rearrange("e (f p) d -> p e f d", p=P)).then_inc(g["w_in"], 16)
            sp.dma_start(wu[:, NE, :], w_up_s).then_inc(g["ws_in"], 16)
            sp.dma_start(wg[:, NE, :], w_gate_s).then_inc(g["ws_in"], 16)
            sp.dma_start(wd[:, NE, :].rearrange("p (f d) -> p f d", d=P),
                         w_down_s.rearrange("(f p) d -> p f d", p=P)).then_inc(g["ws_in"], 16)

            def step(turn):
                t, u = turn.tile(0)
                wait(sp, g["t_done"], t - 1)
                sp.dma_start(xs[:, u, :], tile_of(xrows, t)).then_inc(g[f"x_in{u}"], 16)

            pipeline(sp, 1, step, n_tiles, 2)

        @block.gpsimd
        def _(pool):
            def step(turn):
                if turn.on[3]:
                    t, u = turn.tile(3)
                    pool.wait_ge(g["y_ready"], t + 1)
                    pool.dma_start(tile_of(yrows, t), y[:, u, :]).then_inc(g[f"stored{u}"], 16)

            pipeline(pool, 4, step, n_tiles, 4)

            def shared(turn):
                if turn.on[0]:
                    t, u = turn.tile(0)
                    pool.wait_ge(g["t_done"], t + (n_tiles - 1))
                    nc.gpsimd.tensor_copy(xs[:, u, :], tile_of(r.xn, t)).then_inc(g["x_kept"], 1)

            pipeline(pool, 4, shared, NT, 4)
            for u in range(2):
                pool.wait_ge(g[f"stored{u}"], 16 * (n_tiles // 2))

        @block.tensor
        def _(pe):
            def step(turn, base, routed):
                if turn.on[0]:
                    t, u = turn.tile(0)
                    if routed:
                        pe.wait_ge(g[f"x_in{u}"], turn.half(0) * 16 + 16)
                    else:
                        pe.wait_ge(g["x_kept"], t + 1)
                    wait(pe, g["xt_ready"], t + base)
                    nc.tensor.transpose(p_x[:, 0:P], xs[:, u, :], k.ident[:]).then_inc(g["t_done"], 1)
                if turn.on[1]:
                    t, u = turn.tile(1)
                    if routed:
                        e = pe.value_load(r.tile_expert[0:1, bass.ds(t, 1)], min_val=0, max_val=NE - 1)
                    else:
                        e = NE
                    pe.wait_ge(g["xt_ready"], t + (base + 1))
                    wait(pe, g["u_read"], t + (base - 1))
                    nc.tensor.matmul(p_g[:, u, :], xt[:, u, :], tile_of(wg, e), start=True, stop=True)
                    nc.tensor.matmul(p_u[:, u, :], xt[:, u, :], tile_of(wu, e), start=True, stop=True).then_inc(g["u_done"], 1)
                if turn.on[2]:
                    t, u = turn.tile(2)
                    pe.wait_ge(g["u_read"], t + (base + 1))
                    wait(pe, g["at_ready"], t + base)
                    for f in range(NF):
                        last = nc.tensor.transpose(p_a[:, f * P:(f + 1) * P], a[:, u, f * P:(f + 1) * P], k.ident[:])
                    last.then_inc(g["at_done"], 1)
                if turn.on[3]:
                    t, u = turn.tile(3)
                    if routed:
                        e = pe.value_load(r.tile_expert[0:1, bass.ds(t, 1)], min_val=0, max_val=NE - 1)
                    else:
                        e = NE
                    pe.wait_ge(g["at_ready"], t + (base + 1))
                    wait(pe, g["y_ready"], t + base)
                    for f in range(NF):
                        w = wd[:, e, f * P:(f + 1) * P] if isinstance(e, int) else \
                            wd[:, bass.ds(e, 1), f * P:(f + 1) * P].rearrange("p a n -> p (a n)")
                        last = nc.tensor.matmul(p_y[:, 0:P], at[:, u, f * P:(f + 1) * P], w, start=(f == 0), stop=(f == NF - 1))
                    last.then_inc(g["y_done"], 1)

            pe.wait_ge(g["w_in"], 48)
            pe.wait_ge(g["ws_in"], 48)
            both(pe, 4, lambda turn: step(turn, 0, True), lambda turn: step(turn, n_tiles, False), 4)

        @block.scalar
        def _(act):
            def step(turn, base):
                if turn.on[2]:
                    t, u = turn.tile(2)
                    act.wait_ge(g["at_done"], t + (base + 1))
                    wait(act, g["y_done"], t + (base - 1))
                    nc.scalar.activation(at[:, u, :], p_a[:], ACT.Copy).then_inc(g["at_ready"], 1)
                if turn.on[1]:
                    t, u = turn.tile(1)
                    act.wait_ge(g["u_done"], t + (base + 1))
                    wait(act, g["u_read"], t + (base - 1))
                    nc.scalar.activation(sig[:, u, :], p_g[:, u, :], ACT.Silu).then_inc(g["sig_done"], 1)

            both(act, 4, lambda turn: step(turn, 0), lambda turn: step(turn, n_tiles), 4)

        @block.vector
        def _(dve):
            v = nc.vector

            def step(turn, base, routed):
                if turn.on[0]:
                    t, u = turn.tile(0)
                    dve.wait_ge(g["t_done"], t + (base + 1))
                    wait(dve, g["u_done"], t + (base - 1))
                    v.tensor_copy(xt[:, u, :], p_x[:, 0:P]).then_inc(g["xt_ready"], 1)
                if turn.on[3]:
                    t, u = turn.tile(3)
                    dve.wait_ge(g["y_done"], t + (base + 1))
                    if routed:
                        wait(dve, g[f"stored{u}"], turn.half(3) * 16)
                        v.tensor_copy(y[:, u, :], p_y[:, 0:P]).then_inc(g["y_ready"], 1)
                    else:
                        v.tensor_tensor(tile_of(k.x, t), tile_of(k.x, t), p_y[:, 0:P], ALU.add).then_inc(g["y_ready"], 1)
                if turn.on[1]:
                    t, u = turn.tile(1)
                    dve.wait_ge(g["sig_done"], t + (base + 1))
                    wait(dve, g["at_done"], t + (base - 1))
                    v.tensor_tensor(a[:, u, :], sig[:, u, :], p_u[:, u, :], ALU.mult).then_inc(g["u_read"], 1)

            both(dve, 4, lambda turn: step(turn, 0, True), lambda turn: step(turn, n_tiles, False), 4)


def mixture_swiglu(nc, k, name, w_gate, w_up, w_gt, w_down, w_up_s, w_gt_s, w_down_s):
    n_tiles = NT + E - 2
    rows = n_tiles * P
    s, r = Stage(nc, name), Route()
    xbuf = nc.dram_tensor(f"{name}_xbuf", [rows + NTOK, D], F32, kind="Internal").ap()
    ybuf = nc.dram_tensor(f"{name}_ybuf", [rows, D], F32, kind="Internal").ap()
    with s.ctx:
        route(nc, k, s, r, w_gate, None, 1, None, 0, rows, xbuf)
        experts_swiglu(nc, k, s, r, n_tiles, w_up, w_gt, w_down, w_up_s, w_gt_s, w_down_s, xbuf, ybuf)
        combine(nc, k, s, r, 1, ybuf)


def attention_latent(nc, k, gamma_x, beta_x, gamma_l, beta_l, w_q, w_kv, w_o, cos, sin):
    H, HD = 8, 64
    NP = H // 2
    scale = float(HD) ** -0.5
    s = Stage(nc, "a2")
    with s.ctx:
        wq, wkv, wo = s.sb("wq", [P, H * HD]), s.sb("wkv", [P, 2 * H * HD]), s.sb("wo", [P, NP, P])
        wr = s.sb("wr", [P, H, 2, HD // 2])
        gx, bx, gl, bl = (s.sb(n, [P, 1]) for n in ("gx", "bx", "gl", "bl"))
        cs, sn = s.sb("cs", [P, S]), s.sb("sn", [P, S])
        c_stats, c_mean, c_rstd, l_rstd = s.sb("c_stats", [P, NT, 6]), *(s.sb(n, [P, NT]) for n in ("c_mean", "c_rstd", "l_rstd"))
        var2, root2, inv2, tmp2, tmp3 = (s.sb(n, [P, 2, NT]) for n in ("var2", "root2", "inv2", "tmp2", "tmp3"))
        xn = s.sb("xn", [P, 2, 2, P])
        xl = s.sb("xl", [P, 2, 2, 2, S])
        q, kt = s.sb("q", [P, 2, NP, P]), s.sb("kt", [P, 2, NP, 2, 2, S])
        kc, ks = s.sb("kc", [P, 2, NP * 2, S]), s.sb("ks", [P, 2, NP * 2, S])
        v_s = s.sb("v", [P, 2, 2, H * HD])
        pr = s.sb("pr", [P, 2, H, P])
        top, tot, rec = s.sb("top", [P, 2, H]), s.sb("tot", [P, 2, H]), s.sb("rec", [P, 2, H])
        prt = s.sb("prt", [P, H, P])
        o, ot = s.sb("o", [P, 2, H, HD]), s.sb("ot", [P, NP, P])
        ring = s.ps("ring", [P, 8, 512])
        names = ("w_in wr_ready stats c_stat c_steps xn_ready xt_done xl_ready q_done k_done q_ready kl_ready kx_ready rope_in "
                 "v_done v_ready s_done top_done sub_done exp_done rec_steps t_done prt_ready pv_done o_ready "
                 "ot_done ot_ready wo_done add_step add_done").split()
        g = {n: s.sem(n) for n in names}
        block = s.ctx.enter_context(nc.Block())

        def four(n):
            return ring[:, n, :].rearrange("p (j n) -> p j n", n=P)

        @block.sync
        def _(sp):
            for dst, src in ((wq[:], w_q), (wkv[:], w_kv), (wo[:], w_o.rearrange("(j p) d -> p j d", p=P)), (cs[:], cos), (sn[:], sin)):
                sp.dma_start(dst, src).then_inc(g["w_in"], 16)
            for dst, src in ((gx, gamma_x), (bx, beta_x), (gl, gamma_l), (bl, beta_l)):
                sp.dma_start(dst[:], src.rearrange("(p a) -> p a", a=1)).then_inc(g["w_in"], 16)

        @block.gpsimd
        def _(pool):
            pool.wait_ge(g["w_in"], 144)
            wk = wkv[:, 0:H * HD].rearrange("p (h a d) -> p h a d", h=H, a=2)
            for a in range(2):
                nc.gpsimd.tensor_copy(wr[:, :, a, :], wk[:, :, 1 - a, :]).then_inc(g["wr_ready"], 1)

            def step(turn):
                if turn.on[2]:
                    t, u = turn.tile(2)
                    pool.wait_ge(g["rope_in"], t + 1)
                    wait(pool, g["s_done"], t - 1)
                    nc.gpsimd.tensor_tensor(kt[:, u, :, :, 0, :].rearrange("p j b n -> p (j b) n"), kc[:, u], ks[:, u], ALU.add)\
                        .then_inc(g["kx_ready"], 1)

            pipeline(pool, 6, step)

        @block.tensor
        def _(pe):
            pe.wait_ge(g["w_in"], 144)
            pe.wait_ge(g["wr_ready"], 2)

            def step(turn):
                if turn.on[3]:
                    t, u = turn.tile(3)
                    pe.wait_ge(g["q_ready"], t + 1)
                    pe.wait_ge(g["kl_ready"], t + 1)
                    pe.wait_ge(g["kx_ready"], t + 1)
                    wait(pe, g["v_ready"], t)
                    for b in range(2):
                        last = nc.tensor.matmul(ring[:, 2 + b, :], xl[:, u, b, :, :], wkv[:, H * HD:], start=True, stop=True)
                    last.then_inc(g["v_done"], 1)
                    for j in range(NP):
                        for h in range(2):
                            rows = slice(64 * h, 64 * h + 64)
                            for b in range(2):
                                cols = slice(64 * b, 64 * b + 64)
                                last = nc.tensor.matmul(ring[cols, h, j * P:(j + 1) * P], q[rows, u, j, cols],
                                                        kt[rows, u, j, b, :, :], start=True, stop=True)
                    last.then_inc(g["s_done"], 1)
                if turn.on[1]:
                    t, u = turn.tile(1)
                    pe.wait_ge(g["xn_ready"], t + 1)
                    wait(pe, g["xl_ready"], t)
                    wait(pe, g["add_done"], t - 4)
                    for a in range(2):
                        last = nc.tensor.transpose(four(4)[:, a, :], xn[:, u, a, :], k.ident[:])
                    last.then_inc(g["xt_done"], 1)
                if turn.on[4]:
                    t, u = turn.tile(4)
                    pe.wait_ge(g["exp_done"], t + 1)
                    wait(pe, g["o_ready"], t)
                    wait(pe, g["prt_ready"], t)
                    for h in range(H):
                        last = nc.tensor.transpose(four(5 + h // 4)[:, h % 4, :], pr[:, u, h, :], k.ident[:])
                    last.then_inc(g["t_done"], 1)
                if turn.on[5]:
                    t, u = turn.tile(5)
                    pe.wait_ge(g["o_ready"], t + 1)
                    wait(pe, g["ot_ready"], t)
                    for j in range(NP):
                        last = nc.tensor.transpose(four(7)[:, j, :], o[:, u, 2 * j:2 * j + 2, :].rearrange("p h d -> p (h d)"), k.ident[:])
                    last.then_inc(g["ot_done"], 1)
                if turn.on[2]:
                    t, u = turn.tile(2)
                    pe.wait_ge(g["xl_ready"], t + 1)
                    wait(pe, g["sub_done"], t)
                    for j in range(NP):
                        last = nc.tensor.matmul(four(0)[:, j, :], wq[:, j * P:(j + 1) * P], xl[:, u, :, 1, :], start=True, stop=True)
                    last.then_inc(g["q_done"], 1)
                    wait(pe, g["v_ready"], t)
                    for j in range(NP):
                        nc.tensor.matmul(four(3)[:, j, :], wr[:].rearrange("p h a d -> p (h a d)")[:, j * P:(j + 1) * P],
                                         xl[:, u, :, 0, :], start=True, stop=True)
                        last = nc.tensor.matmul(ring[:, 1 + j // 2, (j % 2) * 256:(j % 2 + 1) * 256], wkv[:, j * P:(j + 1) * P],
                                                xl[:, u], start=True, stop=True)
                    last.then_inc(g["k_done"], 1)
                if turn.on[5]:
                    t, u = turn.tile(5)
                    pe.wait_ge(g["ot_ready"], t + 1)
                    pe.wait_ge(g["xl_ready"], up_to(t + 5))
                    wait(pe, g["add_done"], t)
                    for j in range(NP):
                        last = nc.tensor.matmul(ring[:, 4, 0:P], ot[:, j, :], wo[:, j, :], start=(j == 0), stop=(j == NP - 1))
                    last.then_inc(g["wo_done"], 1)
                if turn.on[4]:
                    t, u = turn.tile(4)
                    pe.wait_ge(g["prt_ready"], t + 1)
                    pe.wait_ge(g["v_ready"], t + 1)
                    for b in range(2):
                        rows = slice(64 * b, 64 * b + 64)
                        for h in range(H):
                            last = nc.tensor.matmul(ring[rows, 5, h * HD:(h + 1) * HD], prt[:, (h % 2) * NP + h // 2, rows],
                                                    v_s[:, u, b, h * HD:(h + 1) * HD], start=True, stop=True)
                    last.then_inc(g["pv_done"], 1)

            pipeline(pe, 6, step)

        @block.scalar
        def _(act):
            finish_statistics(nc, act, None, k, "act", g["stats"])
            act.wait_ge(g["c_steps"], 11)
            nc.scalar.activation(root2[:], var2[:], ACT.Sqrt).then_inc(g["c_steps"], 1)

            def step(turn):
                if turn.on[4]:
                    t, u = turn.tile(4)
                    act.wait_ge(g["t_done"], t + 1)
                    wait(act, g["pv_done"], t)
                    nc.scalar.activation(prt[:], ring[:, 5:7, :].rearrange("p a (j n) -> p (a j) n", n=P), ACT.Copy).then_inc(g["prt_ready"], 1)
                if turn.on[3]:
                    t, u = turn.tile(3)
                    act.wait_ge(g["v_done"], t + 1)
                    wait(act, g["pv_done"], t - 1)
                    nc.scalar.activation(v_s[:, u], ring[:, 2:4, :], ACT.Copy).then_inc(g["v_ready"], 1)
                    act.wait_ge(g["sub_done"], t + 1)
                    nc.scalar.activation(pr[:, u], pr[:, u], ACT.Exp, scale=scale).then_inc(g["exp_done"], 1)
                if turn.on[5]:
                    t, u = turn.tile(5)
                    act.wait_ge(g["ot_done"], t + 1)
                    wait(act, g["wo_done"], t)
                    nc.scalar.activation(ot[:], four(7), ACT.Copy).then_inc(g["ot_ready"], 1)
                if turn.on[2]:
                    t, u = turn.tile(2)
                    act.wait_ge(g["q_done"], t + 1)
                    wait(act, g["s_done"], t - 1)
                    nc.scalar.activation(q[:, u], four(0), ACT.Copy).then_inc(g["q_ready"], 1)
                    act.wait_ge(g["rope_in"], t + 1)
                    keys = ring[:, 1:3, :].rearrange("p a (j b c n) -> p (a j b) c n", j=2, b=2, c=2)
                    nc.scalar.activation(kt[:, u, :, :, 1, :].rearrange("p j b n -> p (j b) n"), keys[:, :, 1, :], ACT.Copy)\
                        .then_inc(g["kl_ready"], 1)

            pipeline(act, 6, step)

        @block.vector
        def _(dve):
            v = nc.vector
            finish_statistics(nc, None, dve, k, "dve", g["stats"])

            def context_statistics(turn):
                t, u = turn.tile(0)
                v.bn_stats(tile_of(c_stats, t), tile_of(k.c, t)).then_inc(g["c_stat"], 1)

            pipeline(dve, 1, context_statistics)
            dve.wait_ge(g["c_stat"], NT)
            c = Chain(dve, g["c_steps"], 0, 0)
            st = c_stats
            c(v.tensor_tensor(c_mean[:], st[:, :, 1], st[:, :, 4], ALU.add))
            c(v.tensor_scalar(c_mean[:], c_mean[:], 0.5, None, ALU.mult))
            c(v.tensor_tensor(tmp2[:, 0], st[:, :, 1], st[:, :, 4], ALU.subtract))
            c(v.tensor_tensor(tmp2[:, 0], tmp2[:, 0], tmp2[:, 0], ALU.mult))
            c(v.tensor_tensor(tmp2[:, 1], st[:, :, 2], st[:, :, 5], ALU.add))
            c(v.tensor_scalar(tmp2[:, 1], tmp2[:, 1], 1.0 / D, None, ALU.mult))
            c(v.scalar_tensor_tensor(var2[:, 0], tmp2[:, 0], 0.25, tmp2[:, 1], ALU.mult, ALU.add))
            c(v.tensor_tensor(tmp3[:, 0], k.rstd[:], k.rstd[:], ALU.mult))
            c(v.tensor_tensor(var2[:, 1], tmp3[:, 0], k.var[:], ALU.mult))
            c(v.tensor_scalar(var2[:], var2[:], EPS, None, ALU.add))
            c(v.tensor_copy(tmp3[:, 1], tmp3[:, 0]))
            c.n += 1
            dve.wait_ge(c.sem, c.n)
            c(v.reciprocal(inv2[:], root2[:]))
            c(v.tensor_tensor(tmp2[:], inv2[:], inv2[:], ALU.mult))
            c(v.tensor_tensor(tmp2[:], tmp2[:], var2[:], ALU.mult))
            c(v.tensor_scalar(tmp2[:], tmp2[:], -0.5, 1.5, ALU.mult, ALU.add))
            c(v.tensor_tensor(inv2[:], inv2[:], tmp2[:], ALU.mult))
            c(v.tensor_copy(c_rstd[:], inv2[:, 0]))
            c(v.tensor_tensor(l_rstd[:], inv2[:, 1], k.rstd[:], ALU.mult))
            dve.wait_ge(g["w_in"], 144)

            def step(turn):
                if turn.on[0]:
                    t, u = turn.tile(0)
                    wait(dve, g["xt_done"], t - 1)
                    v.tensor_scalar(xn[:, u, 0, :], tile_of(k.c, t), c_mean[:, bass.ds(t, 1)], c_rstd[:, bass.ds(t, 1)],
                                    ALU.subtract, ALU.mult)
                    v.tensor_scalar(xn[:, u, 1, :], tile_of(k.x, t), k.mean[:, bass.ds(t, 1)], l_rstd[:, bass.ds(t, 1)],
                                    ALU.subtract, ALU.mult).then_inc(g["xn_ready"], 1)
                if turn.on[4]:
                    t, u = turn.tile(4)
                    dve.wait_ge(g["exp_done"], t + 1)
                    c = Chain(dve, g["rec_steps"], 2, t)
                    c(v.tensor_reduce(tot[:, u], pr[:, u], AX, ALU.add))
                    c(v.reciprocal(rec[:, u], tot[:, u]))
                if turn.on[3]:
                    t, u = turn.tile(3)
                    scores = ring[:, 0:2, :].rearrange("p a (j k) -> p (a j) k", k=P)
                    dve.wait_ge(g["s_done"], t + 1)
                    v.tensor_reduce(top[:, u], scores, AX, ALU.max).then_inc(g["top_done"], 1)
                    dve.wait_ge(g["top_done"], t + 1)
                    wait(dve, g["t_done"], t - 1)
                    v.tensor_tensor(pr[:, u], scores, top[:, u].unsqueeze(2).broadcast_to([P, H, P]), ALU.subtract)\
                        .then_inc(g["sub_done"], 1)
                if turn.on[1]:
                    t, u = turn.tile(1)
                    dve.wait_ge(g["xt_done"], t + 1)
                    wait(dve, g["k_done"], t - 1)
                    wait(dve, g["v_done"], t - 1)
                    for a, (gm, bt) in enumerate(((gx, bx), (gl, bl))):
                        last = v.tensor_scalar(xl[:, u, :, a, :], four(4)[:, a, :].rearrange("p (b n) -> p b n", b=2), gm[:], bt[:],
                                               ALU.mult, ALU.add)
                    last.then_inc(g["xl_ready"], 1)
                if turn.on[2]:
                    t, u = turn.tile(2)
                    dve.wait_ge(g["k_done"], t + 1)
                    wait(dve, g["kx_ready"], t - 1)
                    keys = ring[:, 1:3, :].rearrange("p a (j b c n) -> p (a j b) c n", j=2, b=2, c=2)
                    v.tensor_tensor(kc[:, u], keys[:, :, 0, :], cs[:].unsqueeze(1).broadcast_to([P, 2 * NP, S]), ALU.mult)
                    v.tensor_tensor(ks[:, u], ring[:, 3, :].rearrange("p (j n) -> p j n", n=S),
                                    sn[:].unsqueeze(1).broadcast_to([P, 2 * NP, S]), ALU.mult).then_inc(g["rope_in"], 1)
                if turn.on[5]:
                    t, u = turn.tile(5)
                    dve.wait_ge(g["wo_done"], t + 1)
                    c = Chain(dve, g["add_step"], 1, t)
                    add_residual(nc, dve, k, c, t, ring[:, 4, 0:P]).then_inc(g["add_done"], 1)
                if turn.on[4]:
                    t, u = turn.tile(4)
                    dve.wait_ge(g["pv_done"], t + 1)
                    wait(dve, g["ot_done"], t - 1)
                    v.tensor_tensor(o[:, u].rearrange("p (j h) d -> p h j d", h=2), ring[:, 5, :].rearrange("p (j h d) -> p h j d", h=2, d=HD),
                                    rec[:, u].rearrange("p (h j) -> p h j", h=2).unsqueeze(3).broadcast_to([P, 2, NP, HD]), ALU.mult)\
                        .then_inc(g["o_ready"], 1)

            pipeline(dve, 6, step)


def rope_tables():
    half = np.float32(1.0) / np.float32(10000.0) ** (np.arange(0, 64, 2, dtype=np.float32) / np.float32(64))
    theta = np.arange(S, dtype=np.float32)[:, None] * half[None, :]
    angles = np.concatenate([theta, theta], axis=-1).T
    sign = np.where(np.arange(64) < 32, -1.0, 1.0).astype(np.float32)[:, None]
    cos, sin = np.cos(angles), np.sin(angles) * sign
    return np.ascontiguousarray(np.tile(cos, (2, 1))), np.ascontiguousarray(np.tile(sin, (2, 1)))


def attention_64(nc, k, mask, w_q, w_kv, w_out, b_out):
    H, HD = 16, 64
    NP = H // 2
    scale = float(HD) ** -0.5
    s = Stage(nc, "a3")
    with s.ctx:
        wn, wt = s.sb("wn", [P, 8, P]), s.sb("wt", [P, 4, NP, P])
        mask_i, mask_f = s.sb("mask_i", [P, NT, P], mask.dtype), s.sb("mask_f", [P, NT, P], BF16)
        mb_i, mb_f, mb = s.sb("mb_i", [2, NT, S], mask.dtype), s.sb("mb_f", [2, NT, S]), s.sb("mb", [2, NT, S], BF16)
        own, bo = s.sb("own", [2, P], BF16), s.sb("bo", [P, P])
        xn, xt, ct, cm = (s.sb(n, [P, 2, P]) for n in ("xn", "xt", "ct", "cm"))
        q = s.sb("q", [P, 2, NP, P])
        kb = s.sb("kb", [P, 2, 2, NP, P])
        vb = s.sb("vb", [P, 2, 2, NP, 2, HD])
        pr = s.sb("pr", [P, 2, H, S])
        top, tot, rec = s.sb("top", [P, 2, H]), s.sb("tot", [P, 2, H]), s.sb("rec", [P, 2, H])
        prt = s.sb("prt", [P, NP, P])
        o, ot = s.sb("o", [P, 2, H, HD]), s.sb("ot", [P, NP, P])
        ring = s.ps("ring", [P, 8, 512])
        QW, KW, VW, OW = range(4)

        def bank(n, m=1):
            return ring[:, n:n + m, :]

        names = ("w_in w_t w_ready masks_in consts stats mask_steps xn_ready ct_ready xt_done xt_ready q_done k_done "
                 "q_ready k_ready v_done v_ready s_done top_done sub_done exp_done rec_steps t_done prt_ready pv_done o_ready "
                 "ot_done ot_ready wo_done add_step add_done").split()
        g = {n: s.sem(n) for n in names}
        block = s.ctx.enter_context(nc.Block())
        sources = [w_q.rearrange("(j p) d -> p j d", p=P), w_kv[0:H * HD, :].rearrange("(j p) d -> p j d", p=P),
                   w_kv[H * HD:, :].rearrange("(j p) d -> p j d", p=P), w_out.rearrange("p (j d) -> p j d", d=P)]

        @block.sync
        def _(sp):
            per_batch = mask.rearrange("(t b) s -> b t s", b=2)
            sp.dma_start(mb_i[:], per_batch).then_inc(g["masks_in"], 16)
            sp.dma_start(mask_i[:].rearrange("p t n -> p (t n)"),
                         mask.rearrange("b s -> (b s)").partition_broadcast(P)).then_inc(g["masks_in"], 16)
            sp.dma_start(bo[:], b_out.partition_broadcast(P)).then_inc(g["masks_in"], 16)
            for n in range(4):
                wait(sp, g["w_t"], n)
                sp.dma_start(wn[:], sources[n]).then_inc(g["w_in"], 16)

        @block.gpsimd
        def _(pool):
            nc.gpsimd.memset(own[:], 1.0).then_inc(g["consts"], 1)
            nc.gpsimd.memset(kb[:], 0.0).then_inc(g["consts"], 1)
            nc.gpsimd.memset(vb[:], 0.0).then_inc(g["consts"], 1)
            pool.wait_ge(g["consts"], 3)
            nc.gpsimd.affine_select(out=own[:], in_=own[:], compare_op=ALU.is_ge, fill=0.0, base=0,
                                    pattern=[[1, P]], channel_multiplier=-S).then_inc(g["consts"], 1)
            pool.wait_ge(g["consts"], 4)
            nc.gpsimd.affine_select(out=own[:], in_=own[:], compare_op=ALU.is_ge, fill=0.0, base=S - 1,
                                    pattern=[[-1, P]], channel_multiplier=S).then_inc(g["consts"], 1)
            pool.wait_ge(g["mask_steps"], 3)

            def step(turn):
                if turn.on[2]:
                    t, u = turn.tile(2)
                    wait(pool, g["k_done"], t - 1)
                    wait(pool, g["v_done"], t - 1)
                    nc.gpsimd.tensor_copy(ct[:, u, :], tile_of(k.ct, t))
                    nc.gpsimd.tensor_tensor(cm[:, u, :], tile_of(k.ct, t), tile_of(mask_f, t), ALU.mult)\
                        .then_inc(g["ct_ready"], 1)

            pipeline(pool, 6, step)

        @block.tensor
        def _(pe):
            for n in range(4):
                pe.wait_ge(g["w_in"], 16 * (n + 1))
                wait(pe, g["w_ready"], n - 1)
                for j in range(8):
                    c = 1024 * (n % 2) + j * P
                    last = nc.tensor.transpose(ring[:, c // 512, c % 512:c % 512 + P], wn[:, j, :], k.ident[:])
                last.then_inc(g["w_t"], 1)
            pe.wait_ge(g["w_ready"], 4)
            pe.wait_ge(g["consts"], 5)
            pe.wait_ge(g["mask_steps"], 3)

            def step(turn):
                if turn.on[3]:
                    t, u = turn.tile(3)
                    pe.wait_ge(g["q_ready"], t + 1)
                    pe.wait_ge(g["k_ready"], t + 1)
                    wait(pe, g["v_ready"], t)
                    bias = tile_of(mb, t).unsqueeze(1).broadcast_to([2, 8, S])
                    for n in range(2):
                        nc.tensor.matmul(ring[:, n, :], own[:], bias, start=True, stop=False)
                        for b in range(2):
                            rows = slice(64 * b, 64 * b + 64)
                            for j in range(4):
                                last = nc.tensor.matmul(ring[rows, n, j * P:(j + 1) * P], q[:, u, 4 * n + j, rows],
                                                        kb[:, u, b, 4 * n + j, :], start=False, stop=(j == 3))
                    last.then_inc(g["s_done"], 1)
                if turn.on[1]:
                    t, u = turn.tile(1)
                    pe.wait_ge(g["xn_ready"], t + 1)
                    wait(pe, g["q_ready"], t - 1)
                    wait(pe, g["xt_ready"], t)
                    nc.tensor.transpose(ring[:, 2, 0:P], xn[:, u, :], k.ident[:]).then_inc(g["xt_done"], 1)
                if turn.on[4]:
                    t, u = turn.tile(4)
                    pe.wait_ge(g["exp_done"], t + 1)
                    pe.wait_ge(g["k_ready"], up_to(t + 2))
                    wait(pe, g["prt_ready"], t)
                    for j in range(NP):
                        last = nc.tensor.transpose(ring[:, 3 + j // 4, (j % 4) * P:(j % 4 + 1) * P],
                                                   pr[:, u, 2 * j:2 * j + 2, :].rearrange("p h k -> p (h k)"), k.ident[:])
                    last.then_inc(g["t_done"], 1)
                if turn.on[5]:
                    t, u = turn.tile(5)
                    pe.wait_ge(g["o_ready"], t + 1)
                    wait(pe, g["add_done"], t)
                    wait(pe, g["ot_ready"], t)
                    for j in range(NP):
                        last = nc.tensor.transpose(ring[:, 5 + j // 4, (j % 4) * P:(j % 4 + 1) * P],
                                                   o[:, u, 2 * j:2 * j + 2, :].rearrange("p h d -> p (h d)"), k.ident[:])
                    last.then_inc(g["ot_done"], 1)
                if turn.on[3]:
                    t, u = turn.tile(3)
                    pe.wait_ge(g["ct_ready"], t + 1)
                    wait(pe, g["o_ready"], t - 1)
                    wait(pe, g["v_ready"], t)
                    pe.wait_ge(g["sub_done"], t + 1)
                    for h in range(2):
                        last = nc.tensor.matmul(ring[:, (7 + h) % 8, :], ct[:, u, :],
                                                wt[:, VW].rearrange("p j (h d) -> p h j d", h=2)[:, h], start=True, stop=True)
                    last.then_inc(g["v_done"], 1)
                if turn.on[2]:
                    t, u = turn.tile(2)
                    pe.wait_ge(g["xt_ready"], up_to(t + 2))
                    wait(pe, g["sub_done"], t)
                    for j in range(NP):
                        last = nc.tensor.matmul(ring[:, 1 + j // 4, (j % 4) * P:(j % 4 + 1) * P], wt[:, QW, j, :], xt[:, u, :],
                                                start=True, stop=True)
                    last.then_inc(g["q_done"], 1)
                    pe.wait_ge(g["ct_ready"], t + 1)
                    wait(pe, g["prt_ready"], t - 1)
                    for j in range(NP):
                        last = nc.tensor.matmul(ring[:, 3 + j // 4, (j % 4) * P:(j % 4 + 1) * P], wt[:, KW, j, :], cm[:, u, :],
                                                start=True, stop=True)
                    last.then_inc(g["k_done"], 1)
                if turn.on[5]:
                    t, u = turn.tile(5)
                    pe.wait_ge(g["ot_ready"], t + 1)
                    for j in range(NP):
                        last = nc.tensor.matmul(ring[:, 5, 0:P], ot[:, j, :], wt[:, OW, j, :], start=(j == 0), stop=(j == NP - 1))
                    last.then_inc(g["wo_done"], 1)
                if turn.on[4]:
                    t, u = turn.tile(4)
                    pe.wait_ge(g["prt_ready"], t + 1)
                    pe.wait_ge(g["v_ready"], up_to(t + 2))
                    wait(pe, g["ot_ready"], t)
                    wait(pe, g["o_ready"], t)
                    for b in range(2):
                        rows = slice(64 * b, 64 * b + 64)
                        for j in range(NP):
                            last = nc.tensor.matmul(ring[rows, 6 + j // 4, (j % 4) * P:(j % 4 + 1) * P], prt[:, j, rows],
                                                    vb[:, u, b, j, :, :], start=True, stop=True)
                    last.then_inc(g["pv_done"], 1)

            pipeline(pe, 6, step)

        def pairs(n):
            return bank(n, 2).rearrange("p a (j n) -> p (a j) n", n=P)

        @block.scalar
        def _(act):
            finish_statistics(nc, act, None, k, "act", g["stats"])
            for n in range(4):
                act.wait_ge(g["w_t"], n + 1)
                nc.scalar.activation(wt[:, n], pairs(2 * (n % 2)), ACT.Copy).then_inc(g["w_ready"], 1)
            act.wait_ge(g["consts"], 5)

            def step(turn):
                if turn.on[1]:
                    t, u = turn.tile(1)
                    act.wait_ge(g["xt_done"], t + 1)
                    wait(act, g["q_done"], t - 1)
                    nc.scalar.activation(xt[:, u, :], ring[:, 2, 0:P], ACT.Copy).then_inc(g["xt_ready"], 1)
                if turn.on[4]:
                    t, u = turn.tile(4)
                    act.wait_ge(g["t_done"], t + 1)
                    wait(act, g["pv_done"], t)
                    nc.scalar.activation(prt[:], pairs(3), ACT.Copy).then_inc(g["prt_ready"], 1)
                if turn.on[3]:
                    t, u = turn.tile(3)
                    act.wait_ge(g["sub_done"], t + 1)
                    nc.scalar.activation(pr[:, u], pr[:, u], ACT.Exp, scale=scale).then_inc(g["exp_done"], 1)
                    act.wait_ge(g["v_done"], t + 1)
                    wait(act, g["pv_done"], t - 1)
                    for h in range(2):
                        for b in range(2):
                            last = nc.scalar.activation(vb[64 * h:64 * h + 64, u, b, :, h, :],
                                                        ring[64 * b:64 * b + 64, (7 + h) % 8, :].rearrange("p (j d) -> p j d", d=HD),
                                                        ACT.Copy)
                    last.then_inc(g["v_ready"], 1)
                if turn.on[2]:
                    t, u = turn.tile(2)
                    act.wait_ge(g["q_done"], t + 1)
                    wait(act, g["s_done"], t - 1)
                    nc.scalar.activation(q[:, u], pairs(1), ACT.Copy).then_inc(g["q_ready"], 1)
                    act.wait_ge(g["k_done"], t + 1)
                    for h in range(2):
                        rows = slice(64 * h, 64 * h + 64)
                        for b in range(2):
                            last = nc.scalar.activation(kb[rows, u, b, :, rows], pairs(3)[rows, :, 64 * b:64 * b + 64], ACT.Copy)
                    last.then_inc(g["k_ready"], 1)

            pipeline(act, 6, step)

        @block.vector
        def _(dve):
            v = nc.vector
            finish_statistics(nc, None, dve, k, "dve", g["stats"])
            dve.wait_ge(g["masks_in"], 48)
            v.tensor_scalar(mask_f[:], mask_i[:], 0.0, None, ALU.not_equal).then_inc(g["mask_steps"], 1)
            v.tensor_scalar(mb_f[:], mb_i[:], 0.0, None, ALU.not_equal).then_inc(g["mask_steps"], 1)
            dve.wait_ge(g["mask_steps"], 2)
            v.tensor_scalar(mb[:], mb_f[:], NEG, -NEG, ALU.mult, ALU.add).then_inc(g["mask_steps"], 1)

            def step(turn):
                if turn.on[0]:
                    t, u = turn.tile(0)
                    wait(dve, g["xt_done"], t - 1)
                    v.tensor_scalar(xn[:, u, :], tile_of(k.x, t), k.mean[:, bass.ds(t, 1)], k.rstd[:, bass.ds(t, 1)],
                                    ALU.subtract, ALU.mult).then_inc(g["xn_ready"], 1)
                if turn.on[4]:
                    t, u = turn.tile(4)
                    dve.wait_ge(g["exp_done"], t + 1)
                    c = Chain(dve, g["rec_steps"], 2, t)
                    c(v.tensor_reduce(tot[:, u], pr[:, u], AX, ALU.add))
                    c(v.reciprocal(rec[:, u], tot[:, u]))
                if turn.on[3]:
                    t, u = turn.tile(3)
                    scores = bank(0, 2).rearrange("p a (h k) -> p (a h) k", k=S)
                    dve.wait_ge(g["s_done"], t + 1)
                    v.tensor_reduce(top[:, u], scores, AX, ALU.max).then_inc(g["top_done"], 1)
                    dve.wait_ge(g["top_done"], t + 1)
                    wait(dve, g["t_done"], t - 1)
                    v.tensor_tensor(pr[:, u], scores, top[:, u].unsqueeze(2).broadcast_to([P, H, S]), ALU.subtract)\
                        .then_inc(g["sub_done"], 1)
                if turn.on[5]:
                    t, u = turn.tile(5)
                    dve.wait_ge(g["ot_done"], t + 1)
                    wait(dve, g["wo_done"], t)
                    v.tensor_copy(ot[:], pairs(5)).then_inc(g["ot_ready"], 1)
                    dve.wait_ge(g["wo_done"], t + 1)
                    c = Chain(dve, g["add_step"], 2, t)
                    c(v.tensor_tensor(tile_of(k.x, t), tile_of(k.x, t), bo[:], ALU.add))
                    add_residual(nc, dve, k, c, t, ring[:, 5, 0:P]).then_inc(g["add_done"], 1)
                if turn.on[4]:
                    t, u = turn.tile(4)
                    dve.wait_ge(g["pv_done"], t + 1)
                    wait(dve, g["ot_done"], t - 1)
                    v.tensor_tensor(o[:, u], bank(6, 2).rearrange("p a (h d) -> p (a h) d", d=HD),
                                    rec[:, u].unsqueeze(2).broadcast_to([P, H, HD]), ALU.mult).then_inc(g["o_ready"], 1)

            pipeline(dve, 6, step)


def store_stage(nc, k, out):
    s = Stage(nc, "store")
    with s.ctx:
        stored = s.sem("stored")
        block = s.ctx.enter_context(nc.Block())

        @block.sync
        def _(sp):
            sp.dma_start(out.rearrange("(t b) s d -> (b s) t d", b=2), k.x[:]).then_inc(stored, 16)
            sp.wait_ge(stored, 16)


def program(nc, a, out, stages=range(8)):
    k = Kept()
    with ExitStack() as ctx:
        def sb(name, shape, dt=F32):
            return ctx.enter_context(nc.sbuf_tensor(name, shape, dt))

        k.x, k.c, k.ct = sb("x", [P, NT, D]), sb("c", [P, NT, D]), sb("ct", [P, NT, P])
        k.ident = sb("ident", [P, P])
        k.stats = sb("stats", [P, NT, 6])
        k.mean, k.rstd, k.var, k.vareps, k.root, k.tmp_a, k.tmp_b = (
            sb(n, [P, NT]) for n in ("mean", "rstd", "var", "vareps", "root", "tmp_a", "tmp_b"))
        load_stage(nc, k, a["x"], a["ctx_1024"], a["itok_BxS_0_511"])
        run = {
            1: lambda: ffn_quantised(nc, k, a["L0_ffn_w_gate"], a["L0_ffn_w_up"], a["L0_ffn_w_down"]),
            2: lambda: attention_lookback(nc, k, a["itok_BxS_0_511"], a["L1_xattn_Wq"], a["L1_xattn_Wkv"], a["L1_xattn_Wo"]),
            3: lambda: mixture_gelu(nc, k, "m1", a["L1_ffn_wg"], None, a["L1_ffn_w1"], a["L1_ffn_b1"], a["L1_ffn_w2"],
                                    a["L1_ffn_b2"], 1, NTOK // E),
            7: lambda: mixture_gelu(nc, k, "m3", a["L3_ffn_Wg"], a["L3_ffn_bg"], a["L3_ffn_W1"], a["L3_ffn_b1"], a["L3_ffn_W2"],
                                    a["L3_ffn_b2"], 2, int(np.ceil(1.2 * NTOK * 2 / E))),
            5: lambda: mixture_swiglu(nc, k, "m2", *(a[f"L2_ffn_{n}"] for n in ("Wr", "Wu", "Wg", "Wd", "Wu_s", "Wg_s", "Wd_s"))),
            4: lambda: attention_latent(nc, k, *(a[f"L2_xattn_{n}"] for n in ("gamma_x", "beta_x", "gamma_l", "beta_l", "Wq", "Wkv", "Wo")),
                                        a["rope_cos"], a["rope_sin"]),
            6: lambda: attention_64(nc, k, a["mask_BxS2_bf1"], *(a[f"L3_xattn_{n}"] for n in ("Wq", "Wkv", "Wout", "b_out"))),
            0: lambda: attention_8(nc, k, a["mask_BxS2_if1"], *(a[f"L0_xattn_w_{n}"] for n in "qkvo")),
        }
        for n in stages:
            run[n]()
        store_stage(nc, k, out)


def kernel(**inputs):
    import concourse.bacc as bacc
    from concourse.bass_utils import run_bass_kernel_spmd

    nc = bacc.Bacc("TRN2", target_bir_lowering=False, num_devices=1)
    arrays, args = {}, {}
    cos, sin = rope_tables()
    for name, value in {**inputs, "rope_cos": cos, "rope_sin": sin}.items():
        a = np.ascontiguousarray(value)
        arrays[f"in_{name}"] = a
        args[name] = nc.dram_tensor(f"in_{name}", a.shape, mybir.dt.from_np(a.dtype), kind="ExternalInput").ap()
    out = nc.dram_tensor("out_x", (B, S, D), F32, kind="ExternalOutput").ap()
    program(nc, args, out)
    r = run_bass_kernel_spmd(nc, [arrays], core_ids=[0])
    return r.results[0]["out_x"]
```

```python
from contextlib import ExitStack

import numpy as np

import concourse.bass as bass
from concourse import mybir

F32 = mybir.dt.float32
BF16 = mybir.dt.bfloat16
I32 = mybir.dt.int32
U32 = mybir.dt.uint32
ACT = mybir.ActivationFunctionType
ALU = mybir.AluOpType
AX = mybir.AxisListType.X

P = 128
B, S, D = 64, 64, 128
NTOK = B * S
NT = NTOK // P
EPS = 1e-5
NEG = 1e30
ROUND = 12582912.0


def tile_of(ap, t):
    if isinstance(t, int):
        return ap[:, t, :]
    return ap[:, bass.ds(t, 1), :].rearrange("p a n -> p (a n)")


def tiles_of(ap, t, n):
    return ap[:, t * n:(t + 1) * n] if isinstance(t, int) else ap[:, bass.ds(t * n, n)]


def wait(eng, sem, value):
    if not isinstance(value, int) or value > 0:
        eng.wait_ge(sem, value)


UNROLL = 4


class Turn:

    def __init__(self, t, m, on, unroll, slots, start):
        self.t, self.m, self.on, self.unroll, self.slots, self.start = t, m, on, unroll, slots, start

    def tile(self, p):
        return self.t - p, (self.m - p) % self.slots

    def group(self, p):
        if isinstance(self.t, int):
            return (self.t - p) // self.unroll
        i, first = self.start
        return i + (first - p) // self.unroll

    def half(self, p):
        if isinstance(self.t, int):
            return (self.t - p) // 2
        i, first = self.start
        return i * (self.unroll // 2) + (first - p) // 2


def pipeline_by(eng, depth, step, tiles, unroll, lead=None, slots=None):
    lead = depth - 1 if lead is None else lead
    slots = slots or unroll

    def turn(t):
        step(Turn(t, t % unroll, [0 <= t - p < tiles for p in range(depth)], unroll, slots, None))

    for t in range(lead):
        turn(t)
    full = (tiles - lead) // unroll
    with eng.Fori(0, full) as i:
        for j in range(unroll):
            first = lead + j
            step(Turn(i * unroll + first, first % unroll, [True] * depth, unroll, slots, (i, first)))
    for t in range(lead + unroll * full, tiles + depth - 1):
        turn(t)


def pipeline(eng, depth, step, tiles=NT, lead=None):
    pipeline_by(eng, depth, step, tiles, UNROLL, lead, 2)


def up_to(value, most=NT):
    return min(value, most) if isinstance(value, int) else value


class Stage:

    def __init__(self, nc, name):
        self.nc, self.name, self.ctx, self.sems = nc, name, ExitStack(), []
        self.ctx.callback(self.clear)

    def clear(self):
        self.nc.clear_and_free_semaphores(self.sems)
        self.nc.all_engine_barrier()

    def sb(self, name, shape, dt=F32):
        return self.ctx.enter_context(self.nc.sbuf_tensor(f"{self.name}_{name}", shape, dt))

    def ps(self, name, shape, dt=F32):
        return self.ctx.enter_context(self.nc.psum_tensor(f"{self.name}_{name}", shape, dt))

    def sem(self, name):
        self.sems.append(self.nc.alloc_semaphore(name=f"{self.name}_{name}"))
        return self.sems[-1]


class Chain:

    def __init__(self, eng, sem, per_turn, turn):
        self.eng, self.sem, self.per_turn = eng, sem, per_turn
        self.base, self.n = turn * per_turn, 0

    def __call__(self, ins):
        self.n += 1
        ins.then_inc(self.sem, 1)
        self.eng.wait_ge(self.sem, self.base + self.n)


def finish_statistics(nc, act, dve, k, part, sem):
    st, mu, rs = k.stats, k.mean, k.rstd
    ta, tb, va = k.tmp_a, k.tmp_b, k.var
    if part == "dve":
        c = Chain(dve, sem, 0, 0)
        c(nc.vector.tensor_tensor(mu[:], st[:, :, 1], st[:, :, 4], ALU.add))
        c(nc.vector.tensor_scalar(mu[:], mu[:], 0.5, None, ALU.mult))
        c(nc.vector.tensor_tensor(ta[:], st[:, :, 1], st[:, :, 4], ALU.subtract))
        c(nc.vector.tensor_tensor(ta[:], ta[:], ta[:], ALU.mult))
        c(nc.vector.tensor_tensor(tb[:], st[:, :, 2], st[:, :, 5], ALU.add))
        c(nc.vector.tensor_scalar(tb[:], tb[:], 1.0 / D, None, ALU.mult))
        c(nc.vector.tensor_scalar(ta[:], ta[:], 0.25, None, ALU.mult))
        c(nc.vector.tensor_tensor(va[:], ta[:], tb[:], ALU.add))
        inverse_root(nc, dve, c, k, va, rs)
    else:
        act.wait_ge(sem, 9)
        nc.scalar.activation(k.root[:], k.vareps[:], ACT.Sqrt).then_inc(sem, 1)


def inverse_root(nc, dve, c, k, va, rs):
    c(nc.vector.tensor_scalar(k.vareps[:], va[:], EPS, None, ALU.add))
    c.n += 1
    dve.wait_ge(c.sem, c.base + c.n)
    c(nc.vector.reciprocal(rs[:], k.root[:]))
    c(nc.vector.tensor_tensor(k.tmp_a[:], rs[:], rs[:], ALU.mult))
    c(nc.vector.tensor_tensor(k.tmp_a[:], k.tmp_a[:], k.vareps[:], ALU.mult))
    c(nc.vector.tensor_scalar(k.tmp_a[:], k.tmp_a[:], -0.5, 1.5, ALU.mult, ALU.add))
    c(nc.vector.tensor_tensor(rs[:], rs[:], k.tmp_a[:], ALU.mult))


class Kept:
    pass


def add_residual(nc, dve, k, c, t, r):
    c(nc.vector.tensor_tensor(tile_of(k.x, t), tile_of(k.x, t), r, ALU.add))
    return nc.vector.bn_stats(tile_of(k.stats, t), tile_of(k.x, t))


def load_stage(nc, k, x, ctx):
    s = Stage(nc, "load")
    with s.ctx:
        c_loaded, x_loaded = s.sem("c_loaded"), s.sem("x_loaded")
        ident_set, ctx_t, ctx_copied = s.sem("ident_set"), s.sem("ctx_t"), s.sem("ctx_copied")
        step = s.sem("step")
        pt = [s.ps(f"pt{i}", [P, 4, P]) for i in range(2)]
        block = s.ctx.enter_context(nc.Block())

        @block.sync
        def _(sp):
            sp.dma_start(k.x[:], x.rearrange("(t b) s d -> (b s) t d", b=2)).then_inc(x_loaded, 16)
            sp.dma_start(k.c[:], ctx.rearrange("(t b) s d -> (b s) t d", b=2)).then_inc(c_loaded, 16)

        @block.gpsimd
        def _(pool):
            nc.gpsimd.memset(k.ident[:], 0.0).then_inc(ident_set, 1)
            pool.wait_ge(ident_set, 1)
            nc.gpsimd.affine_select(out=k.ident[:], in_=k.ident[:], compare_op=ALU.not_equal, fill=1.0, base=0,
                                    pattern=[[-1, P]], channel_multiplier=1).then_inc(ident_set, 1)

        @block.tensor
        def _(pe):
            pe.wait_ge(ident_set, 2)
            pe.wait_ge(c_loaded, 16)
            for g in range(NT // 4):
                wait(pe, ctx_copied, g - 1)
                for j in range(4):
                    last = nc.tensor.transpose(pt[g % 2][:, j, :], k.c[:, 4 * g + j, :], k.ident[:])
                last.then_inc(ctx_t, 1)

        @block.scalar
        def _(act):
            for g in range(NT // 4):
                act.wait_ge(ctx_t, g + 1)
                nc.scalar.activation(k.ct[:, 4 * g:4 * g + 4, :], pt[g % 2][:], ACT.Copy).then_inc(ctx_copied, 1)

        @block.vector
        def _(dve):
            dve.wait_ge(x_loaded, 16)
            for t in range(NT):
                nc.vector.bn_stats(k.stats[:, t, :], k.x[:, t, :]).then_inc(step, 1)
            dve.wait_ge(c_loaded, 16)
            for t in range(NT):
                nc.vector.bn_stats(k.c_stats[:, t, :], k.c[:, t, :]).then_inc(step, 1)


def attention_8(nc, k, mask, w_q, w_k, w_v, w_o):
    H, HD = 16, 8
    scale = float(HD) ** -0.5
    s = Stage(nc, "a0")
    with s.ctx:
        wn, wt = s.sb("wn", [P, 4, P]), s.sb("wt", [P, 4, P])
        head = s.sb("head", [P, 8])
        mask_i, mask_f = s.sb("mask_i", [P, NT, P], I32), s.sb("mask_f", [P, NT, P], BF16)
        mb_i, mb = s.sb("mb_i", [2, NT, S], I32), s.sb("mb", [2, NT, S], BF16)
        mb_f = s.sb("mb_f", [2, NT, S])
        own = s.sb("own", [2, P], BF16)
        xn, xt = s.sb("xn", [P, 2, P]), s.sb("xt", [P, 2, P])
        ct, cm = s.sb("ct", [P, 2, P]), s.sb("cm", [P, 2, P])
        q = s.sb("q", [P, 2, 2, P])
        kt = s.sb("kt", [P, 2, 2, S])
        ke = s.sb("ke", [P, 2, 2, 8, S])
        v = s.sb("v", [P, 2, 2, 8, 2, HD])
        pr = s.sb("pr", [P, 2, H, S])
        top, tot, rec = s.sb("top", [P, 2, H]), s.sb("tot", [P, 2, H]), s.sb("rec", [P, 2, H])
        prt = s.sb("prt", [P, 8, P])
        o, ot = s.sb("o", [P, 2, H, HD]), s.sb("ot", [P, P])
        p_xt, p_qkv = s.ps("p_xt", [P, 4, P]), s.ps("p_qkv", [P, 4, P])
        p_s, p_t = s.ps("p_s", [P, 2, 8, S]), s.ps("p_t", [P, 8, P])
        p_o, p_r = s.ps("p_o", [P, 4, H, HD]), s.ps("p_r", [P, 4, P])
        names = ("w_in w_t w_ready masks_in consts stats mask_steps xn_ready ct_ready xt_done xt_ready proj_done "
                 "qkv_ready ke_ready s_done top_done sub_done exp_done rec_steps t_done prt_ready pv_done o_ready "
                 "v_done v_ready ot_done ot_ready wo_done add_step add_done").split()
        g = {n: s.sem(n) for n in names}
        block = s.ctx.enter_context(nc.Block())

        @block.sync
        def _(sp):
            per_batch = mask.rearrange("(t b) s -> b t s", b=2)
            sp.dma_start(mb_i[:], per_batch).then_inc(g["masks_in"], 16)
            sp.dma_start(mask_i[:].rearrange("p t n -> p (t n)"),
                         mask.rearrange("b s -> (b s)").partition_broadcast(P)).then_inc(g["masks_in"], 16)
            for j, w in enumerate((w_q, w_k, w_v, w_o)):
                sp.dma_start(wn[:, j, :], w).then_inc(g["w_in"], 16)

        @block.gpsimd
        def _(pool):
            nc.gpsimd.memset(head[:], 1.0).then_inc(g["consts"], 1)
            nc.gpsimd.memset(own[:], 1.0).then_inc(g["consts"], 1)
            nc.gpsimd.memset(q[:], 0.0).then_inc(g["consts"], 1)
            nc.gpsimd.memset(v[:], 0.0).then_inc(g["consts"], 1)
            pool.wait_ge(g["consts"], 4)
            nc.gpsimd.affine_select(out=own[:], in_=own[:], compare_op=ALU.is_ge, fill=0.0, base=0,
                                    pattern=[[1, P]], channel_multiplier=-S).then_inc(g["consts"], 1)
            for b in range(2):
                part = head[64 * b:64 * b + 64, :]
                nc.gpsimd.affine_select(out=part, in_=part, compare_op=ALU.is_ge, fill=0.0, base=0,
                                        pattern=[[-HD, 8]], channel_multiplier=1).then_inc(g["consts"], 1)
            pool.wait_ge(g["consts"], 7)
            nc.gpsimd.affine_select(out=own[:], in_=own[:], compare_op=ALU.is_ge, fill=0.0, base=S - 1,
                                    pattern=[[-1, P]], channel_multiplier=S).then_inc(g["consts"], 1)
            for b in range(2):
                part = head[64 * b:64 * b + 64, :]
                nc.gpsimd.affine_select(out=part, in_=part, compare_op=ALU.is_ge, fill=0.0, base=HD - 1,
                                        pattern=[[HD, 8]], channel_multiplier=-1).then_inc(g["consts"], 1)
            pool.wait_ge(g["consts"], 10)
            pool.wait_ge(g["mask_steps"], 3)

            def step(turn):
                if turn.on[2]:
                    t, u = turn.tile(2)
                    wait(pool, g["proj_done"], t - 1)
                    wait(pool, g["v_done"], t - 1)
                    nc.gpsimd.tensor_copy(ct[:, u, :], tile_of(k.ct, t))
                    nc.gpsimd.tensor_tensor(cm[:, u, :], tile_of(k.ct, t), tile_of(mask_f, t), ALU.mult)\
                        .then_inc(g["ct_ready"], 1)
                    pool.wait_ge(g["qkv_ready"], t + 1)
                    wait(pool, g["s_done"], t - 1)
                    nc.gpsimd.tensor_tensor(
                        ke[:, u], kt[:, u].unsqueeze(2).broadcast_to([P, 2, 8, S]),
                        head[:].unsqueeze(1).unsqueeze(3).broadcast_to([P, 2, 8, S]), ALU.mult).then_inc(g["ke_ready"], 1)

            pipeline(pool, 6, step)

        @block.tensor
        def _(pe):
            pe.wait_ge(g["w_in"], 64)
            for j in range(4):
                last = nc.tensor.transpose(p_xt[:, j, :], wn[:, j, :], k.ident[:])
            last.then_inc(g["w_t"], 1)
            pe.wait_ge(g["w_ready"], 1)
            pe.wait_ge(g["consts"], 10)
            pe.wait_ge(g["mask_steps"], 3)

            def step(turn):
                if turn.on[3]:
                    t, u = turn.tile(3)
                    pe.wait_ge(g["ct_ready"], t + 1)
                    wait(pe, g["v_ready"], t)
                    wait(pe, g["add_done"], t - 2)
                    for h in range(2):
                        wv = wt[:, 2, :].rearrange("p (j h d) -> p j h d", j=8, h=2)[:, :, h, :]
                        for b in range(2):
                            last = nc.tensor.matmul(p_r[64 * h:64 * h + 64, 2, 64 * b:64 * b + 64],
                                                    ct[:, u, 64 * b:64 * b + 64], wv, start=True, stop=True)
                    last.then_inc(g["v_done"], 1)
                if turn.on[1]:
                    t, u = turn.tile(1)
                    pe.wait_ge(g["xn_ready"], t + 1)
                    wait(pe, g["xt_ready"], t)
                    nc.tensor.transpose(p_xt[:, 0, :], xn[:, u, :], k.ident[:]).then_inc(g["xt_done"], 1)
                if turn.on[3]:
                    t, u = turn.tile(3)
                    pe.wait_ge(g["ke_ready"], t + 1)
                    wait(pe, g["sub_done"], t)
                    bias = tile_of(mb, t).unsqueeze(1).broadcast_to([2, 8, S])
                    for h in range(2):
                        nc.tensor.matmul(p_s[:, h], own[:], bias, start=True, stop=False)
                        last = nc.tensor.matmul(p_s[:, h], q[:, u, h, :], ke[:, u, h], start=False, stop=True)
                    last.then_inc(g["s_done"], 1)
                if turn.on[4]:
                    t, u = turn.tile(4)
                    pe.wait_ge(g["exp_done"], t + 1)
                    wait(pe, g["prt_ready"], t)
                    for j in range(8):
                        last = nc.tensor.transpose(p_t[:, j, :], pr[:, u, 2 * j:2 * j + 2, :].rearrange("p h k -> p (h k)"), k.ident[:])
                    last.then_inc(g["t_done"], 1)
                if turn.on[5]:
                    t, u = turn.tile(5)
                    pe.wait_ge(g["o_ready"], t + 1)
                    pe.wait_ge(g["v_ready"], up_to(t + 3))
                    wait(pe, g["add_done"], t)
                    nc.tensor.transpose(p_r[:, 0, :], o[:, u].rearrange("p h d -> p (h d)"), k.ident[:]).then_inc(g["ot_done"], 1)
                if turn.on[2]:
                    t, u = turn.tile(2)
                    pe.wait_ge(g["xt_ready"], t + 1)
                    pe.wait_ge(g["ct_ready"], t + 1)
                    wait(pe, g["qkv_ready"], t)
                    for b in range(2):
                        rows = slice(64 * b, 64 * b + 64)
                        for h in range(2):
                            cols = slice(64 * h, 64 * h + 64)
                            nc.tensor.matmul(p_qkv[rows, 0, cols], wt[:, 0, cols], xt[:, u, rows], start=True, stop=True)
                            last = nc.tensor.matmul(p_qkv[rows, 1, cols], wt[:, 1, cols], cm[:, u, rows], start=True, stop=True)
                    last.then_inc(g["proj_done"], 1)
                if turn.on[5]:
                    t, u = turn.tile(5)
                    pe.wait_ge(g["ot_ready"], t + 1)
                    nc.tensor.matmul(p_r[:, 1, :], ot[:], wt[:, 3, :], start=True, stop=True).then_inc(g["wo_done"], 1)
                if turn.on[4]:
                    t, u = turn.tile(4)
                    pe.wait_ge(g["prt_ready"], t + 1)
                    wait(pe, g["o_ready"], t)
                    for b in range(2):
                        for j in range(8):
                            last = nc.tensor.matmul(p_o[64 * b:64 * b + 64, 0, 2 * j:2 * j + 2, :],
                                                    prt[:, j, 64 * b:64 * b + 64], v[:, u, b, j, :, :],
                                                    start=True, stop=True)
                    last.then_inc(g["pv_done"], 1)

            pipeline(pe, 6, step)

        @block.scalar
        def _(act):
            finish_statistics(nc, act, None, k, "act", g["stats"])
            act.wait_ge(g["w_t"], 1)
            nc.scalar.activation(wt[:], p_xt[:], ACT.Copy).then_inc(g["w_ready"], 1)
            act.wait_ge(g["consts"], 10)

            def step(turn):
                if turn.on[3]:
                    t, u = turn.tile(3)
                    act.wait_ge(g["v_done"], t + 1)
                    wait(act, g["pv_done"], t - 1)
                    for h in range(2):
                        rows = slice(64 * h, 64 * h + 64)
                        last = nc.scalar.activation(v[rows, u, :, :, h, :],
                                                    p_r[rows, 2, :].rearrange("p (b j d) -> p b j d", b=2, j=8), ACT.Copy)
                    last.then_inc(g["v_ready"], 1)
                if turn.on[1]:
                    t, u = turn.tile(1)
                    act.wait_ge(g["xt_done"], t + 1)
                    wait(act, g["proj_done"], t - 1)
                    nc.scalar.activation(xt[:, u, :], p_xt[:, 0, :], ACT.Copy).then_inc(g["xt_ready"], 1)
                if turn.on[4]:
                    t, u = turn.tile(4)
                    act.wait_ge(g["t_done"], t + 1)
                    wait(act, g["pv_done"], t)
                    nc.scalar.activation(prt[:], p_t[:], ACT.Copy).then_inc(g["prt_ready"], 1)
                if turn.on[2]:
                    t, u = turn.tile(2)
                    act.wait_ge(g["proj_done"], t + 1)
                    wait(act, g["s_done"], t - 1)
                    wait(act, g["ke_ready"], t - 1)
                    for b in range(2):
                        rows = slice(64 * b, 64 * b + 64)
                        nc.scalar.activation(q[rows, u, :, rows], p_qkv[rows, 0, :].rearrange("p (h n) -> p h n", h=2), ACT.Copy)
                    nc.scalar.activation(kt[:, u], p_qkv[:, 1, :].rearrange("p (h n) -> p h n", h=2), ACT.Copy)\
                        .then_inc(g["qkv_ready"], 1)
                if turn.on[5]:
                    t, u = turn.tile(5)
                    act.wait_ge(g["ot_done"], t + 1)
                    wait(act, g["wo_done"], t)
                    nc.scalar.activation(ot[:], p_r[:, 0, :], ACT.Copy).then_inc(g["ot_ready"], 1)
                if turn.on[3]:
                    t, u = turn.tile(3)
                    act.wait_ge(g["sub_done"], t + 1)
                    nc.scalar.activation(pr[:, u], pr[:, u], ACT.Exp, scale=scale).then_inc(g["exp_done"], 1)

            pipeline(act, 6, step)

        @block.vector
        def _(dve):
            finish_statistics(nc, None, dve, k, "dve", g["stats"])
            dve.wait_ge(g["masks_in"], 32)
            nc.vector.tensor_scalar(mask_f[:], mask_i[:], 0.0, None, ALU.not_equal).then_inc(g["mask_steps"], 1)
            nc.vector.tensor_scalar(mb_f[:], mb_i[:], 0.0, None, ALU.not_equal).then_inc(g["mask_steps"], 1)
            dve.wait_ge(g["mask_steps"], 2)
            nc.vector.tensor_scalar(mb[:], mb_f[:], NEG, -NEG, ALU.mult, ALU.add).then_inc(g["mask_steps"], 1)

            def step(turn):
                if turn.on[0]:
                    t, u = turn.tile(0)
                    wait(dve, g["xt_done"], t - 1)
                    nc.vector.tensor_scalar(xn[:, u, :], tile_of(k.x, t), k.mean[:, bass.ds(t, 1)], k.rstd[:, bass.ds(t, 1)],
                                            ALU.subtract, ALU.mult).then_inc(g["xn_ready"], 1)
                if turn.on[4]:
                    t, u = turn.tile(4)
                    dve.wait_ge(g["exp_done"], t + 1)
                    c = Chain(dve, g["rec_steps"], 2, t)
                    c(nc.vector.tensor_reduce(tot[:, u], pr[:, u], AX, ALU.add))
                    c(nc.vector.reciprocal(rec[:, u], tot[:, u]))
                if turn.on[3]:
                    t, u = turn.tile(3)
                    scores = p_s[:].rearrange("p g h k -> p (g h) k")
                    dve.wait_ge(g["s_done"], t + 1)
                    nc.vector.tensor_reduce(top[:, u], scores, AX, ALU.max).then_inc(g["top_done"], 1)
                    dve.wait_ge(g["top_done"], t + 1)
                    wait(dve, g["t_done"], t - 1)
                    nc.vector.tensor_tensor(pr[:, u], scores, top[:, u].unsqueeze(2).broadcast_to([P, H, S]), ALU.subtract)\
                        .then_inc(g["sub_done"], 1)
                if turn.on[5]:
                    t, u = turn.tile(5)
                    dve.wait_ge(g["wo_done"], t + 1)
                    c = Chain(dve, g["add_step"], 1, t)
                    add_residual(nc, dve, k, c, t, p_r[:, 1, :]).then_inc(g["add_done"], 1)
                if turn.on[4]:
                    t, u = turn.tile(4)
                    dve.wait_ge(g["pv_done"], t + 1)
                    wait(dve, g["ot_done"], t - 1)
                    nc.vector.tensor_tensor(o[:, u], p_o[:, 0], rec[:, u].unsqueeze(2).broadcast_to([P, H, HD]), ALU.mult)\
                        .then_inc(g["o_ready"], 1)

            pipeline(dve, 6, step)


def ffn_quantised(nc, k, w_gate, w_up, w_down):
    F, BLK = w_gate.shape[0], 32
    NF, NB = F // P, D // BLK
    CH = 512
    NC = NTOK // CH
    QMAX, WMAX = 32767.0, 7.0
    s = Stage(nc, "f0")
    with s.ctx:
        wn = s.sb("wn", [P, 3 * NF, P])
        wa, ws, wr = s.sb("wa", [P, 3 * NF, NB]), s.sb("ws", [P, 3 * NF, NB]), s.sb("wr", [P, 3 * NF, NB])
        wt = s.sb("wt", [P, 3 * NF, P])
        xq = s.sb("xq", [P, NT, P])
        up, gate = s.sb("up", [P, NF, NTOK]), s.sb("gate", [P, NF, NTOK])
        sig = s.sb("sig", [P, NTOK])
        most = s.sb("most", [P, 5, NF * NC])
        part, whole = s.sb("part", [P, 5]), s.sb("whole", [P, 5])
        sc, rc = s.sb("sc", [P, 5]), s.sb("rc", [P, 5])
        xt = s.sb("xt", [P, NT, P])
        pb = [s.ps(f"pb{i}", [P, CH]) for i in range(6)]
        names = ("w_in stats w_quantised w_t w_ready steps maxes xq_ready xt_done xt_ready up_done up_ready "
                 "up_scaled u_lifted gate_scaled gate_lifted gq_in sig_made sig_done down_done add_step add_done o_ready g_rounded").split()
        g = {n: s.sem(n) for n in names}
        block = s.ctx.enter_context(nc.Block())
        X, UP, GATE, PROD, OUT = range(5)
        HALVES = 2
        sigs = [sig[:]] + [z[:].rearrange("p t d -> p (t d)") for z in (xq, xt)]
        assert NF <= 3

        @block.sync
        def _(sp):
            sp.dma_start(wn[:, 0:NF, :], w_up.rearrange("(j p) d -> p j d", p=P)).then_inc(g["w_in"], 16)
            sp.dma_start(wn[:, NF:2 * NF, :], w_gate.rearrange("(j p) d -> p j d", p=P)).then_inc(g["w_in"], 16)
            sp.dma_start(wn[:, 2 * NF:, :], w_down.rearrange("p (j d) -> p j d", d=P)).then_inc(g["w_in"], 16)

        @block.gpsimd
        def _(pool):
            for n in (X, UP, GATE, PROD, OUT):
                pool.wait_ge(g["maxes"], 2 * n + 1)
                nc.gpsimd.partition_all_reduce(whole[:, n:n + 1], part[:, n:n + 1], P, bass.bass_isa.ReduceOp.absmax)\
                    .then_inc(g["maxes"], 1)

        @block.tensor
        def _(pe):
            pe.wait_ge(g["w_quantised"], 1)
            for j in range(3 * NF):
                last = nc.tensor.transpose(pb[j // 4][:, (j % 4) * P:(j % 4 + 1) * P], wn[:, j, :], k.ident[:])
            last.then_inc(g["w_t"], 1)
            for c in range(NC):
                pe.wait_ge(g["xq_ready"], c * 4 // NC + 1)
                wait(pe, g["xt_ready"], c - 1)
                for j in range(4):
                    last = nc.tensor.transpose(pb[4 + c % 2][:, j * P:(j + 1) * P], xq[:, 4 * c + j, :], k.ident[:])
                last.then_inc(g["xt_done"], 1)
            pe.wait_ge(g["w_ready"], 1)
            for n in range(2 * NF * NC):
                j, c = n // NC, n % NC
                if n < NC:
                    pe.wait_ge(g["xt_ready"], c + 1)
                wait(pe, g["up_ready"], n - 3)
                nc.tensor.matmul(pb[n % 4][:], wt[:, j, :], xt[:, 4 * c:4 * c + 4, :], start=True, stop=True)\
                    .then_inc(g["up_done"], 1)
            pe.wait_ge(g["up_ready"], 2 * NF * NC)
            for c in range(NC):
                pe.wait_ge(g["o_ready"], c * HALVES // NC + 1)
                wait(pe, g["add_done"], c - 3)
                for i in range(4):
                    t = 4 * c + i
                    for j in range(NF):
                        last = nc.tensor.matmul(pb[c % 4][:, i * P:(i + 1) * P], up[:, j, t * P:(t + 1) * P], wt[:, 2 * NF + j, :],
                                                start=(j == 0), stop=(j == NF - 1))
                last.then_inc(g["down_done"], 1)

        @block.scalar
        def _(act):
            finish_statistics(nc, act, None, k, "act", g["stats"])
            act.wait_ge(g["w_t"], 1)
            for b in range(3):
                n = min(4, 3 * NF - 4 * b)
                last = nc.scalar.activation(wt[:, 4 * b:4 * b + n, :], pb[b][:, 0:n * P].rearrange("p (j d) -> p j d", d=P), ACT.Copy)
            last.then_inc(g["w_ready"], 1)
            for c in range(NC):
                act.wait_ge(g["xt_done"], c + 1)
                nc.scalar.activation(xt[:, 4 * c:4 * c + 4, :], pb[4 + c % 2][:].rearrange("p (j d) -> p j d", d=P), ACT.Copy)\
                    .then_inc(g["xt_ready"], 1)
            for n in range(2 * NF * NC):
                j, c = n // NC, n % NC
                act.wait_ge(g["up_done"], n + 1)
                dst = up if j < NF else gate
                nc.scalar.activation(dst[:, j % NF, c * CH:(c + 1) * CH], pb[n % 4][:], ACT.Copy).then_inc(g["up_ready"], 1)
            act.wait_ge(g["up_scaled"], 1)
            for j in range(NF):
                nc.scalar.activation(up[:, j], up[:, j], ACT.Copy, scale=rc[:, UP:UP + 1], bias=ROUND).then_inc(g["u_lifted"], 1)
            act.wait_ge(g["gate_scaled"], 1)
            nc.scalar.activation(gate[:, NF - 1], gate[:, NF - 1], ACT.Copy, scale=rc[:, GATE:GATE + 1], bias=ROUND)\
                .then_inc(g["gate_lifted"], 1)
            for j in range(NF):
                act.wait_ge(g["gq_in"], j + 1)
                nc.scalar.activation(sigs[j], gate[:, j, :], ACT.Sigmoid).then_inc(g["sig_made"], 1)
                act.wait_ge(g["sig_made"], j + 1)
                nc.scalar.activation(sigs[j], sigs[j], ACT.Copy, scale=65536.0, bias=ROUND).then_inc(g["sig_done"], 1)

        @block.vector
        def _(dve):
            finish_statistics(nc, None, dve, k, "dve", g["stats"])
            c = Chain(dve, g["steps"], 0, 0)
            v = nc.vector

            def scales(n, told=None):
                dve.wait_ge(g["maxes"], 2 * n + 2)
                c(v.tensor_scalar(sc[:, n:n + 1], whole[:, n:n + 1], 1.0 / QMAX, 1e-12, ALU.mult, ALU.max))
                c(v.reciprocal(rc[:, n:n + 1], sc[:, n:n + 1]))
                if told is not None:
                    v.tensor_copy(part[:, n:n + 1], rc[:, n:n + 1]).then_inc(told, 1)

            def quantise(ap, n):
                c(v.tensor_scalar(ap, ap, rc[:, n:n + 1], ROUND, ALU.mult, ALU.add))
                c(v.tensor_scalar(ap, ap, ROUND, sc[:, n:n + 1], ALU.subtract, ALU.mult))

            dve.wait_ge(g["w_in"], 48)
            wb = wn[:].rearrange("p j (b n) -> p j b n", n=BLK)
            c(v.tensor_reduce(wa[:], wb, AX, ALU.max, apply_absolute_value=True))
            c(v.tensor_scalar(ws[:], wa[:], 1.0 / WMAX, 1e-12, ALU.mult, ALU.max))
            c(v.reciprocal(wr[:], ws[:]))
            flat = wn[:].rearrange("p j (b n) -> p (j b) n", n=BLK)
            spread = [P, 3 * NF * NB, BLK]
            c(v.tensor_tensor(flat, flat, wr[:].rearrange("p j b -> p (j b)").unsqueeze(2).broadcast_to(spread), ALU.mult))
            c(v.tensor_scalar(flat, flat, ROUND, ROUND, ALU.add, ALU.subtract))
            c(v.tensor_tensor(flat, flat, ws[:].rearrange("p j b -> p (j b)").unsqueeze(2).broadcast_to(spread), ALU.mult))
            v.tensor_copy(part[:, 0:1], ws[:, 0, 0:1]).then_inc(g["w_quantised"], 1)
            dve.wait_ge(g["w_quantised"], 1)
            c(v.tensor_tensor(xq[:], k.x[:], k.mean[:].unsqueeze(2).broadcast_to([P, NT, P]), ALU.subtract))
            c(v.tensor_tensor(xq[:], xq[:], k.rstd[:].unsqueeze(2).broadcast_to([P, NT, P]), ALU.mult))
            v.tensor_reduce(part[:, X:X + 1], xq[:].rearrange("p t d -> p (t d)"), AX, ALU.max, apply_absolute_value=True)\
                .then_inc(g["maxes"], 1)
            scales(X)
            for i in range(4):
                quarter = xq[:, i * NT // 4:(i + 1) * NT // 4, :]
                c(v.tensor_scalar(quarter, quarter, rc[:, X:X + 1], ROUND, ALU.mult, ALU.add))
                v.tensor_scalar(quarter, quarter, ROUND, sc[:, X:X + 1], ALU.subtract, ALU.mult).then_inc(g["xq_ready"], 1)
            for n in range(2 * NF * NC):
                j, ch = n // NC, n % NC
                src = up if j < NF else gate
                dve.wait_ge(g["up_ready"], n + 1)
                kind = UP if j < NF else GATE
                ins = v.tensor_reduce(most[:, kind, (j % NF) * NC + ch:(j % NF) * NC + ch + 1],
                                      src[:, j % NF, ch * CH:(ch + 1) * CH], AX, ALU.max, apply_absolute_value=True)
                if n % (NF * NC) == NF * NC - 1:
                    c(ins)
                    v.tensor_reduce(part[:, kind:kind + 1], most[:, kind, :], AX, ALU.max).then_inc(g["maxes"], 1)
                    if kind == UP:
                        scales(UP, g["up_scaled"])
            scales(GATE, g["gate_scaled"])
            for j in range(NF):
                if j < NF - 1:
                    c(v.tensor_scalar(gate[:, j], gate[:, j], rc[:, GATE:GATE + 1], ROUND, ALU.mult, ALU.add))
                else:
                    dve.wait_ge(g["gate_lifted"], 1)
                v.tensor_scalar(gate[:, j], gate[:, j], ROUND, sc[:, GATE:GATE + 1], ALU.subtract, ALU.mult).then_inc(g["gq_in"], 1)
                dve.wait_ge(g["u_lifted"], j + 1)
                c(v.tensor_scalar(up[:, j], up[:, j], ROUND, sc[:, UP:UP + 1], ALU.subtract, ALU.mult))
            for j in range(NF):
                dve.wait_ge(g["sig_done"], j + 1)
                c(v.tensor_scalar(sigs[j], sigs[j], ROUND, 65535.0, ALU.subtract, ALU.min))
                v.scalar_tensor_tensor(gate[:, j], sigs[j], 1.0 / 65536.0, gate[:, j], ALU.mult, ALU.mult).then_inc(g["g_rounded"], 1)
                dve.wait_ge(g["g_rounded"], j + 1)
                c(v.tensor_reduce(most[:, PROD, j:j + 1], gate[:, j], AX, ALU.max, apply_absolute_value=True))
            v.tensor_reduce(part[:, PROD:PROD + 1], most[:, PROD, 0:NF], AX, ALU.max).then_inc(g["maxes"], 1)
            scales(PROD)
            for j in range(NF):
                quantise(gate[:, j], PROD)
                c(v.tensor_tensor(up[:, j], up[:, j], gate[:, j], ALU.mult))
                c(v.tensor_reduce(most[:, OUT, j:j + 1], up[:, j], AX, ALU.max, apply_absolute_value=True))
            v.tensor_reduce(part[:, OUT:OUT + 1], most[:, OUT, 0:NF], AX, ALU.max).then_inc(g["maxes"], 1)
            scales(OUT)
            for half in range(HALVES):
                toks = slice(half * NTOK // HALVES, (half + 1) * NTOK // HALVES)
                c(v.tensor_scalar(up[:, :, toks], up[:, :, toks], rc[:, OUT:OUT + 1], ROUND, ALU.mult, ALU.add))
                v.tensor_scalar(up[:, :, toks], up[:, :, toks], ROUND, sc[:, OUT:OUT + 1], ALU.subtract, ALU.mult)\
                    .then_inc(g["o_ready"], 1)
            for ch in range(NC):
                dve.wait_ge(g["down_done"], ch + 1)
                x4 = k.x[:, 4 * ch:4 * ch + 4, :]
                v.tensor_tensor(x4, x4, pb[ch % 4][:].rearrange("p (j n) -> p j n", n=P), ALU.add).then_inc(g["add_done"], 1)
                dve.wait_ge(g["add_done"], ch + 1)
                for t in range(4 * ch, 4 * ch + 4):
                    v.bn_stats(tile_of(k.stats, t), tile_of(k.x, t)).then_inc(g["add_step"], 1)


def attention_lookback(nc, k, seg, w_q, w_kv, w_o):
    H, HD, KW = 16, 8, 4
    scale = float(HD) ** -0.5
    s = Stage(nc, "a1")
    with s.ctx:
        wn, wt = s.sb("wn", [P, 4, P]), s.sb("wt", [P, 4, P])
        seg_i, row = s.sb("seg_i", [P, NT, P], I32), s.sb("row", [P, NT, P])
        seg_ti, seg_t = s.sb("seg_ti", [P, NT], I32), s.sb("seg_t", [P, NT])
        keys = s.sb("keys", [P, KW])
        bias = s.sb("bias", [P, NT, KW])
        xn, xt, ct = s.sb("xn", [P, 2, P]), s.sb("xt", [P, 2, P]), s.sb("ct", [P, 2, P])
        pick = s.sb("pick", [P, 2, KW, P])
        kv, q = s.sb("kv", [P, 2, 2 * P]), s.sb("q", [P, 2, P])
        prod = s.sb("prod", [P, 2, KW, H, HD])
        sc, pr = s.sb("sc", [P, KW, H]), s.sb("pr", [P, 2, KW, H])
        vs = s.sb("vs", [P, 4, KW, P])
        top, tot, rec = s.sb("top", [P, H]), s.sb("tot", [P, H]), s.sb("rec", [P, H])
        mix = s.sb("mix", [P, KW, H, HD])
        o, ot = s.sb("o", [P, 2, P]), s.sb("ot", [P, P])
        p_x, p_q, p_kv, p_r = (s.ps(n, [P, 4, P]) for n in ("p_x", "p_q", "p_kv", "p_r"))
        p_g = [s.ps(f"p_g{i}", [P, 2, 2 * P]) for i in range(2)]
        p_ot = s.ps("p_ot", [P, 4, P])
        names = ("w_in w_t w_ready seg_in consts stats pre xn_ready xt_done xt_ready pick_ready ct_ready "
                 "kv_done kv_ready q_done q_ready g_done vs_ready sc_read mid exp_done late o_ready ot_done ot_ready "
                 "wo_done add_step add_done").split()
        g = {n: s.sem(n) for n in names}
        block = s.ctx.enter_context(nc.Block())

        @block.sync
        def _(sp):
            sp.dma_start(wn[:, 0, :], w_q).then_inc(g["w_in"], 16)
            sp.dma_start(wn[:, 1:3, :], w_kv.rearrange("(j p) d -> p j d", p=P)).then_inc(g["w_in"], 16)
            sp.dma_start(wn[:, 3, :], w_o).then_inc(g["w_in"], 16)
            sp.dma_start(seg_i[:].rearrange("p t n -> p (t n)"),
                         seg.rearrange("b s -> (b s)").partition_broadcast(P)).then_inc(g["seg_in"], 16)
            with nc.allow_non_contiguous_dma(reason="one index a token"):
                sp.dma_start(seg_ti[:], seg.rearrange("(t b) s -> (b s) t", b=2)).then_inc(g["seg_in"], 16)

        @block.gpsimd
        def _(pool):
            nc.gpsimd.iota(keys[:], [[1, KW]], base=0, channel_multiplier=1,
                           allow_small_or_imprecise_dtypes=True).then_inc(g["consts"], 1)

            def step(turn):
                if turn.on[1]:
                    t, u4 = turn.tile(1)
                    u = u4 % 2
                    wait(pool, g["kv_done"], t - 1)
                    nc.gpsimd.tensor_copy(ct[:, u, :], tile_of(k.ct, t)).then_inc(g["ct_ready"], 1)

            pipeline_by(pool, 6, step, NT, 4)

        @block.tensor
        def _(pe):
            pe.wait_ge(g["w_in"], 48)
            for j in range(4):
                last = nc.tensor.transpose(p_x[:, j, :], wn[:, j, :], k.ident[:])
            last.then_inc(g["w_t"], 1)
            pe.wait_ge(g["w_ready"], 1)

            def step(turn):
                if turn.on[2]:
                    t, u4 = turn.tile(2)
                    u = u4 % 2
                    pe.wait_ge(g["kv_ready"], t + 1)
                    pe.wait_ge(g["pick_ready"], t + 1)
                    wait(pe, g["vs_ready"], t)
                    wait(pe, g["sc_read"], t)
                    for o_ in range(KW):
                        last = nc.tensor.matmul(p_g[o_ // 2][:, o_ % 2, :], pick[:, u, o_, :], kv[:, u, :], start=True, stop=True)
                    last.then_inc(g["g_done"], 1)
                if turn.on[5]:
                    t, u4 = turn.tile(5)
                    u = u4 % 2
                    pe.wait_ge(g["o_ready"], t + 1)
                    wait(pe, g["ot_ready"], t)
                    nc.tensor.transpose(p_ot[:, 0, :], o[:, u, :], k.ident[:]).then_inc(g["ot_done"], 1)
                if turn.on[5]:
                    t, u4 = turn.tile(5)
                    u = u4 % 2
                    pe.wait_ge(g["ot_ready"], t + 1)
                    wait(pe, g["add_done"], t)
                    nc.tensor.matmul(p_r[:, 0, :], ot[:], wt[:, 3, :], start=True, stop=True).then_inc(g["wo_done"], 1)
                if turn.on[1]:
                    t, u4 = turn.tile(1)
                    u = u4 % 2
                    pe.wait_ge(g["xn_ready"], t + 1)
                    wait(pe, g["xt_ready"], t)
                    nc.tensor.transpose(p_x[:, 0, :], xn[:, u, :], k.ident[:]).then_inc(g["xt_done"], 1)
                    pe.wait_ge(g["ct_ready"], t + 1)
                    wait(pe, g["kv_ready"], t)
                    nc.tensor.matmul(p_kv[:, 0:2, :], ct[:, u, :], wt[:, 1:3, :], start=True, stop=True).then_inc(g["kv_done"], 1)
                if turn.on[1]:
                    t, u4 = turn.tile(1)
                    u = u4 % 2
                    pe.wait_ge(g["xt_ready"], t + 1)
                    wait(pe, g["q_ready"], t)
                    nc.tensor.matmul(p_q[:, 0, :], xt[:, u, :], wt[:, 0, :], start=True, stop=True).then_inc(g["q_done"], 1)

            pipeline_by(pe, 6, step, NT, 4)

        @block.scalar
        def _(act):
            finish_statistics(nc, act, None, k, "act", g["stats"])
            act.wait_ge(g["w_t"], 1)
            nc.scalar.activation(wt[:], p_x[:], ACT.Copy).then_inc(g["w_ready"], 1)

            def step(turn):
                if turn.on[5]:
                    t, u4 = turn.tile(5)
                    u = u4 % 2
                    act.wait_ge(g["ot_done"], t + 1)
                    wait(act, g["wo_done"], t)
                    nc.scalar.activation(ot[:], p_ot[:, 0, :], ACT.Copy).then_inc(g["ot_ready"], 1)
                if turn.on[3]:
                    t, u4 = turn.tile(3)
                    u = u4 % 2
                    act.wait_ge(g["mid"], t * 4 + 4)
                    wait(act, g["o_ready"], t - 1)
                    nc.scalar.activation(pr[:, u], sc[:], ACT.Exp, scale=scale).then_inc(g["exp_done"], 1)
                if turn.on[1]:
                    t, u4 = turn.tile(1)
                    u = u4 % 2
                    act.wait_ge(g["xt_done"], t + 1)
                    wait(act, g["q_done"], t - 1)
                    nc.scalar.activation(xt[:, u, :], p_x[:, 0, :], ACT.Copy).then_inc(g["xt_ready"], 1)
                    act.wait_ge(g["kv_done"], t + 1)
                    wait(act, g["g_done"], t - 1)
                    nc.scalar.activation(kv[:, u, :], p_kv[:, 0:2, :].rearrange("p j d -> p (j d)"), ACT.Copy).then_inc(g["kv_ready"], 1)
                if turn.on[2]:
                    t, u4 = turn.tile(2)
                    u = u4 % 2
                    act.wait_ge(g["g_done"], t + 1)
                    act.wait_ge(g["sc_read"], t + 1)
                    wait(act, g["o_ready"], t - 3)
                    for j in range(2):
                        last = nc.scalar.activation(vs[:, u4, 2 * j:2 * j + 2, :], p_g[j][:, :, P:2 * P], ACT.Copy)
                    last.then_inc(g["vs_ready"], 1)
                if turn.on[1]:
                    t, u4 = turn.tile(1)
                    u = u4 % 2
                    act.wait_ge(g["q_done"], t + 1)
                    wait(act, g["sc_read"], t - 1)
                    nc.scalar.activation(q[:, u, :], p_q[:, 0, :], ACT.Copy).then_inc(g["q_ready"], 1)

            pipeline_by(act, 6, step, NT, 4)

        @block.vector
        def _(dve):
            finish_statistics(nc, None, dve, k, "dve", g["stats"])
            v = nc.vector
            dve.wait_ge(g["seg_in"], 32)
            c = Chain(dve, g["pre"], 0, 0)
            r4, s4 = (z[:].rearrange("p t (b n) -> p t b n", b=2) for z in (row, seg_i))
            for b in range(2):
                v.tensor_scalar(r4[:, :, b, :], s4[:, :, b, :], float(S * b), None, ALU.add)
            c(v.tensor_copy(seg_t[:], seg_ti[:]))
            for o_ in range(KW):
                c(v.tensor_scalar(bias[:, :, o_], seg_t[:], float(o_), NEG, ALU.is_ge, ALU.mult))
            c(v.tensor_scalar(bias[:], bias[:], NEG, None, ALU.subtract))
            dve.wait_ge(g["consts"], 1)

            def step(turn):
                if turn.on[0]:
                    t, u4 = turn.tile(0)
                    u = u4 % 2
                    wait(dve, g["xt_done"], t - 1)
                    v.tensor_scalar(xn[:, u, :], tile_of(k.x, t), k.mean[:, bass.ds(t, 1)], k.rstd[:, bass.ds(t, 1)],
                                    ALU.subtract, ALU.mult).then_inc(g["xn_ready"], 1)
                t, u4 = turn.tile(4)
                u, late, mid = u4 % 2, turn.on[4], turn.on[3]
                if late:
                    dve.wait_ge(g["exp_done"], t + 1)
                    v.tensor_reduce(tot[:], pr[:, u].rearrange("p o h -> p h o"), AX, ALU.add).then_inc(g["late"], 1)
                if mid:
                    dve.wait_ge(g["sc_read"], t + 2)
                    wait(dve, g["exp_done"], t + 1)
                    v.tensor_reduce(sc[:], prod[:, 1 - u], AX, ALU.add).then_inc(g["mid"], 1)
                if late:
                    dve.wait_ge(g["late"], t * 4 + 1)
                    v.reciprocal(rec[:], tot[:]).then_inc(g["late"], 1)
                if mid:
                    dve.wait_ge(g["mid"], t * 4 + 5)
                    v.tensor_tensor(sc[:], sc[:], tile_of(bias, t + 1).unsqueeze(2).broadcast_to([P, KW, H]), ALU.add)\
                        .then_inc(g["mid"], 1)
                if late:
                    dve.wait_ge(g["late"], t * 4 + 2)
                    dve.wait_ge(g["vs_ready"], t + 1)
                    v.tensor_tensor(pr[:, u], pr[:, u], rec[:].unsqueeze(1).broadcast_to([P, KW, H]), ALU.mult).then_inc(g["late"], 1)
                if mid:
                    dve.wait_ge(g["mid"], t * 4 + 6)
                    v.tensor_reduce(top[:], sc[:].rearrange("p o h -> p h o"), AX, ALU.max).then_inc(g["mid"], 1)
                if late:
                    dve.wait_ge(g["late"], t * 4 + 3)
                    v.tensor_tensor(mix[:].rearrange("p o h d -> p (o h) d"),
                                    vs[:, u4].rearrange("p o (h d) -> p (o h) d", h=H),
                                    pr[:, u].rearrange("p o h -> p (o h)").unsqueeze(2).broadcast_to([P, KW * H, HD]), ALU.mult)\
                        .then_inc(g["late"], 1)
                if mid:
                    dve.wait_ge(g["mid"], t * 4 + 7)
                    v.tensor_tensor(sc[:], sc[:], top[:].unsqueeze(1).broadcast_to([P, KW, H]), ALU.subtract).then_inc(g["mid"], 1)
                if late:
                    dve.wait_ge(g["late"], t * 4 + 4)
                    wait(dve, g["ot_done"], t - 1)
                    v.tensor_reduce(o[:, u, :], mix[:].rearrange("p o h d -> p (h d) o"), AX, ALU.add)\
                        .then_inc(g["o_ready"], 1)
                if turn.on[2]:
                    t, u4 = turn.tile(2)
                    u = u4 % 2
                    dve.wait_ge(g["g_done"], t + 1)
                    dve.wait_ge(g["q_ready"], t + 1)
                    for j in range(2):
                        last = v.tensor_tensor(prod[:, u, 2 * j:2 * j + 2].rearrange("p o h d -> p o (h d)"), p_g[j][:, :, 0:P],
                                               q[:, u, :].unsqueeze(1).broadcast_to([P, 2, P]), ALU.mult)
                    last.then_inc(g["sc_read"], 1)
                if turn.on[0]:
                    t, u4 = turn.tile(0)
                    u = u4 % 2
                    wait(dve, g["g_done"], t - 1)
                    for o_ in range(KW):
                        last = v.tensor_scalar(pick[:, u, o_, :], tile_of(row, t), keys[:, o_:o_ + 1], None, ALU.is_equal)
                    last.then_inc(g["pick_ready"], 1)
                if turn.on[5]:
                    t, u4 = turn.tile(5)
                    u = u4 % 2
                    dve.wait_ge(g["wo_done"], t + 1)
                    c = Chain(dve, g["add_step"], 1, t)
                    add_residual(nc, dve, k, c, t, p_r[:, 0, :]).then_inc(g["add_done"], 1)

            pipeline_by(dve, 6, step, NT, 4)


E = 8


class Route:
    pass


def route(nc, k, s, r, w_gate, b_gate, choices, capacity, slots, normal_rows, buf):
    G = 4
    xn, xt = s.sb("xn", [P, 2, G, P]), s.sb("xt", [P, 2, G, P])
    wg, bg = s.sb("wg", [P, E]), s.sb("bg", [P, E])
    logit, expo = s.sb("logit", [P, NT, E]), s.sb("expo", [P, NT, E])
    best, tot, place, keep, diff = (s.sb(n, [P, choices, NT]) for n in ("best", "tot", "place", "keep", "diff"))
    which = s.sb("which", [P, choices, NT])
    hot, hot_b = s.sb("hot", [P, choices, NT, E]), s.sb("hot_b", [P, choices, NT, E], BF16)
    cand, iota_e, iota_far = s.sb("cand", [P, NT, E]), s.sb("iota_e", [P, NT, E]), s.sb("iota_far", [P, NT, E])
    run = s.sb("run", [P, choices, E, NT])
    total, reset = s.sb("total", [P, choices, E, NT]), s.sb("reset", [P, E, NT])
    loc = s.sb("loc", [P, NT, E])
    spare, slot = s.sb("spare", [P, choices, NT]), s.sb("slot", [P, choices, NT])
    before, ones_b = s.sb("before", [P, P], BF16), s.sb("ones_b", [P, P], BF16)
    zero = s.sb("zero", [P, P])
    r.to, r.frm = s.sb("to", [P, choices, NT], I32), s.sb("frm", [P, choices, NT], I32)
    r.weight = s.sb("weight", [P, choices, NT])
    r.xn = s.sb("xn_all", [P, NT, P])
    if capacity is None:
        n_tiles = normal_rows // P
        tiles_e, end_e, start_e = (s.sb(n, [P, E]) for n in ("tiles_e", "end_e", "start_e"))
        one_e = s.sb("one_e", [P, E])
        tile_no, past = s.sb("tile_no", [1, n_tiles, E - 2]), s.sb("past", [1, n_tiles, E - 2])
        tile_f = s.sb("tile_f", [1, n_tiles])
        r.tile_expert = s.sb("tile_expert", [1, n_tiles], I32)
    with ExitStack() as inner:
        p_x = inner.enter_context(nc.psum_tensor(f"{s.name}_p_x", [P, 2, G, P], F32))
        p_l = inner.enter_context(nc.psum_tensor(f"{s.name}_p_l", [P, 2, 512], F32))
        p_c = inner.enter_context(nc.psum_tensor(f"{s.name}_p_c", [P, 2, 2, NT * E], F32))
        names = ("r_in stats xn_ready xt_done xt_ready kept l_done l_copied consts hot_ready exp_in exp_done counted "
                 "steps routed scattered zeroed zero_set").split()
        g = {n: s.sem(n) for n in names}
        block = inner.enter_context(nc.Block())

        @block.sync
        def _(sp):
            sp.dma_start(wg[:], w_gate).then_inc(g["r_in"], 16)
            if b_gate is not None:
                sp.dma_start(bg[:], b_gate.partition_broadcast(P)).then_inc(g["r_in"], 16)
            sp.wait_ge(g["zero_set"], 1)
            rows = normal_rows // P
            sp.dma_start(buf[0:normal_rows, :].rearrange("(n p) d -> p n d", p=P),
                         zero[:].unsqueeze(1).broadcast_to([P, rows, P])).then_inc(g["zeroed"], 16)

        @block.gpsimd
        def _(pool):
            cs = g["consts"]
            nc.gpsimd.memset(zero[:], 0.0).then_inc(g["zero_set"], 1)
            nc.gpsimd.memset(before[:], 1.0).then_inc(cs, 1)
            nc.gpsimd.memset(ones_b[:], 1.0).then_inc(cs, 1)
            nc.gpsimd.memset(reset[:], 1.0).then_inc(cs, 1)
            nc.gpsimd.iota(iota_e[:], [[0, NT], [1, E]], base=0, channel_multiplier=0, allow_small_or_imprecise_dtypes=True).then_inc(cs, 1)
            nc.gpsimd.iota(iota_far[:], [[0, NT], [1, E]], base=E, channel_multiplier=0, allow_small_or_imprecise_dtypes=True).then_inc(cs, 1)
            nc.gpsimd.iota(spare[:], [[NTOK, choices], [P, NT]], base=normal_rows, channel_multiplier=1,
                           allow_small_or_imprecise_dtypes=True).then_inc(cs, 1)
            pool.wait_ge(cs, 6)
            nc.gpsimd.affine_select(out=before[:], in_=before[:], compare_op=ALU.is_gt, fill=0.0, base=0,
                                    pattern=[[1, P]], channel_multiplier=-1).then_inc(cs, 1)
            nc.gpsimd.memset(reset[:, :, 0], 0.0).then_inc(cs, 1)
            if capacity is None:
                nc.gpsimd.memset(one_e[:], 1.0).then_inc(cs, 1)
                nc.gpsimd.iota(tile_no[:], [[1, n_tiles], [0, E - 2]], base=0, channel_multiplier=0,
                               allow_small_or_imprecise_dtypes=True).then_inc(cs, 1)

            def step(turn):
                if turn.on[1]:
                    t, u = turn.tile(1)
                    pool.wait_ge(g["xn_ready"], t + 1)
                    nc.gpsimd.tensor_copy(tiles_of(r.xn, t, G), xn[:, u]).then_inc(g["kept"], 1)

            pipeline(pool, 4, step, NT // G)
            pool.wait_ge(g["kept"], NT // G)
            pool.wait_ge(g["zeroed"], 16)
            for c in range(choices if capacity is not None else 0):
                pool.wait_ge(g["routed"], c + 1)
                for t in range(NT):
                    nc.gpsimd.indirect_dma_start(out=buf, out_offset=bass.IndirectOffsetOnAxis(ap=r.to[:, c, t:t + 1], axis=0),
                                                 in_=r.xn[:, t, :], in_offset=None).then_inc(g["scattered"], 16)
            if capacity is not None:
                pool.wait_ge(g["scattered"], 16 * NT * choices)

        @block.tensor
        def _(pe):
            pe.wait_ge(g["r_in"], 16)

            def step(turn):
                if turn.on[1]:
                    t, u = turn.tile(1)
                    pe.wait_ge(g["xn_ready"], t + 1)
                    wait(pe, g["xt_ready"], t - 1)
                    for j in range(G):
                        last = nc.tensor.transpose(p_x[:, u, j, :], xn[:, u, j, :], k.ident[:])
                    last.then_inc(g["xt_done"], 1)
                if turn.on[2]:
                    t, u = turn.tile(2)
                    pe.wait_ge(g["xt_ready"], t + 1)
                    wait(pe, g["l_copied"], t - 1)
                    for j in range(G):
                        last = nc.tensor.matmul(p_l[:, u, j * E:(j + 1) * E], xt[:, u, j, :], wg[:], start=True, stop=True)
                    last.then_inc(g["l_done"], 1)

            pipeline(pe, 4, step, NT // G)
            pe.wait_ge(g["consts"], 8)
            for c in range(choices):
                pe.wait_ge(g["hot_ready"], c + 1)
                h = hot_b[:, c].rearrange("p t e -> p (t e)")
                nc.tensor.matmul(p_c[:, c, 0, :], before[:], h, start=True, stop=True)
                nc.tensor.matmul(p_c[:, c, 1, :], ones_b[:], h, start=True, stop=True).then_inc(g["counted"], 1)

        @block.scalar
        def _(act):
            finish_statistics(nc, act, None, k, "act", g["stats"])

            def step(turn):
                if turn.on[1]:
                    t, u = turn.tile(1)
                    act.wait_ge(g["xt_done"], t + 1)
                    wait(act, g["l_done"], t - 1)
                    nc.scalar.activation(xt[:, u], p_x[:, u], ACT.Copy).then_inc(g["xt_ready"], 1)

            pipeline(act, 4, step, NT // G)
            act.wait_ge(g["exp_in"], 1)
            if choices == 1:
                nc.scalar.activation(expo[:], expo[:], ACT.Exp).then_inc(g["exp_done"], 1)
            else:
                nc.scalar.activation(diff[:, 1], diff[:, 1], ACT.Exp).then_inc(g["exp_done"], 1)

        @block.vector
        def _(dve):
            v = nc.vector
            finish_statistics(nc, None, dve, k, "dve", g["stats"])
            if b_gate is not None:
                dve.wait_ge(g["r_in"], 32)

            def step(turn):
                if turn.on[0]:
                    t, u = turn.tile(0)
                    wait(dve, g["xt_done"], t - 1)
                    wait(dve, g["kept"], t - 1)
                    for j in range(G):
                        n = t * G + j
                        last = v.tensor_scalar(xn[:, u, j, :], tile_of(k.x, n), k.mean[:, bass.ds(n, 1)], k.rstd[:, bass.ds(n, 1)],
                                               ALU.subtract, ALU.mult)
                    last.then_inc(g["xn_ready"], 1)
                if turn.on[3]:
                    t, u = turn.tile(3)
                    dve.wait_ge(g["l_done"], t + 1)
                    v.tensor_copy(tiles_of(logit, t, G), p_l[:, u, 0:G * E].rearrange("p (j e) -> p j e", e=E)).then_inc(g["l_copied"], 1)

            pipeline(dve, 4, step, NT // G)
            dve.wait_ge(g["l_copied"], NT // G)
            dve.wait_ge(g["consts"], 10 if capacity is None else 8)
            c = Chain(dve, g["steps"], 0, 0)
            if b_gate is not None:
                c(v.tensor_tensor(logit[:], logit[:], bg[:].unsqueeze(1).broadcast_to([P, NT, E]), ALU.add))
            for n in range(choices):
                c(v.tensor_reduce(best[:, n], logit[:], AX, ALU.max))
                top = best[:, n].unsqueeze(2).broadcast_to([P, NT, E])
                c(v.tensor_tensor(cand[:], logit[:], top, ALU.is_equal))
                if choices == 1:
                    v.tensor_tensor(expo[:], logit[:], top, ALU.subtract).then_inc(g["exp_in"], 1)
                c(v.scalar_tensor_tensor(cand[:], cand[:], -float(E), iota_far[:], ALU.mult, ALU.add))
                c(v.tensor_reduce(which[:, n], cand[:], AX, ALU.min))
                c(v.tensor_tensor(hot[:, n], iota_e[:], which[:, n].unsqueeze(2).broadcast_to([P, NT, E]), ALU.is_equal))
                v.tensor_copy(hot_b[:, n], hot[:, n]).then_inc(g["hot_ready"], 1)
                dve.wait_ge(g["counted"], n + 1)
                c(v.tensor_copy(total[:, n], p_c[:, n, 1, :].rearrange("p (t e) -> p e t", e=E)))
                c(v.tensor_tensor_scan(run[:, n].rearrange("p e t -> p (e t)"), reset[:].rearrange("p e t -> p (e t)"),
                                       total[:, n].rearrange("p e t -> p (e t)"), 0.0, ALU.mult, ALU.add))
                c(v.tensor_tensor(total[:, n], run[:, n], total[:, n], ALU.subtract))
                if n == 1:
                    c(v.tensor_tensor(total[:, n], total[:, n], run[:, 0, :, NT - 1:NT].broadcast_to([P, E, NT]), ALU.add))
                c(v.tensor_tensor(loc[:], p_c[:, n, 0, :].rearrange("p (t e) -> p t e", e=E),
                                  total[:, n].rearrange("p e t -> p t e"), ALU.add))
                if capacity is None:
                    c(v.tensor_scalar(tiles_e[:], run[:, 0, :, NT - 1], 1.0 / P, (P - 1.0) / P - (P - 1.0) / (2 * P), ALU.mult, ALU.add))
                    c(v.tensor_scalar(tiles_e[:], tiles_e[:], ROUND, ROUND, ALU.add, ALU.subtract))
                    c(v.tensor_tensor_scan(end_e[:], one_e[:], tiles_e[:], 0.0, ALU.mult, ALU.add))
                    c(v.tensor_tensor(start_e[:], end_e[:], tiles_e[:], ALU.subtract))
                    c(v.tensor_scalar(start_e[:], start_e[:], float(P), None, ALU.mult))
                    c(v.tensor_tensor(loc[:], loc[:], start_e[:].unsqueeze(1).broadcast_to([P, NT, E]), ALU.add))
                    c(v.tensor_tensor(past[:], tile_no[:], end_e[0:1, 0:E - 2].unsqueeze(1).broadcast_to([1, n_tiles, E - 2]), ALU.is_ge))
                    c(v.tensor_reduce(tile_f[:], past[:], AX, ALU.add))
                    c(v.tensor_copy(r.tile_expert[:], tile_f[:]))
                c(v.tensor_tensor(loc[:], loc[:], hot[:, n], ALU.mult))
                c(v.tensor_reduce(place[:, n], loc[:], AX, ALU.add))
                if capacity is None:
                    c(v.tensor_scalar(keep[:, n], which[:, n], float(E - 1), None, ALU.is_lt))
                    c(v.tensor_copy(slot[:, n], place[:, n]))
                else:
                    c(v.tensor_scalar(keep[:, n], place[:, n], float(capacity), None, ALU.is_lt))
                    c(v.scalar_tensor_tensor(slot[:, n], which[:, n], float(slots), place[:, n], ALU.mult, ALU.add))
                c(v.tensor_tensor(place[:, n], slot[:, n], spare[:, n], ALU.subtract))
                c(v.tensor_tensor(place[:, n], place[:, n], keep[:, n], ALU.mult))
                c(v.tensor_tensor(place[:, n], place[:, n], spare[:, n], ALU.add))
                v.tensor_copy(r.to[:, n], place[:, n]).then_inc(g["routed"], 1)
                c(v.tensor_tensor(slot[:, n], slot[:, n], keep[:, n], ALU.mult))
                c(v.tensor_copy(r.frm[:, n], slot[:, n]))
                if n + 1 < choices:
                    c(v.scalar_tensor_tensor(logit[:], hot[:, n], -NEG, logit[:], ALU.mult, ALU.add))
            if choices == 2:
                v.tensor_tensor(diff[:, 1], best[:, 1], best[:, 0], ALU.subtract).then_inc(g["exp_in"], 1)
            dve.wait_ge(g["exp_done"], 1)
            if choices == 1:
                c(v.tensor_reduce(tot[:, 0], expo[:], AX, ALU.add))
                c(v.reciprocal(r.weight[:, 0], tot[:, 0]))
                if capacity is None:
                    c(v.tensor_scalar(keep[:], keep[:], 2.0, None, ALU.mult))
            else:
                c(v.tensor_scalar(diff[:, 0], diff[:, 1], 1.0, None, ALU.add))
                c(v.reciprocal(r.weight[:, 0], diff[:, 0]))
                c(v.tensor_tensor(r.weight[:, 1], r.weight[:, 0], diff[:, 1], ALU.mult))
            c(v.tensor_tensor(r.weight[:], r.weight[:], keep[:], ALU.mult))


def experts_gelu(nc, k, s, per_expert, w1, b1, w2, b2, xbuf, ybuf):
    CH, F = 256, w1.shape[2]
    NF = F // P
    chunks = E * per_expert
    R = 4 if per_expert == 2 else 2
    ws1, ws2 = s.sb("ws1", [P, R, F]), s.sb("ws2", [P, R, NF, P])
    b1n, b1t = s.sb("b1n", [E * NF, P]), s.sb("b1t", [P, E * NF])
    b1c, b2s = s.sb("b1c", [P, R, NF]), s.sb("b2s", [P, E, P])
    xs, xt = s.sb("xs", [P, 2, 2, P]), s.sb("xts", [P, 2, CH])
    h, y = s.sb("h", [P, 2, NF, CH]), s.sb("y", [P, 2, 2, P])
    with ExitStack() as inner:
        p_t = inner.enter_context(nc.psum_tensor(f"{s.name}_p_t", [P, 4, P], F32))
        p_h = inner.enter_context(nc.psum_tensor(f"{s.name}_p_h", [P, 2, NF, CH], F32))
        p_y = inner.enter_context(nc.psum_tensor(f"{s.name}_p_y", [P, 2, 4, P], F32))
        names = ("b1_ready b_in x_in0 x_in1 b_t b_ready t_done e_xt_ready h_done h_ready y_done y_ready stored0 stored1").split()
        g = {n: s.sem("e_" + n) for n in names + [f"w_in{w}" for w in range(R)]}
        block = inner.enter_context(nc.Block())
        xrows = xbuf[0:chunks * CH, :].rearrange("(c j p) d -> p c j d", p=P, j=2)
        yrows = ybuf.rearrange("(c j p) d -> p c j d", p=P, j=2)
        unroll = R * per_expert

        def chunk(ap, c):
            return ap[:, c] if isinstance(c, int) else ap[:, bass.ds(c, 1)].rearrange("p a j d -> p (a j) d")

        def expert_of(turn, p):
            c, m = turn.tile(p)
            if isinstance(c, int):
                return c // per_expert, (c // per_expert) % R
            w = m // per_expert
            return turn.group(p) * R + w, w

        def loop(eng, step):
            pipeline_by(eng, 3, step, chunks, unroll, 3)

        @block.sync
        def _(sp):
            sp.dma_start(b1n[:], b1.rearrange("e (f p) -> (e f) p", p=P)).then_inc(g["b_in"], 16)
            sp.dma_start(b2s[:].rearrange("p e d -> p (e d)"), b2.rearrange("e d -> (e d)").partition_broadcast(P)).then_inc(g["b_in"], 16)

            def step(turn):
                c, m = turn.tile(0)
                wait(sp, g["t_done"], c - 1)
                sp.dma_start(xs[:, m % 2], chunk(xrows, c)).then_inc(g[f"x_in{m % 2}"], 16)

            pipeline_by(sp, 1, step, chunks, unroll, unroll)

        @block.gpsimd
        def _(pool):
            def load_expert(e, w):
                if isinstance(e, int):
                    src1, src2 = w1[e], w2[e].rearrange("(f p) d -> p f d", p=P)
                else:
                    src1 = w1[bass.ds(e, 1)].rearrange("a p f -> p (a f)")
                    src2 = w2[bass.ds(e, 1)].rearrange("a (f p) d -> p (a f) d", p=P)
                pool.dma_start(ws1[:, w, :], src1).then_inc(g[f"w_in{w}"], 16)
                pool.dma_start(ws2[:, w], src2).then_inc(g[f"w_in{w}"], 16)

            def group(i, more):
                for m in range(unroll):
                    pool.wait_ge(g["y_ready"], i * unroll + (m + 1))
                    if more and m % per_expert == per_expert - 1:
                        load_expert(i * R + (m // per_expert + R), m // per_expert)
                    pool.dma_start(chunk(yrows, i * unroll + m), y[:, m % 2]).then_inc(g[f"stored{m % 2}"], 16)

            for e in range(R):
                load_expert(e, e)
            with pool.Fori(0, E // R - 1) as i:
                group(i, True)
            group(E // R - 1, False)
            for u in range(2):
                pool.wait_ge(g[f"stored{u}"], 16 * (chunks // 2))

        @block.tensor
        def _(pe):
            pe.wait_ge(g["b_in"], 32)
            nc.tensor.transpose(p_t[:, 0, 0:E * NF], b1n[:], k.ident[0:E * NF, 0:E * NF]).then_inc(g["b_t"], 1)
            pe.wait_ge(g["b_ready"], 1)

            def step(turn):
                if turn.on[0]:
                    c, m = turn.tile(0)
                    pe.wait_ge(g[f"x_in{m % 2}"], turn.half(0) * 16 + 16)
                    wait(pe, g["e_xt_ready"], c)
                    for j in range(2):
                        last = nc.tensor.transpose(p_t[:, j, :], xs[:, m % 2, j, :], k.ident[:])
                    last.then_inc(g["t_done"], 1)
                if turn.on[1]:
                    c, m = turn.tile(1)
                    e, w = expert_of(turn, 1)
                    pe.wait_ge(g["e_xt_ready"], c + 1)
                    if m % per_expert == 0:
                        pe.wait_ge(g[f"w_in{w}"], (turn.group(1) + 1) * 32)
                    wait(pe, g["h_ready"], c - 1)
                    for f in range(NF):
                        last = nc.tensor.matmul(p_h[:, m % 2, f, :], ws1[:, w, f * P:(f + 1) * P], xt[:, m % 2, :], start=True, stop=True)
                    last.then_inc(g["h_done"], 1)
                if turn.on[2]:
                    c, m = turn.tile(2)
                    e, w = expert_of(turn, 2)
                    pe.wait_ge(g["h_ready"], c + 1)
                    wait(pe, g["y_ready"], c - 1)
                    for j in range(2):
                        for f in range(NF):
                            last = nc.tensor.matmul(p_y[:, m % 2, j, :], h[:, m % 2, f, j * P:(j + 1) * P], ws2[:, w, f, :],
                                                    start=(f == 0), stop=(f == NF - 1))
                    last.then_inc(g["y_done"], 1)

            loop(pe, step)

        @block.scalar
        def _(act):
            act.wait_ge(g["b_t"], 1)
            nc.scalar.activation(b1t[:], p_t[:, 0, 0:E * NF], ACT.Copy).then_inc(g["b_ready"], 1)
            act.wait_ge(g["b_ready"], 1)

            def step(turn):
                if turn.on[1]:
                    c, m = turn.tile(1)
                    e, w = expert_of(turn, 1)
                    act.wait_ge(g["h_done"], c + 1)
                    wait(act, g["y_done"], c - 1)
                    if m % per_expert == 0:
                        act.wait_ge(g["b1_ready"], e + 1)
                    for f in range(NF):
                        last = nc.scalar.activation(h[:, m % 2, f, :], p_h[:, m % 2, f, :], ACT.Gelu_apprx_tanh,
                                                    bias=b1c[:, w, f:f + 1])
                    last.then_inc(g["h_ready"], 1)

            loop(act, step)

        @block.vector
        def _(dve):
            dve.wait_ge(g["b_in"], 32)
            dve.wait_ge(g["b_ready"], 1)

            def step(turn):
                if turn.on[0]:
                    c, m = turn.tile(0)
                    dve.wait_ge(g["t_done"], c + 1)
                    wait(dve, g["h_done"], c - 1)
                    nc.vector.tensor_copy(xt[:, m % 2, :], p_t[:, 0:2, :].rearrange("p j n -> p (j n)")).then_inc(g["e_xt_ready"], 1)
                    if m % per_expert == 0:
                        e, w = expert_of(turn, 0)
                        wait(dve, g["h_ready"], (e - (R - 1)) * per_expert)
                        nc.vector.tensor_copy(b1c[:, w, :], b1t[:, bass.ds(e * NF, NF)]).then_inc(g["b1_ready"], 1)
                if turn.on[2]:
                    c, m = turn.tile(2)
                    e, w = expert_of(turn, 2)
                    dve.wait_ge(g["y_done"], c + 1)
                    wait(dve, g[f"stored{m % 2}"], turn.half(2) * 16)
                    bias = tile_of(b2s, e).unsqueeze(1).broadcast_to([P, 2, P])
                    nc.vector.tensor_tensor(y[:, m % 2], p_y[:, m % 2, 0:2, :], bias, ALU.add).then_inc(g["y_ready"], 1)

            loop(dve, step)


GROUPS = 8


def gather_rows(nc, r, choices, yg, ybuf, gathered):
    for t in range(NT):
        for c in range(choices):
            nc.gpsimd.indirect_dma_start(out=yg[:, c, t, :], out_offset=None, in_=ybuf,
                                         in_offset=bass.IndirectOffsetOnAxis(ap=r.frm[:, c, t:t + 1], axis=0))\
                .then_inc(gathered[t * GROUPS // NT], 16)


def add_weighted_rows(nc, dve, k, r, choices, yg, gathered, added, stat):
    n_group = NT // GROUPS
    c = Chain(dve, added, 0, 0)
    for i in range(GROUPS):
        dve.wait_ge(gathered[i], 16 * choices * n_group)
        tiles = slice(i * n_group, (i + 1) * n_group)
        rows, x = yg[:, :, tiles, :], k.x[:, tiles, :]
        for n in range(choices):
            c(nc.vector.tensor_tensor(rows[:, n], rows[:, n], r.weight[:, n, tiles].unsqueeze(2).broadcast_to([P, n_group, P]), ALU.mult))
        for n in range(choices):
            c(nc.vector.tensor_tensor(x, x, rows[:, n], ALU.add))
        for t in range(i * n_group, (i + 1) * n_group):
            nc.vector.bn_stats(tile_of(k.stats, t), tile_of(k.x, t)).then_inc(stat, 1)


def combine(nc, k, s, r, choices, ybuf):
    yg = s.sb("yg", [P, choices, NT, P])
    with ExitStack() as inner:
        gathered = [s.sem(f"gathered{i}") for i in range(GROUPS)]
        added, stat = s.sem("added"), s.sem("stat")
        block = inner.enter_context(nc.Block())

        @block.gpsimd
        def _(pool):
            gather_rows(nc, r, choices, yg, ybuf, gathered)

        @block.vector
        def _(dve):
            add_weighted_rows(nc, dve, k, r, choices, yg, gathered, added, stat)


def mixture_gelu(nc, k, name, w_gate, b_gate, w1, b1, w2, b2, choices, capacity):
    CH = 256
    per_expert = -(-capacity // CH)
    slots = per_expert * CH
    rows = E * slots
    s, r = Stage(nc, name), Route()
    xbuf = nc.dram_tensor(f"{name}_xbuf", [rows + choices * NTOK, D], F32, kind="Internal").ap()
    ybuf = nc.dram_tensor(f"{name}_ybuf", [rows, D], F32, kind="Internal").ap()
    with s.ctx:
        route(nc, k, s, r, w_gate, b_gate, choices, capacity, slots, rows, xbuf)
        experts_gelu(nc, k, s, per_expert, w1, b1, w2, b2, xbuf, ybuf)
        combine(nc, k, s, r, choices, ybuf)


def experts_swiglu(nc, k, s, r, n_tiles, w_up, w_gate, w_down, w_up_s, w_gate_s, w_down_s, xbuf, ybuf):
    F = w_up.shape[2]
    NF, NE = F // P, w_up.shape[0]
    FIRST = NT // 2
    wu, wg, wd = s.sb("wu", [P, NE + 1, F]), s.sb("wgt", [P, NE + 1, F]), s.sb("wd", [P, (NE + 1), NF * P])
    xs, xt = s.sb("xs", [P, 2, P]), s.sb("xts", [P, 2, P])
    sig, a, at = s.sb("sig", [P, 2, F]), s.sb("a", [P, 2, F]), s.sb("at", [P, 2, F])
    y, yg = s.sb("y", [P, 2, P]), s.sb("yg", [P, 1, NT, P])
    with ExitStack() as inner:
        p_x, p_y, p_a = (inner.enter_context(nc.psum_tensor(f"{s.name}_p_{n}", [P, F], F32)) for n in ("xe", "ye", "ae"))
        p_u, p_g = (inner.enter_context(nc.psum_tensor(f"{s.name}_p_{n}", [P, 2, F], F32)) for n in ("ue", "ge"))
        names = ("w_in ws_in x_in0 x_in1 scattered t_done xt_ready u_done sig_done u_read at_done at_ready y_done y_ready "
                 "stored0 stored1 added stat").split()
        g = {n: s.sem("e_" + n) for n in names}
        gathered = [s.sem(f"e_gathered{i}") for i in range(GROUPS)]
        block = inner.enter_context(nc.Block())
        xrows = xbuf.rearrange("(t p) d -> p t d", p=P)
        yrows = ybuf.rearrange("(t p) d -> p t d", p=P)

        def all_tiles(eng, depth, step, lead):
            eng_step = lambda base, routed, tokens: lambda turn: step(turn, base, routed, tokens)
            pipeline(eng, depth, eng_step(0, False, slice(0, FIRST)), FIRST, lead)
            pipeline(eng, depth, eng_step(FIRST, True, None), n_tiles, lead)
            pipeline(eng, depth, eng_step(FIRST + n_tiles, False, slice(FIRST, NT)), NT - FIRST, lead)

        @block.sync
        def _(sp):
            sp.dma_start(wu[:, NE, :], w_up_s).then_inc(g["ws_in"], 16)
            sp.dma_start(wg[:, NE, :], w_gate_s).then_inc(g["ws_in"], 16)
            sp.dma_start(wd[:, NE, :].rearrange("p (f d) -> p f d", d=P),
                         w_down_s.rearrange("(f p) d -> p f d", p=P)).then_inc(g["ws_in"], 16)
            sp.dma_start(wu[:, 0:NE, :], w_up.rearrange("e p f -> p e f")).then_inc(g["w_in"], 16)
            sp.dma_start(wg[:, 0:NE, :], w_gate.rearrange("e p f -> p e f")).then_inc(g["w_in"], 16)
            sp.dma_start(wd[:, 0:NE, :].rearrange("p e (f d) -> p e f d", d=P),
                         w_down.rearrange("e (f p) d -> p e f d", p=P)).then_inc(g["w_in"], 16)

            def step(turn, base, routed, tokens):
                t, u = turn.tile(0)
                if routed:
                    sp.wait_ge(g["scattered"], 16 * NT)
                wait(sp, g["t_done"], t + (base - 1))
                sp.dma_start(xs[:, u, :], tile_of(xrows if routed else r.xn[:, tokens, :], t)).then_inc(g[f"x_in{u}"], 16)

            all_tiles(sp, 1, step, 2)

        @block.gpsimd
        def _(pool):
            for t in range(NT):
                nc.gpsimd.indirect_dma_start(out=xbuf, out_offset=bass.IndirectOffsetOnAxis(ap=r.to[:, 0, t:t + 1], axis=0),
                                             in_=r.xn[:, t, :], in_offset=None).then_inc(g["scattered"], 16)

            def step(turn):
                t, u = turn.tile(0)
                pool.wait_ge(g["y_ready"], t + (FIRST + 1))
                pool.dma_start(tile_of(yrows, t), y[:, u, :]).then_inc(g[f"stored{u}"], 16)

            pipeline(pool, 1, step, n_tiles, 2)
            for u in range(2):
                pool.wait_ge(g[f"stored{u}"], 16 * (n_tiles // 2))
            gather_rows(nc, r, 1, yg, ybuf, gathered)

        @block.tensor
        def _(pe):
            def step(turn, base, routed, tokens):
                if turn.on[0]:
                    t, u = turn.tile(0)
                    pe.wait_ge(g[f"x_in{u}"], turn.half(0) * 16 + (base // 2 + 1) * 16)
                    wait(pe, g["xt_ready"], t + base)
                    nc.tensor.transpose(p_x[:, 0:P], xs[:, u, :], k.ident[:]).then_inc(g["t_done"], 1)
                if turn.on[1]:
                    t, u = turn.tile(1)
                    if routed:
                        if isinstance(t, int) and t == 0:
                            pe.wait_ge(g["w_in"], 48)
                        e = pe.value_load(r.tile_expert[0:1, bass.ds(t, 1)], min_val=0, max_val=NE - 1)
                    else:
                        e = NE
                    pe.wait_ge(g["xt_ready"], t + (base + 1))
                    wait(pe, g["u_read"], t + (base - 1))
                    nc.tensor.matmul(p_g[:, u, :], xt[:, u, :], tile_of(wg, e), start=True, stop=True)
                    nc.tensor.matmul(p_u[:, u, :], xt[:, u, :], tile_of(wu, e), start=True, stop=True).then_inc(g["u_done"], 1)
                if turn.on[2]:
                    t, u = turn.tile(2)
                    pe.wait_ge(g["u_read"], t + (base + 1))
                    wait(pe, g["at_ready"], t + base)
                    for f in range(NF):
                        last = nc.tensor.transpose(p_a[:, f * P:(f + 1) * P], a[:, u, f * P:(f + 1) * P], k.ident[:])
                    last.then_inc(g["at_done"], 1)
                if turn.on[3]:
                    t, u = turn.tile(3)
                    if routed:
                        e = pe.value_load(r.tile_expert[0:1, bass.ds(t, 1)], min_val=0, max_val=NE - 1)
                    else:
                        e = NE
                    pe.wait_ge(g["at_ready"], t + (base + 1))
                    wait(pe, g["y_ready"], t + base)
                    for f in range(NF):
                        w = wd[:, e, f * P:(f + 1) * P] if isinstance(e, int) else \
                            wd[:, bass.ds(e, 1), f * P:(f + 1) * P].rearrange("p a n -> p (a n)")
                        last = nc.tensor.matmul(p_y[:, 0:P], at[:, u, f * P:(f + 1) * P], w, start=(f == 0), stop=(f == NF - 1))
                    last.then_inc(g["y_done"], 1)

            pe.wait_ge(g["ws_in"], 48)
            all_tiles(pe, 4, step, 4)

        @block.scalar
        def _(act):
            def step(turn, base, routed, tokens):
                if turn.on[2]:
                    t, u = turn.tile(2)
                    act.wait_ge(g["at_done"], t + (base + 1))
                    wait(act, g["y_done"], t + (base - 1))
                    nc.scalar.activation(at[:, u, :], p_a[:], ACT.Copy).then_inc(g["at_ready"], 1)
                if turn.on[1]:
                    t, u = turn.tile(1)
                    act.wait_ge(g["u_done"], t + (base + 1))
                    wait(act, g["u_read"], t + (base - 1))
                    nc.scalar.activation(sig[:, u, :], p_g[:, u, :], ACT.Silu).then_inc(g["sig_done"], 1)

            all_tiles(act, 4, step, 4)

        @block.vector
        def _(dve):
            v = nc.vector

            def step(turn, base, routed, tokens):
                if turn.on[0]:
                    t, u = turn.tile(0)
                    dve.wait_ge(g["t_done"], t + (base + 1))
                    wait(dve, g["u_done"], t + (base - 1))
                    v.tensor_copy(xt[:, u, :], p_x[:, 0:P]).then_inc(g["xt_ready"], 1)
                if turn.on[3]:
                    t, u = turn.tile(3)
                    dve.wait_ge(g["y_done"], t + (base + 1))
                    if routed:
                        wait(dve, g[f"stored{u}"], turn.half(3) * 16)
                        v.tensor_copy(y[:, u, :], p_y[:, 0:P]).then_inc(g["y_ready"], 1)
                    else:
                        x = tile_of(k.x[:, tokens, :], t)
                        v.tensor_tensor(x, x, p_y[:, 0:P], ALU.add).then_inc(g["y_ready"], 1)
                if turn.on[1]:
                    t, u = turn.tile(1)
                    dve.wait_ge(g["sig_done"], t + (base + 1))
                    wait(dve, g["at_done"], t + (base - 1))
                    v.tensor_tensor(a[:, u, :], sig[:, u, :], p_u[:, u, :], ALU.mult).then_inc(g["u_read"], 1)

            all_tiles(dve, 4, step, 4)
            dve.wait_ge(g["y_ready"], NT + n_tiles)
            add_weighted_rows(nc, dve, k, r, 1, yg, gathered, g["added"], g["stat"])


def mixture_swiglu(nc, k, name, w_gate, w_up, w_gt, w_down, w_up_s, w_gt_s, w_down_s):
    n_tiles = NT + E - 2
    rows = n_tiles * P
    s, r = Stage(nc, name), Route()
    xbuf = nc.dram_tensor(f"{name}_xbuf", [rows + NTOK, D], F32, kind="Internal").ap()
    ybuf = nc.dram_tensor(f"{name}_ybuf", [rows, D], F32, kind="Internal").ap()
    with s.ctx:
        route(nc, k, s, r, w_gate, None, 1, None, 0, rows, xbuf)
        experts_swiglu(nc, k, s, r, n_tiles, w_up, w_gt, w_down, w_up_s, w_gt_s, w_down_s, xbuf, ybuf)


def attention_latent(nc, k, gamma_x, beta_x, gamma_l, beta_l, w_q, w_kv, w_o, cos, sin):
    H, HD = 8, 64
    NP = H // 2
    scale = float(HD) ** -0.5
    s = Stage(nc, "a2")
    with s.ctx:
        wq, wkv, wo = s.sb("wq", [P, H * HD]), s.sb("wkv", [P, 2 * H * HD]), s.sb("wo", [P, NP, P])
        wr = s.sb("wr", [P, H, 2, HD // 2])
        gx, bx, gl, bl = (s.sb(n, [P, 1]) for n in ("gx", "bx", "gl", "bl"))
        cs, sn = s.sb("cs", [P, S]), s.sb("sn", [P, S])
        c_mean, c_rstd, l_rstd = (s.sb(n, [P, NT]) for n in ("c_mean", "c_rstd", "l_rstd"))
        var2, root2, inv2, tmp2, tmp3 = (s.sb(n, [P, 2, NT]) for n in ("var2", "root2", "inv2", "tmp2", "tmp3"))
        xn = s.sb("xn", [P, 2, 2, P])
        xl = s.sb("xl", [P, 2, 2, 2, S])
        q, kt = s.sb("q", [P, 2, NP, P]), s.sb("kt", [P, 2, NP, 2, 2, S])
        kc, ks = s.sb("kc", [P, 2, NP * 2, S]), s.sb("ks", [P, 2, NP * 2, S])
        v_s = s.sb("v", [P, 2, 2, H * HD])
        pr = s.sb("pr", [P, 2, H, P])
        top, tot, rec = s.sb("top", [P, 2, H]), s.sb("tot", [P, 2, H]), s.sb("rec", [P, 2, H])
        prt = s.sb("prt", [P, H, P])
        o, ot = s.sb("o", [P, 2, H, HD]), s.sb("ot", [P, NP, P])
        ring = s.ps("ring", [P, 8, 512])
        names = ("w_in wr_ready stats c_steps xn_ready xt_done xl_ready q_done k_done q_ready kl_ready kx_ready rope_in "
                 "v_done v_ready s_done top_done sub_done exp_done rec_steps t_done prt_ready pv_done o_ready "
                 "ot_done ot_ready wo_done add_step add_done").split()
        g = {n: s.sem(n) for n in names}
        block = s.ctx.enter_context(nc.Block())

        def four(n):
            return ring[:, n, :].rearrange("p (j n) -> p j n", n=P)

        @block.sync
        def _(sp):
            for dst, src in ((wq[:], w_q), (wkv[:], w_kv), (wo[:], w_o.rearrange("(j p) d -> p j d", p=P)), (cs[:], cos), (sn[:], sin)):
                sp.dma_start(dst, src).then_inc(g["w_in"], 16)
            for dst, src in ((gx, gamma_x), (bx, beta_x), (gl, gamma_l), (bl, beta_l)):
                sp.dma_start(dst[:], src.rearrange("(p a) -> p a", a=1)).then_inc(g["w_in"], 16)

        @block.gpsimd
        def _(pool):
            pool.wait_ge(g["w_in"], 144)
            wk = wkv[:, 0:H * HD].rearrange("p (h a d) -> p h a d", h=H, a=2)
            for a in range(2):
                nc.gpsimd.tensor_copy(wr[:, :, a, :], wk[:, :, 1 - a, :]).then_inc(g["wr_ready"], 1)

            def step(turn):
                if turn.on[2]:
                    t, u = turn.tile(2)
                    pool.wait_ge(g["rope_in"], t + 1)
                    wait(pool, g["s_done"], t - 1)
                    nc.gpsimd.tensor_tensor(kt[:, u, :, :, 0, :].rearrange("p j b n -> p (j b) n"), kc[:, u], ks[:, u], ALU.add)\
                        .then_inc(g["kx_ready"], 1)

            pipeline(pool, 6, step)

        @block.tensor
        def _(pe):
            pe.wait_ge(g["w_in"], 144)
            pe.wait_ge(g["wr_ready"], 2)

            def step(turn):
                def transposes():
                    t, u = turn.tile(1)
                    pe.wait_ge(g["xn_ready"], t + 1)
                    wait(pe, g["xl_ready"], t)
                    wait(pe, g["add_done"], t - 4)
                    for a in range(2):
                        last = nc.tensor.transpose(four(4)[:, a, :], xn[:, u, a, :], k.ident[:])
                    last.then_inc(g["xt_done"], 1)

                def values():
                    t, u = turn.tile(3)
                    pe.wait_ge(g["kl_ready"], t + 1)
                    wait(pe, g["v_ready"], t)
                    for b in range(2):
                        last = nc.tensor.matmul(ring[:, 2 + b, :], xl[:, u, b, :, :], wkv[:, H * HD:], start=True, stop=True)
                    last.then_inc(g["v_done"], 1)

                if turn.on[3]:
                    if turn.on[1]:
                        values()
                    t, u = turn.tile(3)
                    pe.wait_ge(g["q_ready"], t + 1)
                    pe.wait_ge(g["kx_ready"], t + 1)
                    if not turn.on[1]:
                        values()
                if turn.on[1]:
                    transposes()
                if turn.on[3]:
                    for j in range(NP):
                        for h in range(2):
                            rows = slice(64 * h, 64 * h + 64)
                            for b in range(2):
                                cols = slice(64 * b, 64 * b + 64)
                                last = nc.tensor.matmul(ring[cols, h, j * P:(j + 1) * P], q[rows, u, j, cols],
                                                        kt[rows, u, j, b, :, :], start=True, stop=True)
                    last.then_inc(g["s_done"], 1)
                if turn.on[4]:
                    t, u = turn.tile(4)
                    pe.wait_ge(g["exp_done"], t + 1)
                    wait(pe, g["o_ready"], t)
                    wait(pe, g["prt_ready"], t)
                    for h in range(H):
                        last = nc.tensor.transpose(four(5 + h // 4)[:, h % 4, :], pr[:, u, h, :], k.ident[:])
                    last.then_inc(g["t_done"], 1)
                if turn.on[5]:
                    t, u = turn.tile(5)
                    pe.wait_ge(g["o_ready"], t + 1)
                    wait(pe, g["ot_ready"], t)
                    for j in range(NP):
                        last = nc.tensor.transpose(four(7)[:, j, :], o[:, u, 2 * j:2 * j + 2, :].rearrange("p h d -> p (h d)"), k.ident[:])
                    last.then_inc(g["ot_done"], 1)
                if turn.on[2]:
                    t, u = turn.tile(2)
                    pe.wait_ge(g["xl_ready"], t + 1)
                    wait(pe, g["v_ready"], t)
                    for j in range(NP):
                        nc.tensor.matmul(four(3)[:, j, :], wr[:].rearrange("p h a d -> p (h a d)")[:, j * P:(j + 1) * P],
                                         xl[:, u, :, 0, :], start=True, stop=True)
                    wait(pe, g["sub_done"], t)
                    for j in range(NP):
                        last = nc.tensor.matmul(four(0)[:, j, :], wq[:, j * P:(j + 1) * P], xl[:, u, :, 1, :], start=True, stop=True)
                    last.then_inc(g["q_done"], 1)
                    for j in range(NP):
                        last = nc.tensor.matmul(ring[:, 1 + j // 2, (j % 2) * 256:(j % 2 + 1) * 256], wkv[:, j * P:(j + 1) * P],
                                                xl[:, u], start=True, stop=True)
                    last.then_inc(g["k_done"], 1)
                if turn.on[5]:
                    t, u = turn.tile(5)
                    pe.wait_ge(g["ot_ready"], t + 1)
                    pe.wait_ge(g["xl_ready"], up_to(t + 5))
                    wait(pe, g["add_done"], t)
                    for j in range(NP):
                        last = nc.tensor.matmul(ring[:, 4, 0:P], ot[:, j, :], wo[:, j, :], start=(j == 0), stop=(j == NP - 1))
                    last.then_inc(g["wo_done"], 1)
                if turn.on[4]:
                    t, u = turn.tile(4)
                    pe.wait_ge(g["prt_ready"], t + 1)
                    pe.wait_ge(g["v_ready"], t + 1)
                    for h in range(H):
                        for b in range(2):
                            rows = slice(64 * b, 64 * b + 64)
                            last = nc.tensor.matmul(ring[rows, 5, h * HD:(h + 1) * HD], prt[:, (h % 2) * NP + h // 2, rows],
                                                    v_s[:, u, b, h * HD:(h + 1) * HD], start=True, stop=True)
                    last.then_inc(g["pv_done"], 1)

            pipeline(pe, 6, step)

        @block.scalar
        def _(act):
            finish_statistics(nc, act, None, k, "act", g["stats"])
            act.wait_ge(g["c_steps"], 11)
            nc.scalar.activation(root2[:], var2[:], ACT.Sqrt).then_inc(g["c_steps"], 1)

            def step(turn):
                if turn.on[3]:
                    t, u = turn.tile(3)
                    act.wait_ge(g["v_done"], t + 1)
                    wait(act, g["pv_done"], t - 1)
                    nc.scalar.activation(v_s[:, u], ring[:, 2:4, :], ACT.Copy).then_inc(g["v_ready"], 1)
                if turn.on[5]:
                    t, u = turn.tile(5)
                    act.wait_ge(g["ot_done"], t + 1)
                    wait(act, g["wo_done"], t)
                    nc.scalar.activation(ot[:], four(7), ACT.Copy).then_inc(g["ot_ready"], 1)
                if turn.on[4]:
                    t, u = turn.tile(4)
                    act.wait_ge(g["t_done"], t + 1)
                    wait(act, g["pv_done"], t)
                    nc.scalar.activation(prt[:], ring[:, 5:7, :].rearrange("p a (j n) -> p (a j) n", n=P), ACT.Copy).then_inc(g["prt_ready"], 1)
                if turn.on[3]:
                    t, u = turn.tile(3)
                    act.wait_ge(g["sub_done"], t + 1)
                    nc.scalar.activation(pr[:, u], pr[:, u], ACT.Exp, scale=scale).then_inc(g["exp_done"], 1)
                if turn.on[2]:
                    t, u = turn.tile(2)
                    act.wait_ge(g["q_done"], t + 1)
                    wait(act, g["s_done"], t - 1)
                    nc.scalar.activation(q[:, u], four(0), ACT.Copy).then_inc(g["q_ready"], 1)
                    act.wait_ge(g["rope_in"], t + 1)
                    keys = ring[:, 1:3, :].rearrange("p a (j b c n) -> p (a j b) c n", j=2, b=2, c=2)
                    nc.scalar.activation(kt[:, u, :, :, 1, :].rearrange("p j b n -> p (j b) n"), keys[:, :, 1, :], ACT.Copy)\
                        .then_inc(g["kl_ready"], 1)

            pipeline(act, 6, step)

        @block.vector
        def _(dve):
            v = nc.vector
            finish_statistics(nc, None, dve, k, "dve", g["stats"])

            c = Chain(dve, g["c_steps"], 0, 0)
            st = k.c_stats
            c(v.tensor_tensor(c_mean[:], st[:, :, 1], st[:, :, 4], ALU.add))
            c(v.tensor_scalar(c_mean[:], c_mean[:], 0.5, None, ALU.mult))
            c(v.tensor_tensor(tmp2[:, 0], st[:, :, 1], st[:, :, 4], ALU.subtract))
            c(v.tensor_tensor(tmp2[:, 0], tmp2[:, 0], tmp2[:, 0], ALU.mult))
            c(v.tensor_tensor(tmp2[:, 1], st[:, :, 2], st[:, :, 5], ALU.add))
            c(v.tensor_scalar(tmp2[:, 1], tmp2[:, 1], 1.0 / D, None, ALU.mult))
            c(v.scalar_tensor_tensor(var2[:, 0], tmp2[:, 0], 0.25, tmp2[:, 1], ALU.mult, ALU.add))
            c(v.tensor_tensor(tmp3[:, 0], k.rstd[:], k.rstd[:], ALU.mult))
            c(v.tensor_tensor(var2[:, 1], tmp3[:, 0], k.var[:], ALU.mult))
            c(v.tensor_scalar(var2[:], var2[:], EPS, None, ALU.add))
            c(v.tensor_copy(tmp3[:, 1], tmp3[:, 0]))
            c.n += 1
            dve.wait_ge(c.sem, c.n)
            c(v.reciprocal(inv2[:], root2[:]))
            c(v.tensor_tensor(tmp2[:], inv2[:], inv2[:], ALU.mult))
            c(v.tensor_tensor(tmp2[:], tmp2[:], var2[:], ALU.mult))
            c(v.tensor_scalar(tmp2[:], tmp2[:], -0.5, 1.5, ALU.mult, ALU.add))
            c(v.tensor_tensor(inv2[:], inv2[:], tmp2[:], ALU.mult))
            c(v.tensor_copy(c_rstd[:], inv2[:, 0]))
            c(v.tensor_tensor(l_rstd[:], inv2[:, 1], k.rstd[:], ALU.mult))
            dve.wait_ge(g["w_in"], 144)

            def step(turn):
                if turn.on[0]:
                    t, u = turn.tile(0)
                    wait(dve, g["xt_done"], t - 1)
                    v.tensor_scalar(xn[:, u, 0, :], tile_of(k.c, t), c_mean[:, bass.ds(t, 1)], c_rstd[:, bass.ds(t, 1)],
                                    ALU.subtract, ALU.mult)
                    v.tensor_scalar(xn[:, u, 1, :], tile_of(k.x, t), k.mean[:, bass.ds(t, 1)], l_rstd[:, bass.ds(t, 1)],
                                    ALU.subtract, ALU.mult).then_inc(g["xn_ready"], 1)
                if turn.on[4]:
                    t, u = turn.tile(4)
                    dve.wait_ge(g["exp_done"], t + 1)
                    c = Chain(dve, g["rec_steps"], 2, t)
                    c(v.tensor_reduce(tot[:, u], pr[:, u], AX, ALU.add))
                    c(v.reciprocal(rec[:, u], tot[:, u]))
                if turn.on[1]:
                    t, u = turn.tile(1)
                    dve.wait_ge(g["xt_done"], t + 1)
                    wait(dve, g["k_done"], t - 1)
                    wait(dve, g["v_done"], t - 1)
                    for a, (gm, bt) in enumerate(((gx, bx), (gl, bl))):
                        last = v.tensor_scalar(xl[:, u, :, a, :], four(4)[:, a, :].rearrange("p (b n) -> p b n", b=2), gm[:], bt[:],
                                               ALU.mult, ALU.add)
                    last.then_inc(g["xl_ready"], 1)
                if turn.on[3]:
                    t, u = turn.tile(3)
                    scores = ring[:, 0:2, :].rearrange("p a (j k) -> p (a j) k", k=P)
                    dve.wait_ge(g["s_done"], t + 1)
                    v.tensor_reduce(top[:, u], scores, AX, ALU.max).then_inc(g["top_done"], 1)
                    dve.wait_ge(g["top_done"], t + 1)
                    wait(dve, g["t_done"], t - 1)
                    v.tensor_tensor(pr[:, u], scores, top[:, u].unsqueeze(2).broadcast_to([P, H, P]), ALU.subtract)\
                        .then_inc(g["sub_done"], 1)
                if turn.on[2]:
                    t, u = turn.tile(2)
                    dve.wait_ge(g["k_done"], t + 1)
                    wait(dve, g["kx_ready"], t - 1)
                    keys = ring[:, 1:3, :].rearrange("p a (j b c n) -> p (a j b) c n", j=2, b=2, c=2)
                    v.tensor_tensor(kc[:, u], keys[:, :, 0, :], cs[:].unsqueeze(1).broadcast_to([P, 2 * NP, S]), ALU.mult)
                    v.tensor_tensor(ks[:, u], ring[:, 3, :].rearrange("p (j n) -> p j n", n=S),
                                    sn[:].unsqueeze(1).broadcast_to([P, 2 * NP, S]), ALU.mult).then_inc(g["rope_in"], 1)
                if turn.on[5]:
                    t, u = turn.tile(5)
                    dve.wait_ge(g["wo_done"], t + 1)
                    c = Chain(dve, g["add_step"], 1, t)
                    add_residual(nc, dve, k, c, t, ring[:, 4, 0:P]).then_inc(g["add_done"], 1)
                if turn.on[4]:
                    t, u = turn.tile(4)
                    dve.wait_ge(g["pv_done"], t + 1)
                    wait(dve, g["ot_done"], t - 1)
                    v.tensor_tensor(o[:, u].rearrange("p (j h) d -> p h j d", h=2), ring[:, 5, :].rearrange("p (j h d) -> p h j d", h=2, d=HD),
                                    rec[:, u].rearrange("p (h j) -> p h j", h=2).unsqueeze(3).broadcast_to([P, 2, NP, HD]), ALU.mult)\
                        .then_inc(g["o_ready"], 1)

            pipeline(dve, 6, step)


def rope_tables():
    half = np.float32(1.0) / np.float32(10000.0) ** (np.arange(0, 64, 2, dtype=np.float32) / np.float32(64))
    theta = np.arange(S, dtype=np.float32)[:, None] * half[None, :]
    angles = np.concatenate([theta, theta], axis=-1).T
    sign = np.where(np.arange(64) < 32, -1.0, 1.0).astype(np.float32)[:, None]
    cos, sin = np.cos(angles), np.sin(angles) * sign
    return np.ascontiguousarray(np.tile(cos, (2, 1))), np.ascontiguousarray(np.tile(sin, (2, 1)))


def attention_64(nc, k, mask, w_q, w_kv, w_out, b_out):
    H, HD = 16, 64
    NP = H // 2
    scale = float(HD) ** -0.5
    s = Stage(nc, "a3")
    with s.ctx:
        wn, wt = s.sb("wn", [P, 4, 8, P]), s.sb("wt", [P, 4, NP, P])
        mask_i, mask_f = s.sb("mask_i", [P, NT, P], mask.dtype), s.sb("mask_f", [P, NT, P], BF16)
        mb_i, mb_f, mb = s.sb("mb_i", [2, NT, S], mask.dtype), s.sb("mb_f", [2, NT, S]), s.sb("mb", [2, NT, S], BF16)
        own, bo = s.sb("own", [2, P], BF16), s.sb("bo", [P, P])
        xn, xt, ct, cm = (s.sb(n, [P, 2, P]) for n in ("xn", "xt", "ct", "cm"))
        q = s.sb("q", [P, 2, NP, P])
        kb = s.sb("kb", [P, 2, 2, NP, P])
        vb = s.sb("vb", [P, 2, 2, NP, 2, HD])
        pr = s.sb("pr", [P, 2, H, S])
        top, tot, rec = s.sb("top", [P, 2, H]), s.sb("tot", [P, 2, H]), s.sb("rec", [P, 2, H])
        prt = s.sb("prt", [P, NP, P])
        o, ot = s.sb("o", [P, 2, H, HD]), s.sb("ot", [P, NP, P])
        ring = s.ps("ring", [P, 8, 512])
        QW, KW, VW, OW = range(4)

        def bank(n, m=1):
            return ring[:, n:n + m, :]

        names = ("w_in0 w_in1 w_in2 w_in3 w_t w_ready masks_in consts stats mask_steps xn_ready ct_ready xt_done xt_ready q_done k_done "
                 "q_ready k_ready v_done v_ready s_done top_done sub_done exp_done rec_steps t_done prt_ready pv_done o_ready "
                 "ot_done ot_ready wo_done add_step add_done").split()
        g = {n: s.sem(n) for n in names}
        block = s.ctx.enter_context(nc.Block())
        sources = [w_q.rearrange("(j p) d -> p j d", p=P), w_kv[0:H * HD, :].rearrange("(j p) d -> p j d", p=P),
                   w_kv[H * HD:, :].rearrange("(j p) d -> p j d", p=P), w_out.rearrange("p (j d) -> p j d", d=P)]

        @block.sync
        def _(sp):
            per_batch = mask.rearrange("(t b) s -> b t s", b=2)
            sp.dma_start(mb_i[:], per_batch).then_inc(g["masks_in"], 16)
            sp.dma_start(mask_i[:].rearrange("p t n -> p (t n)"),
                         mask.rearrange("b s -> (b s)").partition_broadcast(P)).then_inc(g["masks_in"], 16)
            sp.dma_start(bo[:], b_out.partition_broadcast(P)).then_inc(g["masks_in"], 16)
            for n in range(4):
                sp.dma_start(wn[:, n], sources[n]).then_inc(g[f"w_in{n}"], 16)

        @block.gpsimd
        def _(pool):
            nc.gpsimd.memset(own[:], 1.0).then_inc(g["consts"], 1)
            nc.gpsimd.memset(kb[:], 0.0).then_inc(g["consts"], 1)
            nc.gpsimd.memset(vb[:], 0.0).then_inc(g["consts"], 1)
            pool.wait_ge(g["consts"], 3)
            nc.gpsimd.affine_select(out=own[:], in_=own[:], compare_op=ALU.is_ge, fill=0.0, base=0,
                                    pattern=[[1, P]], channel_multiplier=-S).then_inc(g["consts"], 1)
            pool.wait_ge(g["consts"], 4)
            nc.gpsimd.affine_select(out=own[:], in_=own[:], compare_op=ALU.is_ge, fill=0.0, base=S - 1,
                                    pattern=[[-1, P]], channel_multiplier=S).then_inc(g["consts"], 1)
            pool.wait_ge(g["mask_steps"], 3)

            def step(turn):
                if turn.on[2]:
                    t, u = turn.tile(2)
                    wait(pool, g["k_done"], t - 1)
                    wait(pool, g["v_done"], t - 1)
                    nc.gpsimd.tensor_copy(ct[:, u, :], tile_of(k.ct, t))
                    nc.gpsimd.tensor_tensor(cm[:, u, :], tile_of(k.ct, t), tile_of(mask_f, t), ALU.mult)\
                        .then_inc(g["ct_ready"], 1)

            pipeline(pool, 6, step)

        @block.tensor
        def _(pe):
            for n in range(4):
                pe.wait_ge(g[f"w_in{n}"], 16)
                wait(pe, g["w_ready"], n - 1)
                for j in range(8):
                    c = 1024 * (n % 2) + j * P
                    last = nc.tensor.transpose(ring[:, c // 512, c % 512:c % 512 + P], wn[:, n, j, :], k.ident[:])
                last.then_inc(g["w_t"], 1)
            pe.wait_ge(g["w_ready"], 4)
            pe.wait_ge(g["consts"], 5)
            pe.wait_ge(g["mask_steps"], 3)

            def step(turn):
                if turn.on[3]:
                    t, u = turn.tile(3)
                    pe.wait_ge(g["q_ready"], t + 1)
                    pe.wait_ge(g["k_ready"], t + 1)
                    wait(pe, g["v_ready"], t)
                    bias = tile_of(mb, t).unsqueeze(1).broadcast_to([2, 8, S])
                    for n in range(2):
                        nc.tensor.matmul(ring[:, n, :], own[:], bias, start=True, stop=False)
                        for j in range(4):
                            for b in range(2):
                                rows = slice(64 * b, 64 * b + 64)
                                last = nc.tensor.matmul(ring[rows, n, j * P:(j + 1) * P], q[:, u, 4 * n + j, rows],
                                                        kb[:, u, b, 4 * n + j, :], start=False, stop=(j == 3))
                    last.then_inc(g["s_done"], 1)
                if turn.on[1]:
                    t, u = turn.tile(1)
                    pe.wait_ge(g["xn_ready"], t + 1)
                    wait(pe, g["q_ready"], t - 1)
                    wait(pe, g["xt_ready"], t)
                    nc.tensor.transpose(ring[:, 2, 0:P], xn[:, u, :], k.ident[:]).then_inc(g["xt_done"], 1)
                if turn.on[4]:
                    t, u = turn.tile(4)
                    pe.wait_ge(g["exp_done"], t + 1)
                    pe.wait_ge(g["k_ready"], up_to(t + 2))
                    wait(pe, g["prt_ready"], t)
                    for j in range(NP):
                        last = nc.tensor.transpose(ring[:, 3 + j // 4, (j % 4) * P:(j % 4 + 1) * P],
                                                   pr[:, u, 2 * j:2 * j + 2, :].rearrange("p h k -> p (h k)"), k.ident[:])
                    last.then_inc(g["t_done"], 1)
                if turn.on[5]:
                    t, u = turn.tile(5)
                    pe.wait_ge(g["o_ready"], t + 1)
                    wait(pe, g["add_done"], t)
                    wait(pe, g["ot_ready"], t)
                    for j in range(NP):
                        last = nc.tensor.transpose(ring[:, 5 + j // 4, (j % 4) * P:(j % 4 + 1) * P],
                                                   o[:, u, 2 * j:2 * j + 2, :].rearrange("p h d -> p (h d)"), k.ident[:])
                    last.then_inc(g["ot_done"], 1)
                if turn.on[3]:
                    t, u = turn.tile(3)
                    pe.wait_ge(g["ct_ready"], t + 1)
                    wait(pe, g["o_ready"], t - 1)
                    wait(pe, g["v_ready"], t)
                    for h in range(2):
                        if h == 1:
                            pe.wait_ge(g["sub_done"], t + 1)
                        last = nc.tensor.matmul(ring[:, (7 + h) % 8, :], ct[:, u, :],
                                                wt[:, VW].rearrange("p j (h d) -> p h j d", h=2)[:, h], start=True, stop=True)
                    last.then_inc(g["v_done"], 1)
                if turn.on[2]:
                    t, u = turn.tile(2)
                    pe.wait_ge(g["xt_ready"], up_to(t + 2))
                    wait(pe, g["sub_done"], t)
                    for j in range(NP):
                        last = nc.tensor.matmul(ring[:, 1 + j // 4, (j % 4) * P:(j % 4 + 1) * P], wt[:, QW, j, :], xt[:, u, :],
                                                start=True, stop=True)
                    last.then_inc(g["q_done"], 1)
                    pe.wait_ge(g["ct_ready"], t + 1)
                    wait(pe, g["prt_ready"], t - 1)
                    for j in range(NP):
                        last = nc.tensor.matmul(ring[:, 3 + j // 4, (j % 4) * P:(j % 4 + 1) * P], wt[:, KW, j, :], cm[:, u, :],
                                                start=True, stop=True)
                    last.then_inc(g["k_done"], 1)
                if turn.on[5]:
                    t, u = turn.tile(5)
                    pe.wait_ge(g["ot_ready"], t + 1)
                    for j in range(NP):
                        last = nc.tensor.matmul(ring[:, 5, 0:P], ot[:, j, :], wt[:, OW, j, :], start=(j == 0), stop=(j == NP - 1))
                    last.then_inc(g["wo_done"], 1)
                if turn.on[4]:
                    t, u = turn.tile(4)
                    pe.wait_ge(g["prt_ready"], t + 1)
                    pe.wait_ge(g["v_ready"], up_to(t + 2))
                    wait(pe, g["ot_ready"], t)
                    wait(pe, g["o_ready"], t)
                    for j in range(NP):
                        for b in range(2):
                            rows = slice(64 * b, 64 * b + 64)
                            last = nc.tensor.matmul(ring[rows, 6 + j // 4, (j % 4) * P:(j % 4 + 1) * P], prt[:, j, rows],
                                                    vb[:, u, b, j, :, :], start=True, stop=True)
                    last.then_inc(g["pv_done"], 1)

            pipeline(pe, 6, step)

        def pairs(n):
            return bank(n, 2).rearrange("p a (j n) -> p (a j) n", n=P)

        @block.scalar
        def _(act):
            finish_statistics(nc, act, None, k, "act", g["stats"])
            for n in range(4):
                act.wait_ge(g["w_t"], n + 1)
                nc.scalar.activation(wt[:, n], pairs(2 * (n % 2)), ACT.Copy).then_inc(g["w_ready"], 1)
            act.wait_ge(g["consts"], 5)

            def step(turn):
                if turn.on[1]:
                    t, u = turn.tile(1)
                    act.wait_ge(g["xt_done"], t + 1)
                    wait(act, g["q_done"], t - 1)
                    nc.scalar.activation(xt[:, u, :], ring[:, 2, 0:P], ACT.Copy).then_inc(g["xt_ready"], 1)
                if turn.on[4]:
                    t, u = turn.tile(4)
                    act.wait_ge(g["t_done"], t + 1)
                    wait(act, g["pv_done"], t)
                    nc.scalar.activation(prt[:], pairs(3), ACT.Copy).then_inc(g["prt_ready"], 1)
                if turn.on[3]:
                    t, u = turn.tile(3)
                    act.wait_ge(g["sub_done"], t + 1)
                    nc.scalar.activation(pr[:, u], pr[:, u], ACT.Exp, scale=scale).then_inc(g["exp_done"], 1)
                    act.wait_ge(g["v_done"], t + 1)
                    wait(act, g["pv_done"], t - 1)
                    for h in range(2):
                        for b in range(2):
                            last = nc.scalar.activation(vb[64 * h:64 * h + 64, u, b, :, h, :],
                                                        ring[64 * b:64 * b + 64, (7 + h) % 8, :].rearrange("p (j d) -> p j d", d=HD),
                                                        ACT.Copy)
                    last.then_inc(g["v_ready"], 1)
                if turn.on[2]:
                    t, u = turn.tile(2)
                    act.wait_ge(g["q_done"], t + 1)
                    wait(act, g["s_done"], t - 1)
                    nc.scalar.activation(q[:, u], pairs(1), ACT.Copy).then_inc(g["q_ready"], 1)
                    act.wait_ge(g["k_done"], t + 1)
                    for h in range(2):
                        rows = slice(64 * h, 64 * h + 64)
                        for b in range(2):
                            last = nc.scalar.activation(kb[rows, u, b, :, rows], pairs(3)[rows, :, 64 * b:64 * b + 64], ACT.Copy)
                    last.then_inc(g["k_ready"], 1)

            pipeline(act, 6, step)

        @block.vector
        def _(dve):
            v = nc.vector
            finish_statistics(nc, None, dve, k, "dve", g["stats"])
            dve.wait_ge(g["masks_in"], 48)
            v.tensor_scalar(mask_f[:], mask_i[:], 0.0, None, ALU.not_equal).then_inc(g["mask_steps"], 1)
            v.tensor_scalar(mb_f[:], mb_i[:], 0.0, None, ALU.not_equal).then_inc(g["mask_steps"], 1)
            dve.wait_ge(g["mask_steps"], 2)
            v.tensor_scalar(mb[:], mb_f[:], NEG, -NEG, ALU.mult, ALU.add).then_inc(g["mask_steps"], 1)

            def step(turn):
                if turn.on[3]:
                    t, u = turn.tile(3)
                    scores = bank(0, 2).rearrange("p a (h k) -> p (a h) k", k=S)
                    dve.wait_ge(g["s_done"], t + 1)
                    v.tensor_reduce(top[:, u], scores, AX, ALU.max).then_inc(g["top_done"], 1)
                    dve.wait_ge(g["top_done"], t + 1)
                    wait(dve, g["t_done"], t - 1)
                    v.tensor_tensor(pr[:, u], scores, top[:, u].unsqueeze(2).broadcast_to([P, H, S]), ALU.subtract)\
                        .then_inc(g["sub_done"], 1)
                if turn.on[5]:
                    t, u = turn.tile(5)
                    dve.wait_ge(g["ot_done"], t + 1)
                    wait(dve, g["wo_done"], t)
                    v.tensor_copy(ot[:], pairs(5)).then_inc(g["ot_ready"], 1)
                    dve.wait_ge(g["wo_done"], t + 1)
                    c = Chain(dve, g["add_step"], 2, t)
                    c(v.tensor_tensor(tile_of(k.x, t), tile_of(k.x, t), bo[:], ALU.add))
                    add_residual(nc, dve, k, c, t, ring[:, 5, 0:P]).then_inc(g["add_done"], 1)
                if turn.on[0]:
                    t, u = turn.tile(0)
                    wait(dve, g["xt_done"], t - 1)
                    v.tensor_scalar(xn[:, u, :], tile_of(k.x, t), k.mean[:, bass.ds(t, 1)], k.rstd[:, bass.ds(t, 1)],
                                    ALU.subtract, ALU.mult).then_inc(g["xn_ready"], 1)
                if turn.on[4]:
                    t, u = turn.tile(4)
                    dve.wait_ge(g["exp_done"], t + 1)
                    c = Chain(dve, g["rec_steps"], 2, t)
                    c(v.tensor_reduce(tot[:, u], pr[:, u], AX, ALU.add))
                    c(v.reciprocal(rec[:, u], tot[:, u]))
                if turn.on[4]:
                    t, u = turn.tile(4)
                    dve.wait_ge(g["pv_done"], t + 1)
                    wait(dve, g["ot_done"], t - 1)
                    v.tensor_tensor(o[:, u], bank(6, 2).rearrange("p a (h d) -> p (a h) d", d=HD),
                                    rec[:, u].unsqueeze(2).broadcast_to([P, H, HD]), ALU.mult).then_inc(g["o_ready"], 1)

            pipeline(dve, 6, step)


def store_stage(nc, k, out):
    s = Stage(nc, "store")
    with s.ctx:
        stored = s.sem("stored")
        block = s.ctx.enter_context(nc.Block())

        @block.sync
        def _(sp):
            sp.dma_start(out.rearrange("(t b) s d -> (b s) t d", b=2), k.x[:]).then_inc(stored, 16)
            sp.wait_ge(stored, 16)


def program(nc, a, out, stages=range(8)):
    k = Kept()
    with ExitStack() as ctx:
        def sb(name, shape, dt=F32):
            return ctx.enter_context(nc.sbuf_tensor(name, shape, dt))

        k.x, k.c, k.ct = sb("x", [P, NT, D]), sb("c", [P, NT, D]), sb("ct", [P, NT, P])
        k.ident = sb("ident", [P, P])
        k.stats, k.c_stats = sb("stats", [P, NT, 6]), sb("c_stats", [P, NT, 6])
        k.mean, k.rstd, k.var, k.vareps, k.root, k.tmp_a, k.tmp_b = (
            sb(n, [P, NT]) for n in ("mean", "rstd", "var", "vareps", "root", "tmp_a", "tmp_b"))
        load_stage(nc, k, a["x"], a["ctx_1024"])
        run = {
            1: lambda: ffn_quantised(nc, k, a["L0_ffn_w_gate"], a["L0_ffn_w_up"], a["L0_ffn_w_down"]),
            2: lambda: attention_lookback(nc, k, a["itok_BxS_0_511"], a["L1_xattn_Wq"], a["L1_xattn_Wkv"], a["L1_xattn_Wo"]),
            3: lambda: mixture_gelu(nc, k, "m1", a["L1_ffn_wg"], None, a["L1_ffn_w1"], a["L1_ffn_b1"], a["L1_ffn_w2"],
                                    a["L1_ffn_b2"], 1, NTOK // E),
            7: lambda: mixture_gelu(nc, k, "m3", a["L3_ffn_Wg"], a["L3_ffn_bg"], a["L3_ffn_W1"], a["L3_ffn_b1"], a["L3_ffn_W2"],
                                    a["L3_ffn_b2"], 2, int(np.ceil(1.2 * NTOK * 2 / E))),
            5: lambda: mixture_swiglu(nc, k, "m2", *(a[f"L2_ffn_{n}"] for n in ("Wr", "Wu", "Wg", "Wd", "Wu_s", "Wg_s", "Wd_s"))),
            4: lambda: attention_latent(nc, k, *(a[f"L2_xattn_{n}"] for n in ("gamma_x", "beta_x", "gamma_l", "beta_l", "Wq", "Wkv", "Wo")),
                                        a["rope_cos"], a["rope_sin"]),
            6: lambda: attention_64(nc, k, a["mask_BxS2_bf1"], *(a[f"L3_xattn_{n}"] for n in ("Wq", "Wkv", "Wout", "b_out"))),
            0: lambda: attention_8(nc, k, a["mask_BxS2_if1"], *(a[f"L0_xattn_w_{n}"] for n in "qkvo")),
        }
        for n in stages:
            run[n]()
        store_stage(nc, k, out)


def kernel(**inputs):
    import concourse.bacc as bacc
    from concourse.bass_utils import run_bass_kernel_spmd

    nc = bacc.Bacc("TRN2", target_bir_lowering=False, num_devices=1)
    arrays, args = {}, {}
    cos, sin = rope_tables()
    for name, value in {**inputs, "rope_cos": cos, "rope_sin": sin}.items():
        a = np.ascontiguousarray(value)
        arrays[f"in_{name}"] = a
        args[name] = nc.dram_tensor(f"in_{name}", a.shape, mybir.dt.from_np(a.dtype), kind="ExternalInput").ap()
    out = nc.dram_tensor("out_x", (B, S, D), F32, kind="ExternalOutput").ap()
    program(nc, args, out)
    r = run_bass_kernel_spmd(nc, [arrays], core_ids=[0])
    return r.results[0]["out_x"]
```
